# Optimizing a Trainium2 kernel written in Bass

```python
import numpy as np
import jax
import jax.numpy as jnp

def _softmax(x, axis=-1):
    return jax.nn.softmax(x, axis=axis)

def _gelu(x):
    return jax.nn.gelu(x, approximate=True)

def _silu(x):
    return jax.nn.silu(x)

def _sigmoid(x):
    return jax.nn.sigmoid(x)

def _layernorm(x, axis=-1, eps=1e-05):
    m = jnp.mean(x, axis=axis, keepdims=True)
    v = jnp.var(x, axis=axis, keepdims=True)
    return (x - m) / jnp.sqrt(v + eps)

def _scatter_add(tgt, idx, src, axis=0):
    return tgt.at[idx].add(src)

def _segment_sum(src, seg, n):
    return jax.ops.segment_sum(src, seg, n)
kernel_name = 'mk_sandwich_d1_jaxref_r8_27681c'

def setup_inputs(seed: int=0):
    np.random.seed(seed)
    _w = jnp.asarray

    def _L0_attn_setup():
        import jax, jax.numpy as jnp
        import numpy as np
        BLOCK = 32
        NUM_HEADS = 16
        HEAD_DIM = 128
        FP4_GRID = jnp.array([0.0, 0.5, 1.0, 1.5, 2.0, 3.0, 4.0, 6.0], dtype=jnp.float32)

        def quantize_to_mxfp4(w, block_size=BLOCK):
            D, F = w.shape
            blocks = w.reshape(D // block_size, block_size, F)
            amax = jnp.max(jnp.abs(blocks), axis=1)
            e = jnp.floor(jnp.log2(jnp.maximum(amax, 1e-12) / 6.0))
            scale = jnp.exp2(e)
            v = blocks / scale[:, None, :]
            idx = jnp.argmin(jnp.abs(jnp.abs(v)[..., None] - FP4_GRID), axis=-1)
            codes = jnp.sign(v) * FP4_GRID[idx]
            return (codes.reshape(D, F).astype(jnp.float32), scale.astype(jnp.float32))

        def _mxfp4_matmul(x, codes, scales, block_size=BLOCK):
            w = codes * jnp.repeat(scales, block_size, axis=0)
            return x @ w
        key = jax.random.key(seed)
        ks = jax.random.split(key, 9)
        B, S, D = (2, 256, 256)
        feat = NUM_HEADS * HEAD_DIM
        x = jax.random.normal(ks[0], (B, S, D), dtype=jnp.float32)

        def make_w(k, din, dout):
            w = jax.random.normal(k, (din, dout), dtype=jnp.float32) * (1.0 / np.sqrt(din))
            return quantize_to_mxfp4(w, BLOCK)
        wq_codes, wq_scales = make_w(ks[1], D, feat)
        wk_codes, wk_scales = make_w(ks[2], D, feat)
        wv_codes, wv_scales = make_w(ks[3], D, feat)
        wo_codes, wo_scales = make_w(ks[4], feat, D)
        bq = jnp.zeros((feat,), jnp.float32)
        bk = jnp.zeros((feat,), jnp.float32)
        bv = jnp.zeros((feat,), jnp.float32)
        bo = jnp.zeros((D,), jnp.float32)
        return {'x': x, 'wq_codes': wq_codes, 'wq_scales': wq_scales, 'bq': bq, 'wk_codes': wk_codes, 'wk_scales': wk_scales, 'bk': bk, 'wv_codes': wv_codes, 'wv_scales': wv_scales, 'bv': bv, 'wo_codes': wo_codes, 'wo_scales': wo_scales, 'bo': bo}
    _L0_attn_in = _L0_attn_setup()

    def _L0_ffn_setup():
        import jax, jax.numpy as jnp
        import numpy as np
        TOP_K = 6
        N_GROUP = 8
        TOPK_GROUP = 3
        CAPACITY = 96
        RSF = 1.0
        key = jax.random.key(seed)
        ks = jax.random.split(key, 8)
        B, S, H = (1, 512, 256)
        E, M = (64, 176)
        MS = 352
        sc = 0.02
        return {'hidden_states': jax.random.normal(ks[0], (B, S, H), jnp.float32), 'gate_weight': jax.random.normal(ks[1], (E, H), jnp.float32) * sc, 'Wg': jax.random.normal(ks[2], (E, M, H), jnp.float32) * sc, 'Wu': jax.random.normal(ks[3], (E, M, H), jnp.float32) * sc, 'Wd': jax.random.normal(ks[4], (E, H, M), jnp.float32) * sc, 'Sg': jax.random.normal(ks[5], (MS, H), jnp.float32) * sc, 'Su': jax.random.normal(ks[6], (MS, H), jnp.float32) * sc, 'Sd': jax.random.normal(ks[7], (H, MS), jnp.float32) * sc}
    _L0_ffn_in = _L0_ffn_setup()
    _d = {'L0_attn_x': _L0_attn_in['x'], 'L0_attn_wq_codes': _L0_attn_in['wq_codes'], 'L0_attn_wq_scales': _L0_attn_in['wq_scales'], 'L0_attn_bq': _L0_attn_in['bq'], 'L0_attn_wk_codes': _L0_attn_in['wk_codes'], 'L0_attn_wk_scales': _L0_attn_in['wk_scales'], 'L0_attn_bk': _L0_attn_in['bk'], 'L0_attn_wv_codes': _L0_attn_in['wv_codes'], 'L0_attn_wv_scales': _L0_attn_in['wv_scales'], 'L0_attn_bv': _L0_attn_in['bv'], 'L0_attn_wo_codes': _L0_attn_in['wo_codes'], 'L0_attn_wo_scales': _L0_attn_in['wo_scales'], 'L0_attn_bo': _L0_attn_in['bo'], 'L0_ffn_gate_weight': _L0_ffn_in['gate_weight'], 'L0_ffn_Wg': _L0_ffn_in['Wg'], 'L0_ffn_Wu': _L0_ffn_in['Wu'], 'L0_ffn_Wd': _L0_ffn_in['Wd'], 'L0_ffn_Sg': _L0_ffn_in['Sg'], 'L0_ffn_Su': _L0_ffn_in['Su'], 'L0_ffn_Sd': _L0_ffn_in['Sd']}
    _x0 = _d['L0_attn_x']
    _d['L0_attn_x'] = jax.random.normal(jax.random.fold_in(jax.random.key(seed), 1), (16, 256, 256), dtype=_x0.dtype)
    del _x0
    return _d

def reference(L0_attn_x, L0_attn_wq_codes, L0_attn_wq_scales, L0_attn_bq, L0_attn_wk_codes, L0_attn_wk_scales, L0_attn_bk, L0_attn_wv_codes, L0_attn_wv_scales, L0_attn_bv, L0_attn_wo_codes, L0_attn_wo_scales, L0_attn_bo, L0_ffn_gate_weight, L0_ffn_Wg, L0_ffn_Wu, L0_ffn_Wd, L0_ffn_Sg, L0_ffn_Su, L0_ffn_Sd):

    def _L0_attn_ref(x, wq_codes, wq_scales, bq, wk_codes, wk_scales, bk, wv_codes, wv_scales, bv, wo_codes, wo_scales, bo):
        import jax, jax.numpy as jnp
        import numpy as np
        BLOCK = 32
        NUM_HEADS = 16
        HEAD_DIM = 128
        FP4_GRID = jnp.array([0.0, 0.5, 1.0, 1.5, 2.0, 3.0, 4.0, 6.0], dtype=jnp.float32)

        def quantize_to_mxfp4(w, block_size=BLOCK):
            D, F = w.shape
            blocks = w.reshape(D // block_size, block_size, F)
            amax = jnp.max(jnp.abs(blocks), axis=1)
            e = jnp.floor(jnp.log2(jnp.maximum(amax, 1e-12) / 6.0))
            scale = jnp.exp2(e)
            v = blocks / scale[:, None, :]
            idx = jnp.argmin(jnp.abs(jnp.abs(v)[..., None] - FP4_GRID), axis=-1)
            codes = jnp.sign(v) * FP4_GRID[idx]
            return (codes.reshape(D, F).astype(jnp.float32), scale.astype(jnp.float32))

        def _mxfp4_matmul(x, codes, scales, block_size=BLOCK):
            w = codes * jnp.repeat(scales, block_size, axis=0)
            return x @ w
        B, S, D = x.shape
        q = _mxfp4_matmul(x, wq_codes, wq_scales) + bq
        k = _mxfp4_matmul(x, wk_codes, wk_scales) + bk
        v = _mxfp4_matmul(x, wv_codes, wv_scales) + bv
        q = q.reshape(B, S, NUM_HEADS, HEAD_DIM)
        k = k.reshape(B, S, NUM_HEADS, HEAD_DIM)
        v = v.reshape(B, S, NUM_HEADS, HEAD_DIM)
        scores = jnp.einsum('bqhd,bkhd->bhqk', q, k) / jnp.sqrt(jnp.float32(HEAD_DIM))
        attn = jax.nn.softmax(scores, axis=-1)
        out = jnp.einsum('bhqk,bkhd->bqhd', attn, v).reshape(B, S, NUM_HEADS * HEAD_DIM)
        return _mxfp4_matmul(out, wo_codes, wo_scales) + bo

    def _L0_ffn_ref(hidden_states, gate_weight, Wg, Wu, Wd, Sg, Su, Sd):
        import jax, jax.numpy as jnp
        import numpy as np
        TOP_K = 6
        N_GROUP = 8
        TOPK_GROUP = 3
        CAPACITY = 96
        RSF = 1.0
        B, S, H = hidden_states.shape
        E, M, _ = Wg.shape
        K, NG, TG, C = (TOP_K, N_GROUP, TOPK_GROUP, CAPACITY)
        x = hidden_states.reshape(-1, H)
        T = x.shape[0]
        logits = x.astype(jnp.float32) @ gate_weight.astype(jnp.float32).T
        scores = jax.nn.softmax(logits, axis=-1)
        group_scores = scores.reshape(T, NG, E // NG).max(axis=-1)
        _, gidx = jax.lax.top_k(group_scores, TG)
        gmask = jnp.zeros((T, NG), scores.dtype).at[jnp.arange(T)[:, None], gidx].set(1.0)
        smask = jnp.repeat(gmask, E // NG, axis=1)
        tmp_scores = jnp.where(smask > 0, scores, 0.0)
        topk_w, topk_i = jax.lax.top_k(tmp_scores, K)
        topk_w = topk_w * RSF
        flat = topk_i.reshape(-1)
        oh = jax.nn.one_hot(flat, E, dtype=jnp.int32)
        pos = jnp.sum(jnp.cumsum(oh, axis=0) * oh, axis=-1) - 1
        slot = flat * C + jnp.minimum(pos, C - 1)
        tok = jnp.arange(T * K) // K
        buf = jnp.zeros((E * C, H), x.dtype).at[slot].set(x[tok]).reshape(E, C, H)
        g = jnp.einsum('ech,emh->ecm', buf, Wg)
        u = jnp.einsum('ech,emh->ecm', buf, Wu)
        out = jnp.einsum('ecm,ehm->ech', jax.nn.silu(g) * u, Wd).reshape(E * C, H)
        yk = out[slot].reshape(T, K, H)
        y = jnp.sum(yk * topk_w[..., None].astype(yk.dtype), axis=1)
        shared = jax.nn.silu(x @ Sg.T) * (x @ Su.T) @ Sd.T
        return (y + shared).reshape(B, S, H)
    x = L0_attn_x
    x = x + _layernorm(_L0_attn_ref(_layernorm(x, axis=-1), L0_attn_wq_codes, L0_attn_wq_scales, L0_attn_bq, L0_attn_wk_codes, L0_attn_wk_scales, L0_attn_bk, L0_attn_wv_codes, L0_attn_wv_scales, L0_attn_bv, L0_attn_wo_codes, L0_attn_wo_scales, L0_attn_bo), axis=-1)
    x = x + _layernorm(_L0_ffn_ref(_layernorm(x, axis=-1), L0_ffn_gate_weight, L0_ffn_Wg, L0_ffn_Wu, L0_ffn_Wd, L0_ffn_Sg, L0_ffn_Su, L0_ffn_Sd), axis=-1)
    return x

_drawn_inputs = setup_inputs


def setup_inputs(seed=0):
    import zlib

    import numpy as np

    out = dict(_drawn_inputs(seed))
    spreads = {'L0_attn_bq': (0.0, 0.1),
     'L0_attn_bk': (0.0, 0.1),
     'L0_attn_bv': (0.0, 0.1),
     'L0_attn_bo': (0.0, 0.1)}
    factors = {}
    for name, (base, spread) in spreads.items():
        noise = np.random.default_rng([zlib.crc32(name.encode()), seed]).standard_normal(out[name].shape)
        drawn = base * np.exp(spread * noise) if base else spread * noise
        out[name] = jnp.asarray(drawn.astype(out[name].dtype))
    for name, factor in factors.items():
        out[name] = (out[name] * factor).astype(out[name].dtype)
    return out
```

```python
from contextlib import ExitStack

import concourse.bass as bass
from concourse import mybir

F32 = mybir.dt.float32
F16 = mybir.dt.float16
U32 = mybir.dt.uint32
I32 = mybir.dt.int32
ALU = mybir.AluOpType
ACT = mybir.ActivationFunctionType
AX = mybir.AxisListType.X

NP = 8
NH = 16
NI = NP * NH
NU = 2 * NI
D = 256
E = 64
CAP = 96
NST = 3
SCALE = 128.0 ** -0.5
SX, SW, SQ, SV, SP_, SO = 4.0, 4.0, 16.0, 2.0, 64.0, 128.0
SG, SA = 64.0, 64.0
EPS = 1e-5
RSQRT_MAGIC = float(0x5F3759DF)
FAR = 1.0e6
ROW = D + E + 1
NRING = 6
NB = 6


class Chain:

    def __init__(self, sem, plan):
        self.sem, self.plan, self.n = sem, plan, 0

    def step(self, engine, slot, fn, waits=()):
        before = self.n
        self.n += 1

        def run(eng):
            eng.wait_ge(self.sem, before)
            for s, v in waits:
                eng.wait_ge(s, v)
            fn(eng).then_inc(self.sem, 1)

        self.plan[engine].setdefault(slot, []).append(run)
        return self.n


def build(nc, x, wc, wsc, wo_c, wo_s, bqkv, bo, gateT, sguT, sdT, ewT, ewd, out):
    ctx = ExitStack()
    with ctx:
        def sb(name, shape, dt=F32):
            return ctx.enter_context(nc.sbuf_tensor(name, shape, dt))

        def sem(name):
            return ctx.enter_context(nc.semaphore(name))

        bank = [ctx.enter_context(nc.psum_tensor(f"bank{i}", [128, 512], F32)) for i in range(8)]
        bS, bPT, bO, bACC, bP0, bP1 = bank[0:2], bank[2], bank[3], bank[4:6], bank[6], bank[7]

        Hd = nc.dram_tensor("Hd", [4096, D], F32, kind="Internal").ap()
        Xd = nc.dram_tensor("Xd", [4096, D], F32, kind="Internal").ap()
        BUF = nc.dram_tensor("BUF", [CAP * E, ROW], F32, kind="Internal").ap()
        Y = [nc.dram_tensor(f"Y{i}", [4096, D], F32, kind="Internal").ap() for i in range(2)]

        X = sb("X", [128, 4, 4, D])
        W = sb("W", [128, 4, 2, 4096], F16)
        SC_ = sb("SC_", [128, NST, 512])
        SS_ = sb("SS_", [128, NST, 512])
        XN = sb("XN", [128, 4, D])
        RB = sb("RB", [128, 8192])
        RBh = RB[:, :].bitcast(F16)
        XT = RBh[:, 0:4096].rearrange("p (b l c n) -> p b l c n", b=2, l=2, c=2)
        QK = RBh[:, 4096:8192].rearrange("p (b m l n) -> p b m l n", b=2, m=2, l=2)
        V = RBh[:, 8192:16384].rearrange("p (b l t n) -> p b l t n", b=2, l=2, t=4)
        P = sb("P", [128, 2, 512])
        PT = sb("PT", [128, 2, 2, 512], F16)
        O = sb("O", [128, 2, 2, 256], F16)
        A = sb("A", [128, 4, D])
        RT = sb("RT", [128, 2, 4, ROW])
        HT = sb("HT", [128, 2, 2, 4096], F16)
        W95 = sb("W95", [128, 32, E])
        ident = sb("ident", [128, 128])
        tri = sb("tri", [128, 128], F16)
        ones = sb("ones", [128, 128], F16)
        bo2 = sb("bo2", [128, 512])
        bqk = sb("bqk", [128, 3, NH])
        gTf = sb("gTf", [128, 2, E])
        gT = sb("gT", [128, 2, 2, E], F16)
        iota64 = sb("iota64", [128, E])
        iota8 = sb("iota8", [128, 8])
        K64 = sb("K64", [128, E])
        tid = sb("tid", [128, 32])
        nm0 = sb("nm0", [128, 4, 2])
        nm = sb("nm", [128, 4, 2])
        rs = sb("rs", [128, 4, 2])
        rr = sb("rr", [128, 4, 2])
        st = sb("st", [128, 2, 4, 6])
        mv = sb("mv", [128, 2, 4, 2])
        nw = sb("nw", [128, 2, 4, 4])
        gm0 = sb("gm0", [128, 4])
        gm1 = sb("gm1", [128, 4])
        gsum = sb("gsum", [128, 4])
        grec = sb("grec", [128, 4])
        Sx = sb("Sx", [128, 4, E])
        Tm = sb("Tm", [128, 4, E])
        gs = sb("gs", [128, 4, 8])
        g8 = sb("g8", [128, 4, 8])
        gi = sb("gi", [128, 4, 8], U32)
        geq = sb("geq", [128, 4, 3, 8])
        gk = sb("gk", [128, 4, 8])
        t8 = sb("t8", [128, 4, 8])
        ti = sb("ti", [128, 4, 8], U32)
        teq = sb("teq", [128, 4, 6, E], F16)
        M = sb("M", [128, 4, E], F16)
        MC = sb("MC", [128, E], F16)
        Ms = sb("Ms", [128, E])
        L = sb("L", [128, E])
        Ls = sb("Ls", [128, E])
        C1 = sb("C1", [128, 4, E])
        Lt = C1
        KP = Sx
        c8 = sb("c8", [128, 4, 8])
        ix = sb("ix", [128, 2, 4, 8], U32)
        zrow = sb("zrow", [128, ROW])

        Wf = W[:, :, :, :].rearrange("p a b c -> p (a b c)").bitcast(F32)
        at = [0]

        def take(n, dt=F32):
            a = Wf[:, at[0]:at[0] + n]
            at[0] += n
            return a if dt == F32 else a.bitcast(dt)

        sgf = take(1408).rearrange("p (m c n) -> p m c n", m=2, c=2)
        sdf = take(768).rearrange("p (j n) -> p j n", j=3)
        sgh = take(1408, F16).rearrange("p (l m c n) -> p l m c n", l=2, m=2, c=2)
        sdh = take(768, F16).rearrange("p (l j n) -> p l j n", l=2, j=3)
        sl = take(1024).rearrange("p (b n) -> p b n", b=2)
        af = take(1024).rearrange("p (b n) -> p b n", b=2)
        ah = take(3072, F16).rearrange("p (b l j n) -> p b l j n", b=2, l=2, j=3)
        yst = take(2048).rearrange("p (b t n) -> p b t n", b=2, t=4)
        shared_end = at[0]
        BE = take(NB * ROW).rearrange("p (b n) -> p b n", b=NB)
        BT = take(2 * 192).rearrange("p (b n) -> p b n", b=2)
        sl2 = take(2 * 192).rearrange("p (b n) -> p b n", b=2)
        ac2 = take(2 * 192).rearrange("p (b j n) -> p b j n", b=2, j=2)
        OW = take(4 * 256).rearrange("p (b n) -> p b n", b=4)
        OUT95 = take(256)
        LB = take(ROW)
        assert at[0] <= 16384
        fin = Wf[:, 0:3 * 2 * 1024].rearrange("p (b k t n) -> p b k t n", b=2, k=3, t=4)
        ft = Wf[:, 6144:6144 + 2048].rearrange("p (b t n) -> p b t n", b=2, t=4)
        assert 6144 + 2048 <= shared_end
        EG = RB[:, 0:NRING * 704].rearrange("p (b n) -> p b n", b=NRING)
        ED = RB[:, NRING * 704:NRING * (704 + 512)].rearrange("p (b n) -> p b n", b=NRING)
        W95T = HT[0:64, :, :, :].rearrange("p a b c -> p (a b c)").bitcast(F32)[:, 0:4096]
        wix = sb("wix", [96, NB, 1], U32)
        lmax = sb("lmax", [64, 1])
        lix = sb("lix", [64, 1], U32)

        names = ("c0 cg cd gt S nm e r pn pt ph pl pv oh ol wo q qh ql k kh kl v vh vl xc po fc wm wh wl "
                 "hd bi yi dd lb sw swh swl sg ssl saf sah sal sdn sy et ebt eg esl eac eo eow wix wt wtc").split()
        s = {n: sem(f"s_{n}") for n in names + ["mx"]}
        s_x = [sem(f"s_x{i}") for i in range(4)]
        s_st = [sem(f"s_st{i}") for i in range(NST)]
        s_x1 = [sem(f"s_x1{i}") for i in range(2)]
        s_sc = [sem(f"s_sc{i}") for i in range(2)]
        s_ew = [sem(f"s_ew{i}") for i in range(NRING)]
        s_be = [sem(f"s_be{i}") for i in range(NB)]
        s_ya = [sem(f"s_ya{i}") for i in range(2)]
        s_o95 = [sem(f"s_o95{i}") for i in range(4)]
        s_ys = [sem(f"s_ys{i}") for i in range(2)]
        s_fl = [sem(f"s_fl{i}") for i in range(2)]
        s_fo = [sem(f"s_fo{i}") for i in range(2)]

        plan = {k: {} for k in ("pe", "act", "dve", "pool", "sp")}
        XC, PO, FC = Chain(s["xc"], plan), Chain(s["po"], plan), Chain(s["fc"], plan)
        PRO = -1
        END = NU + 3

        def stats(ch, which, slots, src, waits=()):
            v, y, a, b = (nw[:, which, k, :] for k in range(4))

            def bn(eng):
                for t in range(4):
                    r = eng.bn_stats(st[:, which, t, :], src(t))
                return r

            def ag(eng):
                for t in range(4):
                    r = eng.bn_aggr(mv[:, which, t, :], st[:, which, t, :])
                return r

            ch.step("dve", slots[0], bn, waits)
            ch.step("dve", slots[0], ag)
            ch.step("dve", slots[1], lambda e: e.tensor_scalar(v, mv[:, which, :, 1], EPS, None, ALU.add))
            ch.step("dve", slots[1], lambda e: e.tensor_scalar(y.bitcast(I32), v.bitcast(I32), -0.5, RSQRT_MAGIC,
                                                              ALU.mult, ALU.add))
            for k in range(3):
                sl_ = slots[1 + k]
                ch.step("dve", sl_, lambda e: e.tensor_tensor(a, y, y, ALU.mult))
                ch.step("dve", sl_, lambda e: e.scalar_tensor_tensor(out=b, in0=a, scalar=-0.5, in1=v,
                                                                     op0=ALU.mult, op1=ALU.mult))
                ch.step("dve", sl_, lambda e: e.scalar_tensor_tensor(out=y, in0=b, scalar=1.5, in1=y,
                                                                     op0=ALU.add, op1=ALU.mult))

        def normal(ch, which, slot, dst, src, waits=()):
            def f(eng):
                for t in range(4):
                    r = eng.tensor_scalar(dst(t), src(t), mv[:, which, t, 0:1], nw[:, which, 1, t:t + 1],
                                          ALU.subtract, ALU.mult)
                return r
            return ch.step("dve", slot, f, waits)

        p1_busy = {}

        def turn(ch, slot, src, c, dst, waits=(), wr=()):
            def pe(eng):
                for t in range(4):
                    r = eng.transpose(bP1[:, t * 128:(t + 1) * 128], src(t, c), ident[:, :])
                return r
            ch.step("pe", slot, pe, waits)
            ch.step("act", slot + 1 if slot >= 0 else slot,
                    lambda e: e.activation(dst(0), bP1[:, :], ACT.Copy, scale=SX), wr)
            n = ch.step("dve", slot + 1 if slot >= 0 else slot,
                        lambda e: e.scalar_tensor_tensor(out=dst(1), in0=bP1[:, :], scalar=SX, in1=dst(0),
                                                         op0=ALU.mult, op1=ALU.subtract))
            p1_busy[slot] = (ch.sem, n)

        def k_read(slot):
            return (s["kl"], min(NI, slot // 2 + 2))

        xt_ready = {}

        def x_jobs(bp):
            g = bp % 4
            base = (bp - 1) * 32

            def load(eng):
                if bp >= 4:
                    eng.wait_ge(s_x1[bp % 2], 16 * ((bp - 4) // 2 + 1))
                eng.dma_start(X[:, g, :, :], x[bp * 512:(bp + 1) * 512, :].rearrange("(t p) d -> p t d", p=128)
                              ).then_inc(s_x[g], 16)

            plan["sp"].setdefault(PRO if bp < 3 else base, []).append(load)
            sl_ = [PRO] * 8 if bp == 0 else [base + k for k in (2, 3, 4, 5, 6, 11, 13)]
            stats(XC, 0, sl_, lambda t: X[:, g, t, :], [(s_x[g], 16 * (bp // 4 + 1))])
            normal(XC, 0, sl_[4], lambda t: XN[:, t, :], lambda t: X[:, g, t, :])
            for c in range(2):
                w = [(s["cg"], 2)] if bp == 0 else [k_read(sl_[5 + c])]
                turn(XC, sl_[5 + c], lambda t, c: XN[:, t, c * 128:(c + 1) * 128], c,
                     lambda l, c=c: XT[:, bp % 2, l, c, :], w, [(s["k"], max(0, 16 * (bp - 1)))])
            xt_ready[bp] = XC.n

        wjobs = []
        for m, ch in [(0, 0), (1, 0), (2, 0), (2, 1), (3, 0), (0, 1), (1, 1), (2, 2), (3, 1),
                      (0, 2), (1, 2), (2, 3), (3, 2), (0, 3), (1, 3), (3, 3)]:
            wjobs += [(m, ch, 0), (m, ch, 1)]
        w_ready = {}

        def w_job(n):
            m, chn, c = wjobs[n]
            b = n % NST
            slot = PRO if n < 10 else n - 10

            def load(eng):
                if n >= NST:
                    eng.wait_ge(s["wl"], n - NST + 1)
                if m < 3:
                    src = wc[m, c * 128:(c + 1) * 128, chn * 512:(chn + 1) * 512]
                    eng.dma_start(SC_[:, b, :], src).then_inc(s_st[b], 16)
                    for g in range(4):
                        eng.dma_start(SS_[32 * g:32 * g + 32, b, :],
                                      wsc[m, c * 4 + g:c * 4 + g + 1, chn * 512:(chn + 1) * 512].broadcast_to([32, 512])
                                      ).then_inc(s_st[b], 16)
                else:
                    h = chn * 4 + c * 2
                    eng.dma_start(SC_[:, b, :].rearrange("p (h n) -> p h n", h=2),
                                  wo_c[h * 128:(h + 2) * 128, :].rearrange("(h p) n -> p h n", p=128)
                                  ).then_inc(s_st[b], 16)
                    for g in range(4):
                        for q in range(2):
                            eng.dma_start(SS_[32 * g:32 * g + 32, b, q * 256:(q + 1) * 256],
                                          wo_s[(h + q) * 4 + g:(h + q) * 4 + g + 1, :].broadcast_to([32, 256])
                                          ).then_inc(s_st[b], 16)

            cnt = sum(5 if wjobs[k][0] < 3 else 9 for k in range(b, n + 1, NST))
            plan["sp"].setdefault(slot, []).append(load)
            if m < 3:
                o = c * 2048 + chn * 512
            else:
                o = (chn * 4 + c * 2) * 256
            hi, lo = W[:, m, 0, o:o + 512], W[:, m, 1, o:o + 512]

            def scaled(eng):
                eng.wait_ge(s_st[b], 16 * cnt)
                eng.tensor_tensor(SC_[:, b, :], SC_[:, b, :], SS_[:, b, :], ALU.mult).then_inc(s["wm"], 1)

            def high(eng):
                eng.wait_ge(s["wm"], n + 1)
                eng.activation(hi, SC_[:, b, :], ACT.Copy, scale=SW).then_inc(s["wh"], 1)

            def low(eng):
                eng.wait_ge(s["wh"], n + 1)
                eng.scalar_tensor_tensor(out=lo, in0=SC_[:, b, :], scalar=SW, in1=hi,
                                         op0=ALU.mult, op1=ALU.subtract).then_inc(s["wl"], 1)

            first = slot == PRO
            plan["pool"].setdefault(slot, []).append(scaled)
            plan["act"].setdefault(PRO if first else slot + 1, []).append(high)
            plan["dve"].setdefault(PRO if first else slot + 2, []).append(low)
            w_ready[wjobs[n]] = n + 1

        def after_w(m, chn):
            return w_ready[(m, chn, 1)]

        ht_ready, acc_free, m_ready = {}, {}, {}

        def post_jobs(bp):
            g, base = bp % 4, (bp + 1) * 32
            rt = bp % 2

            def at_(k):
                return base + k

            for h in range(2):
                acc_free[(bp, h)] = PO.step(
                    "dve", at_(2 + h),
                    lambda e, h=h: e.scalar_tensor_tensor(out=A[:, 2 * h:2 * h + 2, :].rearrange("p t n -> p (t n)"),
                                                          in0=bACC[h][:, :], scalar=1.0 / (SO * SW), in1=bo2[:, :],
                                                          op0=ALU.mult, op1=ALU.add),
                    [(s["wo"], (bp + 1) * 32 - 1 + h), (s["cd"], 16 * 3)])
            stats(PO, 1, [at_(k) for k in (4, 5, 6, 7)], lambda t: A[:, t, :])
            normal(PO, 1, at_(8), lambda t: A[:, t, :], lambda t: A[:, t, :])
            PO.step("dve", at_(9), lambda e: e.tensor_tensor(X[:, g, :, :].rearrange("p t n -> p (t n)"),
                                                             X[:, g, :, :].rearrange("p t n -> p (t n)"),
                                                             A[:, :, :].rearrange("p t n -> p (t n)"), ALU.add))
            stats(PO, 1, [at_(k) for k in (10, 11, 12, 12)], lambda t: X[:, g, t, :])
            w = []
            if bp >= 2:
                w = [(s_sc[rt], 16 * 24 * (bp // 2)), (s["hd"], 16 * (bp - 1))]
            n = normal(PO, 1, at_(13), lambda t: RT[:, rt, t, 0:D], lambda t: X[:, g, t, :], w)

            def store(eng, n=n):
                eng.wait_ge(s["po"], n)
                eng.dma_start(Xd[bp * 512:(bp + 1) * 512, :].rearrange("(t p) d -> p t d", p=128), X[:, g, :, :]
                              ).then_inc(s_x1[bp % 2], 16)
                if bp:
                    eng.wait_ge(s["hd"], 16 * bp)
                eng.dma_start(Hd[bp * 512:(bp + 1) * 512, :].rearrange("(t p) d -> p t d", p=128),
                              RT[:, rt, :, 0:D]).then_inc(s["hd"], 16)

            plan["sp"].setdefault(at_(14), []).append(store)
            for c in range(2):
                w = [k_read(at_(15 + 2 * c))]
                turn(PO, at_(15 + 2 * c), lambda t, c: RT[:, rt, t, c * 128:(c + 1) * 128], c,
                     lambda l, c=c: HT[:, l, c, bp * 512:(bp + 1) * 512], w)
            ht_ready[bp] = PO.n

            def logits(eng):
                for t in range(4):
                    k = 0
                    for c in range(2):
                        for a, b in ((0, 0), (0, 1), (1, 0)):
                            r = eng.matmul(bP1[:, t * E:(t + 1) * E],
                                           HT[:, a, c, bp * 512 + t * 128:bp * 512 + (t + 1) * 128],
                                           gT[:, b, c, :], start=(k == 0), stop=(k == 5))
                            k += 1
                return r

            PO.step("pe", at_(21), logits, [k_read(at_(21)), (s["c0"], 4)])
            lg = bP1[:, 0:4 * E].rearrange("p (t e) -> p t e", t=4)
            PO.step("dve", at_(22), lambda e: e.tensor_reduce(gm0[:, :], lg, AX, ALU.max, negate=True))
            PO.step("dve", at_(22), lambda e: e.tensor_scalar(gm1[:, :], gm0[:, :], 1.0 / (SX * SG), None, ALU.mult))

            def gexp(eng):
                for t in range(4):
                    r = eng.activation(Sx[:, t, :], bP1[:, t * E:(t + 1) * E], ACT.Exp, bias=gm1[:, t:t + 1],
                                       scale=1.0 / (SX * SG), accum_out=gsum[:, t:t + 1])
                return r

            n = PO.step("act", at_(22), gexp)
            p1_busy[at_(21)] = (PO.sem, n)
            PO.step("dve", at_(23), lambda e: e.reciprocal(grec[:, :], gsum[:, :]))
            PO.step("dve", at_(23), lambda e: e.tensor_tensor(Sx[:, :, :], Sx[:, :, :],
                                                              grec[:, :].unsqueeze(2).broadcast_to([128, 4, E]), ALU.mult))
            PO.step("dve", at_(23), lambda e: e.tensor_reduce(
                gs[:, :, :], Sx[:, :, :].rearrange("p t (g k) -> p t g k", k=8), AX, ALU.max))

            def four(f):
                def run(eng):
                    for t in range(4):
                        r = f(eng, t)
                    return r
                return run

            PO.step("dve", at_(24), four(lambda e, t: e.max(g8[:, t, :], gs[:, t, :])))
            PO.step("dve", at_(24), four(lambda e, t: e.max_index(gi[:, t, :], g8[:, t, :], gs[:, t, :])))
            PO.step("dve", at_(24), lambda e: e.tensor_tensor(
                geq[:, :, :, :], iota8[:, :].unsqueeze(1).unsqueeze(1).broadcast_to([128, 4, 3, 8]),
                gi[:, :, 0:3].unsqueeze(3).broadcast_to([128, 4, 3, 8]), ALU.is_equal), [(s["cg"], 13)])
            PO.step("dve", at_(24), lambda e: e.tensor_reduce(
                gk[:, :, :], geq[:, :, :, :].rearrange("p t k g -> p t g k"), AX, ALU.max))
            PO.step("dve", at_(25), lambda e: e.tensor_tensor(
                Tm[:, :, :].rearrange("p t (g k) -> p (t g) k", k=8),
                Sx[:, :, :].rearrange("p t (g k) -> p (t g) k", k=8),
                gk[:, :, :].rearrange("p t g -> p (t g)").unsqueeze(2).broadcast_to([128, 32, 8]), ALU.mult))
            PO.step("dve", at_(25), four(lambda e, t: e.max(t8[:, t, :], Tm[:, t, :])))
            PO.step("dve", at_(25), four(lambda e, t: e.max_index(ti[:, t, :], t8[:, t, :], Tm[:, t, :])))
            PO.step("dve", at_(26), four(lambda e, t: e.tensor_tensor(
                teq[:, t, :, :], iota64[:, :].unsqueeze(1).broadcast_to([128, 6, E]),
                ti[:, t, 0:6].unsqueeze(2).broadcast_to([128, 6, E]), ALU.is_equal)))
            PO.step("dve", at_(27), four(lambda e, t: e.tensor_reduce(
                M[:, t, :], teq[:, t, :, :].rearrange("p k e -> p e k"), AX, ALU.max)))
            PO.step("dve", at_(28), lambda e: e.tensor_tensor(RT[:, rt, :, D:D + E], Tm[:, :, :], M[:, :, :], ALU.mult))
            PO.step("dve", at_(28), lambda e: e.tensor_copy(RT[:, rt, :, D + E], tid[:, 4 * bp:4 * bp + 4]))

            def pos(eng):
                for t in range(4):
                    o = bP1[:, t * E:(t + 1) * E]
                    eng.matmul(o, ones[:, :], MC[:, :], start=True, stop=False)
                    for q in range(t):
                        eng.matmul(o, ones[:, :], M[:, q, :], start=False, stop=False)
                    r = eng.matmul(o, tri[:, :], M[:, t, :], start=False, stop=True)
                return r

            PO.step("pe", at_(29), pos, [k_read(at_(29))])
            pp = bP1[:, 0:4 * E].rearrange("p (t e) -> p t e", t=4)
            PO.step("dve", at_(30), lambda e: e.scalar_tensor_tensor(
                out=W95[:, 4 * bp:4 * bp + 4, :], in0=pp, scalar=CAP - 1.5, in1=RT[:, rt, :, D:D + E],
                op0=ALU.is_ge, op1=ALU.mult))
            PO.step("dve", at_(30), lambda e: e.scalar_tensor_tensor(
                out=KP[:, :, :], in0=pp, scalar=CAP - 1.5, in1=M[:, :, :], op0=ALU.is_lt, op1=ALU.mult))
            n = PO.step("dve", at_(30), lambda e: e.scalar_tensor_tensor(
                out=C1[:, :, :], in0=pp, scalar=-float(E), in1=K64[:, :].unsqueeze(1).broadcast_to([128, 4, E]),
                op0=ALU.mult, op1=ALU.add))
            p1_busy[at_(29)] = (PO.sem, n)
            PO.step("dve", at_(31), lambda e: e.tensor_tensor(C1[:, :, :], C1[:, :, :], KP[:, :, :], ALU.mult))
            PO.step("dve", at_(31), four(lambda e, t: e.max(c8[:, t, :], C1[:, t, :])))
            w = [(s_sc[rt], 16 * 24 * (bp // 2))] if bp >= 2 else []
            n = PO.step("dve", at_(31), lambda e: e.tensor_scalar(
                ix[:, rt, :, :].rearrange("p t k -> p (t k)"), c8[:, :, :].rearrange("p t k -> p (t k)"),
                -1.0, 8192.0, ALU.mult, ALU.add), w)
            for t in range(4):
                for k in range(6):
                    def scatter(eng, t=t, k=k, n=n):
                        eng.wait_ge(s["po"], n)
                        eng.wait_ge(s["bi"], 16 * 4)
                        eng.indirect_dma_start(BUF, bass.IndirectOffsetOnAxis(ap=ix[:, rt, t, k:k + 1], axis=0),
                                               RT[:, rt, t, :], None, bounds_check=CAP * E - 1, oob_is_err=False
                                               ).then_inc(s_sc[rt], 16)
                    plan["pool"].setdefault(at_(32 + t * 6 + k), []).append(scatter)
            PO.step("dve", at_(31), lambda e: e.tensor_reduce(
                Ms[:, :], M[:, :, :].rearrange("p t e -> p e t"), AX, ALU.add))
            PO.step("dve", at_(31), lambda e: e.tensor_tensor(MC[:, :], MC[:, :], Ms[:, :], ALU.add))
            PO.step("dve", at_(32), lambda e: e.scalar_tensor_tensor(
                out=Lt[:, :, :], in0=tid[:, 4 * bp:4 * bp + 4].unsqueeze(2).broadcast_to([128, 4, E]), scalar=1.0,
                in1=M[:, :, :], op0=ALU.add, op1=ALU.mult))
            PO.step("dve", at_(32), lambda e: e.tensor_reduce(
                Ls[:, :], Lt[:, :, :].rearrange("p t e -> p e t"), AX, ALU.max))
            PO.step("dve", at_(32), lambda e: e.tensor_tensor(L[:, :], L[:, :], Ls[:, :], ALU.max))

        x_jobs(0)
        for n in range(32):
            w_job(n)
        for bp in range(NP):
            if bp + 1 < NP:
                x_jobs(bp + 1)
            post_jobs(bp)

        LAST = NU + 33
        PO.step("dve", LAST, lambda e: e.memset(LB[0:E, D:D + E], 1.0), [(s["wo"], NU)])
        PO.step("dve", LAST, lambda e: e.memset(LB[0:E, D + E:ROW], FAR))
        PO.step("pe", LAST, lambda e: e.transpose(bP1[0:E, 0:128], L[:, :], ident[:, :]))
        PO.step("dve", LAST, lambda e: e.tensor_reduce(lmax[:, :], bP1[0:E, 0:128], AX, ALU.max))
        PO_END = PO.step("dve", LAST, lambda e: e.tensor_scalar(lix[:, :], lmax[:, :], -1.0, 0.0, ALU.add, ALU.max))

        fin_out = {}

        def final_jobs(g):
            b, slot = g % 2, 1000 + g
            banks = (bACC[0], bACC[1]) if b == 0 else (bP0, bP1)

            def mm(eng):
                for t in range(4):
                    r = eng.matmul(banks[t // 2][:, t % 2 * 256:(t % 2 + 1) * 256],
                                   W95T[:, (4 * g + t) * 128:(4 * g + t + 1) * 128], OUT95[0:E, :],
                                   start=True, stop=True)
                return r

            w = [(s["wtc"], NP)] + [(s_o95[k], 16 * E // 4) for k in range(4)] if g == 0 else []
            FC.step("pe", slot, mm, w)
            for h in range(2):
                w = [(s_fl[b], 48 * (g // 2 + 1))]
                if g >= 2:
                    w.append((s_fo[b], 16 * (g // 2)))
                FC.step("dve", slot, lambda e, h=h: e.tensor_tensor(
                    ft[:, b, 2 * h:2 * h + 2, :].rearrange("p t n -> p (t n)"), banks[h][:, :],
                    fin[:, b, 0, 2 * h:2 * h + 2, :].rearrange("p t n -> p (t n)"), ALU.add), w)
            FC.step("dve", slot, lambda e: e.tensor_tensor(ft[:, b, :, :], ft[:, b, :, :], fin[:, b, 1, :, :], ALU.add))
            stats(FC, 0, [slot] * 4, lambda t: ft[:, b, t, :])
            normal(FC, 0, slot, lambda t: ft[:, b, t, :], lambda t: ft[:, b, t, :])
            fin_out[g] = FC.step("dve", slot, lambda e: e.tensor_tensor(ft[:, b, :, :], ft[:, b, :, :],
                                                                       fin[:, b, 2, :, :], ALU.add))

        last_slot = max(max(v) for v in plan.values())
        for g in range(NP):
            final_jobs(g)

        def run_plan(who, eng, slot):
            for f in plan[who].get(slot, []):
                f(eng)

        SLOTS = range(0, END)
        TAIL = range(END, last_slot + 1)
        UP = {NU + 6: 0, NU + 12: 1, NU + 20: 2, NU + 26: 3, NU + 34: 4, NU + 35: 5, NU + 36: 6, NU + 37: 7}
        DN = {NU + 19: 0, NU + 24: 1, NU + 30: 2, NU + 34: 3, NU + 35: 4, NU + 36: 5, NU + 37: 6, NU + 38: 7}
        GB = ((bS[0], bS[1]), (bPT, bO))
        MT = (128, 128, 96)

        block = ctx.enter_context(nc.Block())

        @block.sync
        def _(eng):
            eng.dma_start(bqk[:, :, :], bqkv).then_inc(s["cd"], 16)
            for k in range(2):
                eng.dma_start(bo2[:, 256 * k:256 * k + 256],
                              bo.rearrange("(a n) -> a n", a=1).broadcast_to([128, 256])).then_inc(s["cd"], 16)
            eng.dma_start(gTf[:, :, :], gateT.rearrange("(c p) e -> p c e", p=128)).then_inc(s["gt"], 16)
            run_plan("sp", eng, PRO)
            for slot in SLOTS:
                run_plan("sp", eng, slot)
                if 24 <= slot < 32 and slot % 2 == 0:
                    n = (slot - 24) // 2
                    eng.wait_ge(s["S"], slot)
                    eng.wait_ge(s["cg"], 11)
                    eng.dma_start(BUF[n * 1536:(n + 1) * 1536, :].rearrange("(k p) c -> p k c", p=128),
                                  zrow[:, :].unsqueeze(1).broadcast_to([128, 12, ROW])).then_inc(s["bi"], 16)
                if 32 <= slot < 48 and slot % 2 == 0:
                    n = (slot - 32) // 2
                    eng.wait_ge(s["S"], slot)
                    eng.dma_start(Y[1][n * 512:(n + 1) * 512, :].rearrange("(k p) c -> p k c", p=128),
                                  zrow[:, 0:D].unsqueeze(1).broadcast_to([128, 4, D])).then_inc(s["yi"], 16)
            eng.wait_ge(s["wo"], NU)
            for m in range(2):
                eng.dma_start(sgf[:, m, :, :], sguT[m].rearrange("(c p) n -> p c n", p=128)).then_inc(s["sw"], 16)
            eng.dma_start(sdf[:, 0:2, :], sdT[0:256, :].rearrange("(j p) n -> p j n", p=128)).then_inc(s["sw"], 16)
            eng.dma_start(sdf[0:96, 2, :], sdT[256:352, :]).then_inc(s["sw"], 16)

            def expert_weights(e):
                b = e % NRING
                if e >= NRING:
                    eng.wait_ge(s["eo"], e - NRING + 1)
                eng.dma_start(EG[:, b, :], ewT[e]).then_inc(s_ew[b], 16)
                eng.dma_start(ED[0:88, b, :], ewd[e]).then_inc(s_ew[b], 16)

            def expert_rows(e):
                b = e % NB
                if e >= NB:
                    eng.wait_ge(s["eow"], e - NB + 1)
                    eng.wait_ge(s["wix"], e - NB + 1)
                eng.dma_start(BE[0:CAP, b, :], BUF.rearrange("(s e) c -> e s c", e=E)[e]).then_inc(s_be[b], 16)

            for e in range(NRING):
                expert_weights(e)
            g = 0
            for slot in TAIL:
                run_plan("sp", eng, slot)
                if slot - 1 in DN:
                    eng.wait_ge(s["sy"], 2 * (g + 1))
                    eng.dma_start(Y[0][g * 512:(g + 1) * 512, :].rearrange("(t p) d -> p t d", p=128),
                                  yst[:, g % 2, :, :]).then_inc(s_ys[g % 2], 16)
                    g += 1
            assert g == NP
            eng.wait_ge(s["lb"], 16)
            eng.wait_ge(s["po"], PO_END)
            for k in range(2):
                eng.wait_ge(s_sc[k], 16 * 24 * 4)
            eng.dma_start(BUF[(CAP - 1) * E:CAP * E, :], LB[0:E, :]).then_inc(s["dd"], 16)
            eng.wait_ge(s["dd"], 16)
            for e in range(NB):
                expert_rows(e)
            for e in range(E):
                if e + NRING < E:
                    expert_weights(e + NRING)
                if e + NB < E:
                    expert_rows(e + NB)
                eng.wait_ge(s["eow"], e + 1)
                eng.dma_start(OUT95[e:e + 1, :], OW[CAP - 1:CAP, e % 4, :]).then_inc(s_o95[e % 4], 16)

            def put(g):
                eng.wait_ge(s["fc"], fin_out[g])
                eng.dma_start(out[g * 512:(g + 1) * 512, :].rearrange("(t p) d -> p t d", p=128), ft[:, g % 2, :, :]
                              ).then_inc(s_fo[g % 2], 16)

            for k in range(2):
                eng.wait_ge(s_ya[k], 16 * 32)
                eng.wait_ge(s_x1[k], 16 * 4)
            eng.wait_ge(s["sdn"], 4 * NP)
            for g in range(NP):
                b = g % 2
                if g >= 2:
                    eng.wait_ge(s["fc"], fin_out[g - 2])
                for k, src in enumerate((Y[0], Y[1], Xd)):
                    eng.dma_start(fin[:, b, k, :, :], src[g * 512:(g + 1) * 512, :].rearrange("(t p) d -> p t d", p=128)
                                  ).then_inc(s_fl[b], 16)
                if g >= 1:
                    put(g - 1)
            put(NP - 1)
            for k in range(2):
                eng.wait_ge(s_fo[k], 16 * 4)

        @block.gpsimd
        def _(eng):
            cg = [0]

            def c(ins, wait=False):
                ins.then_inc(s["cg"], 1)
                cg[0] += 1
                if wait:
                    eng.wait_ge(s["cg"], cg[0])

            c(eng.memset(ident[:, :], 0.0), True)
            c(eng.affine_select(out=ident[:, :], in_=ident[:, :], compare_op=ALU.not_equal, fill=1.0, base=0,
                                pattern=[[-1, 128]], channel_multiplier=1))
            run_plan("pool", eng, PRO)
            c(eng.memset(tri[:, :], 1.0), True)
            c(eng.affine_select(out=tri[:, :], in_=tri[:, :], compare_op=ALU.is_gt, fill=0.0, base=0,
                                pattern=[[1, 128]], channel_multiplier=-1))
            c(eng.memset(ones[:, :], 1.0))
            for t_, pat, base, cm in ((iota8, [[1, 8]], 0, 0), (iota64, [[1, E]], 0, 0), (K64, [[-1, E]], 8192, 0),
                                      (tid, [[128, 32]], 0, 1)):
                c(eng.iota(t_[:, :], pattern=pat, base=base, channel_multiplier=cm,
                           allow_small_or_imprecise_dtypes=True))
            c(eng.memset(zrow[:, :], 0.0), True)
            c(eng.memset(zrow[:, ROW - 1:ROW], FAR))
            c(eng.memset(MC[:, :], 0.0))
            c(eng.memset(L[:, :], 0.0))
            for u in SLOTS:
                if u < NU:
                    b = u % 2
                    eng.wait_ge(s["r"], u + 1)
                    p = P[:, b, :].rearrange("p (t k) -> p t k", t=2)
                    eng.tensor_tensor(p, p, rr[:, u % 4, :].unsqueeze(2).broadcast_to([128, 2, 256]), ALU.mult
                                      ).then_inc(s["pn"], 1)
                run_plan("pool", eng, u)
            for slot in TAIL:
                run_plan("pool", eng, slot)
            eng.wait_ge(s["po"], PO_END)
            eng.wait_ge(s["hd"], 16 * NP)
            eng.indirect_dma_start(LB[0:E, 0:D], None, Hd, bass.IndirectOffsetOnAxis(ap=lix[:, 0:1], axis=0),
                                   bounds_check=4095, oob_is_err=False).then_inc(s["lb"], 16)
            for k in range(2):
                eng.wait_ge(s_ys[k], 16 * 4)
            eng.wait_ge(s["yi"], 16 * 8)
            for e in range(E):
                eng.wait_ge(s["eow"], e + 1)
                eng.wait_ge(s["wix"], e + 1)
                if e >= 2:
                    eng.wait_ge(s_ya[e % 2], 16 * (e // 2))
                eng.indirect_dma_start(Y[e % 2], bass.IndirectOffsetOnAxis(ap=wix[:, e % NB, :], axis=0),
                                       OW[0:CAP, e % 4, :], None, bounds_check=4095, oob_is_err=False,
                                       compute_op=ALU.add).then_inc(s_ya[e % 2], 16)

        @block.tensor
        def _(eng):
            PASS = ((0, 0), (0, 1), (1, 0))

            def proj_qk(i, m):
                bp, h = i // NH, i % NH
                bk_ = bP0 if m == 0 else bP1
                eng.wait_ge(s["xc"], xt_ready[bp])
                if bp == 0:
                    eng.wait_ge(s["wl"], w_ready[(m, h // 4, 1)])
                if m == 0:
                    if i:
                        eng.wait_ge(s["vl"], min(NI, i + 3))
                else:
                    eng.wait_ge(s["kl"], i)
                    if 2 * (i - 1) - 1 in p1_busy and i:
                        eng.wait_ge(*p1_busy[2 * (i - 1) - 1])
                k = 0
                for c in range(2):
                    for a, b in PASS:
                        r = eng.matmul(bk_[:, :], W[:, m, a, c * 2048 + h * 128:c * 2048 + (h + 1) * 128],
                                       XT[:, bp % 2, b, c, :], start=(k == 0), stop=(k == 5))
                        k += 1
                r.then_inc(s["q" if m == 0 else "k"], 1)

            def proj_v(j):
                g, t = j // 4, j % 4
                bp, hg = g // 4, g % 4
                eng.wait_ge(s["xc"], xt_ready[bp])
                if bp == 0:
                    eng.wait_ge(s["wl"], w_ready[(2, hg, 1)])
                eng.wait_ge(s["ql"], 1 if j < 4 else j - 2)
                if j < 4:
                    eng.wait_ge(s["vl"], j)
                k = 0
                for c in range(2):
                    for a, b in PASS:
                        r = eng.matmul(bP0[:, :], XT[:, bp % 2, a, c, t * 128:(t + 1) * 128],
                                       W[:, 2, b, c * 2048 + hg * 512:c * 2048 + (hg + 1) * 512],
                                       start=(k == 0), stop=(k == 5))
                        k += 1
                r.then_inc(s["v"], 1)

            def scores(u):
                i, q = u // 2, u % 2
                if q == 0:
                    eng.wait_ge(s["ql"], i + 1)
                    eng.wait_ge(s["kl"], i + 1)
                if u >= 2:
                    eng.wait_ge(s["e"], u - 1)
                for t in range(2):
                    for k, (a, b) in enumerate(PASS):
                        r = eng.matmul(bS[u % 2][:, t * 256:(t + 1) * 256],
                                       QK[:, i % 2, 0, a, q * 256 + t * 128:q * 256 + (t + 1) * 128],
                                       QK[:, i % 2, 1, b, q * 256:(q + 1) * 256], start=(k == 0), stop=(k == 2))
                r.then_inc(s["S"], 1)

            def turn_p(u):
                eng.wait_ge(s["pn"], u + 1)
                eng.wait_ge(s["pl"], u)
                for kc in range(2):
                    for t in range(2):
                        r = eng.transpose(bPT[:, kc * 256 + t * 128:kc * 256 + (t + 1) * 128],
                                          P[:, u % 2, t * 256 + kc * 128:t * 256 + (kc + 1) * 128], ident[:, :])
                r.then_inc(s["pt"], 1)

            def pv(u):
                i, q = u // 2, u % 2
                h = i % NH
                if u % 8 == 0:
                    eng.wait_ge(s["vl"], 4 * (i // 4 + 1))
                eng.wait_ge(s["pl"], u + 1)
                eng.wait_ge(s["ol"], u)
                k = 0
                for kc in range(2):
                    for a, b in PASS:
                        r = eng.matmul(bO[:, 0:256],
                                       V[:, i // 4 % 2, a, 2 * q + kc, h % 4 * 128:(h % 4 + 1) * 128],
                                       PT[:, u % 2, b, kc * 256:(kc + 1) * 256], start=(k == 0), stop=(k == 5))
                        k += 1
                r.then_inc(s["pv"], 1)

            def proj_o(u):
                i, q = u // 2, u % 2
                bp, h = i // NH, i % NH
                if bp == 0:
                    eng.wait_ge(s["wl"], w_ready[(3, h // 4, 1)])
                if h == 0 and bp:
                    eng.wait_ge(s["po"], acc_free[(bp - 1, q)])
                eng.wait_ge(s["ol"], u + 1)
                for t in range(2):
                    for k, (a, b) in enumerate(PASS):
                        r = eng.matmul(bACC[q][:, t * 256:(t + 1) * 256], O[:, u % 2, a, t * 128:(t + 1) * 128],
                                       W[:, 3, b, h * 256:(h + 1) * 256], start=(h == 0 and t == 0 and k == 0),
                                       stop=(h == NH - 1 and k == 2), skip_group_check=True)
                r.then_inc(s["wo"], 1)

            run_plan("pe", eng, PRO)
            proj_qk(0, 0)
            proj_qk(0, 1)
            for j in range(4):
                proj_v(j)
            for u in SLOTS:
                i = u // 2
                if u < NU:
                    scores(u)
                    if u % 2 == 0 and i + 1 < NI:
                        proj_qk(i + 1, 0)
                        proj_qk(i + 1, 1)
                    if u % 2 == 1 and i + 4 < NI:
                        proj_v(i + 4)
                if 0 <= u - 2 < NU:
                    pv(u - 2)
                if 0 <= u - 3 < NU:
                    proj_o(u - 3)
                if 0 <= u - 1 < NU:
                    turn_p(u - 1)
                run_plan("pe", eng, u)

            def shared_up(g):
                for j in range(3):
                    k = 3 * g + j
                    M_ = MT[j]
                    if k == 0:
                        eng.wait_ge(s["swl"], 3)
                        eng.wait_ge(s["e"], NU)
                    if k == 1:
                        eng.wait_ge(s["pl"], NU)
                        eng.wait_ge(s["ol"], NU)
                    if k >= 2:
                        eng.wait_ge(s["saf"], k - 1)
                    if j == 0:
                        eng.wait_ge(s["po"], ht_ready[g])
                    for m in range(2):
                        q = 0
                        for c in range(2):
                            for a, b in PASS:
                                r = eng.matmul(GB[k % 2][m][0:M_, :], sgh[:, a, m, c, j * 128:j * 128 + M_],
                                               HT[:, b, c, g * 512:(g + 1) * 512], start=(q == 0), stop=(q == 5))
                                q += 1
                    r.then_inc(s["sg"], 1)

            def shared_down(g):
                eng.wait_ge(s["sal"], 3 * (g + 1))
                for t in range(4):
                    if t % 2 == 0:
                        if g == 0:
                            eng.wait_ge(s["po"], acc_free[(NP - 1, t // 2)])
                        else:
                            eng.wait_ge(s["sy"], 2 * (g - 1) + t // 2 + 1)
                    q = 0
                    for j in range(3):
                        for a, b in PASS:
                            r = eng.matmul(bACC[t // 2][:, t % 2 * 256:(t % 2 + 1) * 256],
                                           ah[0:MT[j], g % 2, a, j, t * 128:(t + 1) * 128],
                                           sdh[0:MT[j], b, j, :], start=(q == 0), stop=(q == 8))
                            q += 1
                    r.then_inc(s["sdn"], 1)

            for slot in TAIL:
                run_plan("pe", eng, slot)
                if slot in UP:
                    shared_up(UP[slot])
                if slot in DN:
                    shared_down(DN[slot])

            for g in range(NP):
                if g == 0:
                    eng.wait_ge(s["sy"], 2 * NP)
                    eng.wait_ge(s["po"], PO_END)
                if g >= 2:
                    eng.wait_ge(s["wtc"], g - 1)
                for t in range(4):
                    r = eng.transpose(bACC[g % 2][0:E, t * 128:(t + 1) * 128], W95[:, 4 * g + t, :], ident[:, :])
                r.then_inc(s["wt"], 1)

            def e_turn(e):
                b = e % NB
                eng.wait_ge(s_be[b], 16 * (e // NB + 1))
                if e >= 2:
                    eng.wait_ge(s["ebt"], e - 1)
                for c in range(2):
                    r = eng.transpose((bP0, bP1)[e % 2][:, c * CAP:(c + 1) * CAP],
                                      BE[0:CAP, b, c * 128:(c + 1) * 128], ident[0:CAP, 0:CAP])
                r.then_inc(s["et"], 1)

            def e_up(e):
                b = e % NRING
                eng.wait_ge(s_ew[b], 32 * (e // NRING + 1))
                eng.wait_ge(s["ebt"], e + 1)
                if e >= 2:
                    eng.wait_ge(s["eac"], e - 1)
                else:
                    eng.wait_ge(s["saf"], 3 * NP)
                for m in range(2):
                    for j in range(2):
                        for c in range(2):
                            o = (m * 2 + c) * 176 + j * 88
                            r = eng.matmul(bS[e % 2][0:88, (m * 2 + j) * CAP:(m * 2 + j + 1) * CAP],
                                           EG[:, b, o:o + 88], BT[:, e % 2, c * CAP:(c + 1) * CAP],
                                           start=(c == 0), stop=(c == 1))
                r.then_inc(s["eg"], 1)

            def e_down(e):
                b = e % NRING
                eng.wait_ge(s["eac"], e + 1)
                if e >= 2:
                    eng.wait_ge(s["eow"], e - 1)
                for j in range(2):
                    r = eng.matmul((bPT, bO)[e % 2][0:CAP, 0:256], ac2[0:88, e % 2, j, :],
                                   ED[0:88, b, j * 256:(j + 1) * 256], start=(j == 0), stop=(j == 1))
                r.then_inc(s["eo"], 1)

            for e in range(E + 2):
                if e < E:
                    e_turn(e)
                if 0 <= e - 1 < E:
                    e_up(e - 1)
                if 0 <= e - 2 < E:
                    e_down(e - 2)
            for g in range(NP):
                run_plan("pe", eng, 1000 + g)

        @block.scalar
        def _(eng):
            def q_high(i, m):
                h = i % NH
                eng.wait_ge(s["q" if m == 0 else "k"], i + 1)
                if i >= 2:
                    eng.wait_ge(s["S"], 2 * i - 2)
                if i == 0:
                    eng.wait_ge(s["c0"], 2)
                eng.activation(QK[:, i % 2, m, 0, :], (bP0 if m == 0 else bP1)[:, :], ACT.Identity,
                               bias=bqk[:, m, h:h + 1]).then_inc(s["qh" if m == 0 else "kh"], 1)

            def v_high(j):
                eng.wait_ge(s["v"], j + 1)
                if j >= 8:
                    eng.wait_ge(s["pv"], 8 * (j // 4 - 1))
                eng.activation(V[:, j // 4 % 2, 0, j % 4, :], bP0[:, :], ACT.Copy, scale=SV / (SX * SW)
                               ).then_inc(s["vh"], 1)

            run_plan("act", eng, PRO)
            q_high(0, 0)
            q_high(0, 1)
            for j in range(4):
                v_high(j)
            for u in SLOTS:
                i = u // 2
                if 0 <= u - 2 < NU:
                    w = u - 2
                    eng.wait_ge(s["pt"], w + 1)
                    if w >= 2:
                        eng.wait_ge(s["pv"], w - 1)
                    eng.activation(PT[:, w % 2, 0, :], bPT[:, :], ACT.Copy, scale=SP_).then_inc(s["ph"], 1)
                run_plan("act", eng, u)
                if u < NU:
                    eng.wait_ge(s["nm"], u + 1)
                    if u >= 2:
                        eng.wait_ge(s["pt"], u - 1)
                    for t in range(2):
                        r = eng.activation(P[:, u % 2, t * 256:(t + 1) * 256], bS[u % 2][:, t * 256:(t + 1) * 256],
                                           ACT.Exp, bias=nm[:, u % 4, t:t + 1], scale=SCALE / (SQ * SQ),
                                           accum_out=rs[:, u % 4, t:t + 1])
                    r.then_inc(s["e"], 1)
                    if u % 2 == 0 and i + 1 < NI:
                        q_high(i + 1, 0)
                        q_high(i + 1, 1)
                    if u % 2 == 1 and i + 4 < NI:
                        v_high(i + 4)
                if 0 <= u - 2 < NU:
                    w = u - 2
                    h = w // 2 % NH
                    eng.wait_ge(s["pv"], w + 1)
                    if w >= 2:
                        eng.wait_ge(s["wo"], w - 1)
                    eng.activation(O[:, w % 2, 0, :], bO[:, 0:256], ACT.Identity, bias=bqk[:, 2, h:h + 1]
                                   ).then_inc(s["oh"], 1)
            eng.wait_ge(s["sw"], 16 * 4)
            eng.activation(sgh[:, 0, :, :, :], sgf, ACT.Copy, scale=SG).then_inc(s["swh"], 1)
            eng.activation(sdh[:, 0, 0:2, :], sdf[:, 0:2, :], ACT.Copy, scale=SG).then_inc(s["swh"], 1)
            eng.activation(sdh[0:96, 0, 2, :], sdf[0:96, 2, :], ACT.Copy, scale=SG).then_inc(s["swh"], 1)

            def act_up(g):
                for j in range(3):
                    k = 3 * g + j
                    eng.wait_ge(s["sg"], k + 1)
                    if k >= 2:
                        eng.wait_ge(s["saf"], k - 1)
                    eng.activation(sl[0:MT[j], k % 2, :], GB[k % 2][0][0:MT[j], :], ACT.Silu, scale=1.0 / (SX * SG)
                                   ).then_inc(s["ssl"], 1)
                    eng.wait_ge(s["saf"], k + 1)
                    if g >= 2:
                        eng.wait_ge(s["sdn"], 4 * (g - 1))
                    eng.activation(ah[0:MT[j], g % 2, 0, j, :], af[0:MT[j], k % 2, :], ACT.Copy
                                   ).then_inc(s["sah"], 1)

            def act_down(g):
                for h in range(2):
                    eng.wait_ge(s["sdn"], 4 * g + 2 * h + 2)
                    if g >= 2:
                        eng.wait_ge(s_ys[g % 2], 16 * (g // 2))
                    eng.activation(yst[:, g % 2, 2 * h:2 * h + 2, :].rearrange("p t n -> p (t n)"), bACC[h][:, :],
                                   ACT.Copy, scale=1.0 / (SA * SG)).then_inc(s["sy"], 1)

            for slot in TAIL:
                run_plan("act", eng, slot)
                if slot in UP:
                    act_up(UP[slot])
                if slot in DN:
                    act_down(DN[slot])
            for g in range(NP):
                eng.wait_ge(s["wt"], g + 1)
                if g == 0:
                    eng.wait_ge(s["sg"], 3 * NP)
                eng.activation(W95T[:, g * 512:(g + 1) * 512], bACC[g % 2][0:E, :], ACT.Copy).then_inc(s["wtc"], 1)

            def e_silu(e):
                eng.wait_ge(s["eg"], e + 1)
                if e >= 2:
                    eng.wait_ge(s["eac"], e - 1)
                eng.activation(sl2[0:88, e % 2, :], bS[e % 2][0:88, 0:192], ACT.Silu).then_inc(s["esl"], 1)

            def e_out(e):
                eng.wait_ge(s["eo"], e + 1)
                if e >= 4:
                    eng.wait_ge(s_ya[e % 2], 16 * (e // 2 - 1))
                    eng.wait_ge(s_o95[e % 4], 16 * (e // 4))
                eng.activation(OW[0:CAP, e % 4, :], (bPT, bO)[e % 2][0:CAP, 0:256], ACT.Copy,
                               scale=BE[0:CAP, e % NB, D + e:D + e + 1]).then_inc(s["eow"], 1)

            for e in range(E + 2):
                if 0 <= e - 1 < E:
                    e_silu(e - 1)
                if 0 <= e - 2 < E:
                    e_out(e - 2)

        @block.vector
        def _(eng):
            eng.wait_ge(s["cd"], 16 * 3)
            eng.tensor_scalar(bqk[:, 0:2, :], bqk[:, 0:2, :], SQ, None, ALU.mult).then_inc(s["c0"], 1)
            eng.tensor_scalar(bqk[:, 2, :], bqk[:, 2, :], SO, None, ALU.mult).then_inc(s["c0"], 1)
            run_plan("dve", eng, PRO)

            def q_low(i, m):
                h = i % NH
                eng.wait_ge(s["qh" if m == 0 else "kh"], i + 1)
                eng.scalar_tensor_tensor(out=QK[:, i % 2, m, 1, :], in0=(bP0 if m == 0 else bP1)[:, :],
                                         scalar=bqk[:, m, h:h + 1], in1=QK[:, i % 2, m, 0, :],
                                         op0=ALU.add, op1=ALU.subtract).then_inc(s["ql" if m == 0 else "kl"], 1)

            def v_low(j):
                eng.wait_ge(s["vh"], j + 1)
                eng.scalar_tensor_tensor(out=V[:, j // 4 % 2, 1, j % 4, :], in0=bP0[:, :], scalar=SV / (SX * SW),
                                         in1=V[:, j // 4 % 2, 0, j % 4, :], op0=ALU.mult, op1=ALU.subtract
                                         ).then_inc(s["vl"], 1)

            q_low(0, 0)
            q_low(0, 1)
            for j in range(4):
                v_low(j)
            eng.wait_ge(s["gt"], 16)
            eng.tensor_scalar(gT[:, 0, :, :], gTf[:, :, :], SG, None, ALU.mult).then_inc(s["c0"], 1)
            eng.wait_ge(s["c0"], 3)
            eng.scalar_tensor_tensor(out=gT[:, 1, :, :], in0=gTf[:, :, :], scalar=SG, in1=gT[:, 0, :, :],
                                     op0=ALU.mult, op1=ALU.subtract).then_inc(s["c0"], 1)
            for u in SLOTS:
                i = u // 2
                if u < NU:
                    eng.wait_ge(s["S"], u + 1)
                    eng.tensor_reduce(nm0[:, u % 4, :], bS[u % 2][:, :].rearrange("p (t k) -> p t k", t=2), AX,
                                      ALU.max, negate=True).then_inc(s["mx"], 1)
                    eng.wait_ge(s["mx"], u + 1)
                    eng.tensor_scalar(nm[:, u % 4, :], nm0[:, u % 4, :], SCALE / (SQ * SQ), None, ALU.mult
                                      ).then_inc(s["nm"], 1)
                if 0 <= u - 2 < NU:
                    w = u - 2
                    eng.wait_ge(s["ph"], w + 1)
                    eng.scalar_tensor_tensor(out=PT[:, w % 2, 1, :], in0=bPT[:, :], scalar=SP_,
                                             in1=PT[:, w % 2, 0, :], op0=ALU.mult, op1=ALU.subtract
                                             ).then_inc(s["pl"], 1)
                run_plan("dve", eng, u)
                if u < NU:
                    eng.wait_ge(s["e"], u + 1)
                    eng.reciprocal(rr[:, u % 4, :], rs[:, u % 4, :]).then_inc(s["r"], 1)
                    if u % 2 == 0 and i + 1 < NI:
                        q_low(i + 1, 0)
                        q_low(i + 1, 1)
                    if u % 2 == 1 and i + 4 < NI:
                        v_low(i + 4)
                if 0 <= u - 2 < NU:
                    w = u - 2
                    h = w // 2 % NH
                    eng.wait_ge(s["oh"], w + 1)
                    eng.scalar_tensor_tensor(out=O[:, w % 2, 1, :], in0=bO[:, 0:256], scalar=bqk[:, 2, h:h + 1],
                                             in1=O[:, w % 2, 0, :], op0=ALU.add, op1=ALU.subtract
                                             ).then_inc(s["ol"], 1)
            for n, (lo, f, hi) in enumerate(((sgh[:, 1, :, :, :], sgf, sgh[:, 0, :, :, :]),
                                             (sdh[:, 1, 0:2, :], sdf[:, 0:2, :], sdh[:, 0, 0:2, :]),
                                             (sdh[0:96, 1, 2, :], sdf[0:96, 2, :], sdh[0:96, 0, 2, :]))):
                eng.wait_ge(s["swh"], n + 1)
                for m in range(2 if n == 0 else 1):
                    pick = (lambda a: a[:, m, :, :]) if n == 0 else (lambda a: a)
                    r = eng.scalar_tensor_tensor(out=pick(lo), in0=pick(f), scalar=SG, in1=pick(hi),
                                                 op0=ALU.mult, op1=ALU.subtract)
                r.then_inc(s["swl"], 1)

            def dve_up(g):
                for j in range(3):
                    k = 3 * g + j
                    eng.wait_ge(s["ssl"], k + 1)
                    eng.scalar_tensor_tensor(out=af[0:MT[j], k % 2, :], in0=GB[k % 2][1][0:MT[j], :],
                                             scalar=SA / (SX * SG), in1=sl[0:MT[j], k % 2, :],
                                             op0=ALU.mult, op1=ALU.mult).then_inc(s["saf"], 1)
                    eng.wait_ge(s["sah"], k + 1)
                    eng.tensor_tensor(ah[0:MT[j], g % 2, 1, j, :], af[0:MT[j], k % 2, :],
                                      ah[0:MT[j], g % 2, 0, j, :], ALU.subtract).then_inc(s["sal"], 1)

            for slot in TAIL:
                run_plan("dve", eng, slot)
                if slot in UP:
                    dve_up(UP[slot])

            def e_rows(e):
                eng.wait_ge(s["et"], e + 1)
                if e >= 2:
                    eng.wait_ge(s["eg"], e - 1)
                eng.tensor_copy(BT[:, e % 2, :], (bP0, bP1)[e % 2][:, 0:192]).then_inc(s["ebt"], 1)
                if e >= NB:
                    eng.wait_ge(s_ya[e % 2], 16 * ((e - NB) // 2 + 1))
                eng.tensor_copy(wix[:, e % NB, :], BE[0:CAP, e % NB, ROW - 1:ROW]).then_inc(s["wix"], 1)

            def e_act(e):
                eng.wait_ge(s["esl"], e + 1)
                if e >= 2:
                    eng.wait_ge(s["eo"], e - 1)
                eng.tensor_tensor(ac2[0:88, e % 2, :, :].rearrange("p j n -> p (j n)"), bS[e % 2][0:88, 192:384],
                                  sl2[0:88, e % 2, :], ALU.mult).then_inc(s["eac"], 1)

            for e in range(E + 1):
                if e < E:
                    e_rows(e)
                if e >= 1:
                    e_act(e - 1)
            for g in range(NP):
                run_plan("dve", eng, 1000 + g)


def kernel(**inputs):
    import numpy as _np
    import concourse.bacc as _bacc
    from concourse import mybir as _mybir
    from concourse.bass_utils import run_bass_kernel_spmd as _run

    g = {k: _np.asarray(v) for k, v in inputs.items()}
    at = lambda n: g["L0_attn_" + n]
    ff = lambda n: g["L0_ffn_" + n]
    gu = _np.stack([ff("Wg"), ff("Wu")], 1)
    arrays = {
        "in_x": at("x").reshape(4096, 256),
        "in_wc": _np.stack([at("wq_codes"), at("wk_codes"), at("wv_codes")]),
        "in_ws": _np.stack([at("wq_scales"), at("wk_scales"), at("wv_scales")]),
        "in_oc": at("wo_codes"),
        "in_os": at("wo_scales"),
        "in_b": _np.stack([at("bq"), at("bk"), at("bv")]).reshape(3, 16, 128).transpose(2, 0, 1),
        "in_bo": at("bo"),
        "in_gate": ff("gate_weight").T,
        "in_sgu": _np.stack([ff("Sg").T, ff("Su").T]),
        "in_sd": ff("Sd").T,
        "in_ewT": gu.reshape(64, 2, 176, 2, 128).transpose(0, 4, 1, 3, 2).reshape(64, 128, 704),
        "in_ewd": ff("Wd").reshape(64, 256, 2, 88).transpose(0, 3, 2, 1).reshape(64, 88, 512),
    }
    arrays = {k: _np.ascontiguousarray(v) for k, v in arrays.items()}
    nc = _bacc.Bacc("TRN2", target_bir_lowering=False, num_devices=1)
    args = [nc.dram_tensor(k, a.shape, _mybir.dt.from_np(a.dtype), kind="ExternalInput").ap()
            for k, a in arrays.items()]
    out = nc.dram_tensor("out_0", (4096, 256), _mybir.dt.float32, kind="ExternalOutput").ap()
    build(nc, *args, out)
    r = _run(nc, [arrays], core_ids=[0])
    return r.results[0]["out_0"].reshape(16, 256, 256)
```

```python
from contextlib import ExitStack

import concourse.bass as bass
from concourse import mybir

F32 = mybir.dt.float32
F16 = mybir.dt.float16
U32 = mybir.dt.uint32
I32 = mybir.dt.int32
ALU = mybir.AluOpType
ACT = mybir.ActivationFunctionType
AX = mybir.AxisListType.X

NP = 8
NH = 16
NI = NP * NH
NU = 2 * NI
D = 256
E = 64
CAP = 96
NST = 3
SCALE = 128.0 ** -0.5
SX, SW, SQ, SV, SP_, SO = 4.0, 4.0, 16.0, 2.0, 64.0, 128.0
SG, SA = 64.0, 64.0
EPS = 1e-5
RSQRT_MAGIC = float(0x5F3759DF)
NOSIGN = 0x7FFF7FFF
FAR = 1.0e6
ROW = D + E + 1
NRING = 6
NB = 6


class Chain:

    def __init__(self, sem, plan):
        self.sem, self.plan, self.n = sem, plan, 0

    def step(self, engine, slot, fn, waits=()):
        before = self.n
        self.n += 1

        def run(eng):
            eng.wait_ge(self.sem, before)
            for s, v in waits:
                eng.wait_ge(s, v)
            fn(eng).then_inc(self.sem, 1)

        self.plan[engine].setdefault(slot, []).append(run)
        return self.n


def build(nc, x, wc, wsc, wo_c, wo_s, bqkv, bo, gateT, sguT, sdT, ewT, ewd, out):
    ctx = ExitStack()
    with ctx:
        def sb(name, shape, dt=F32):
            return ctx.enter_context(nc.sbuf_tensor(name, shape, dt))

        def sem(name):
            return ctx.enter_context(nc.semaphore(name))

        bank = [ctx.enter_context(nc.psum_tensor(f"bank{i}", [128, 512], F32)) for i in range(8)]
        bS, bPT, bO, bACC, bP0, bP1 = bank[0:2], bank[2], bank[3], bank[4:6], bank[6], bank[7]

        Hd = nc.dram_tensor("Hd", [4096, D], F32, kind="Internal").ap()
        Xd = nc.dram_tensor("Xd", [4096, D], F32, kind="Internal").ap()
        BUF = nc.dram_tensor("BUF", [CAP * E, ROW], F32, kind="Internal").ap()
        Y = [nc.dram_tensor(f"Y{i}", [4096, D], F32, kind="Internal").ap() for i in range(2)]

        X = sb("X", [128, 4, 4, D])
        W = sb("W", [128, 4, 2, 4096], F16)
        SC_ = sb("SC_", [128, NST, 512])
        SS_ = sb("SS_", [128, NST, 512])
        XN = sb("XN", [128, 4, D])
        RB = sb("RB", [128, 8192])
        RBh = RB[:, :].bitcast(F16)
        XT = RBh[:, 0:4096].rearrange("p (b l c n) -> p b l c n", b=2, l=2, c=2)
        QK = RBh[:, 4096:8192].rearrange("p (b m l n) -> p b m l n", b=2, m=2, l=2)
        V = RBh[:, 8192:16384].rearrange("p (b l t n) -> p b l t n", b=2, l=2, t=4)
        P = sb("P", [128, 2, 512])
        PT = sb("PT", [128, 2, 2, 512], F16)
        O = sb("O", [128, 2, 2, 256], F16)
        A = sb("A", [128, 4, D])
        RT = sb("RT", [128, 2, 4, ROW])
        HT = sb("HT", [128, 2, 2, 4096], F16)
        W95 = sb("W95", [128, 32, E])
        ident = sb("ident", [128, 128])
        tri = sb("tri", [128, 128], F16)
        ones = sb("ones", [128, 128], F16)
        bo2 = sb("bo2", [128, 512])
        bqk = sb("bqk", [128, 3, NH])
        gTf = sb("gTf", [128, 2, E])
        gT = sb("gT", [128, 2, 2, E], F16)
        iota64 = sb("iota64", [128, E])
        iota8 = sb("iota8", [128, 8])
        K64 = sb("K64", [128, E])
        tid = sb("tid", [128, 32])
        nm0 = sb("nm0", [128, 4, 2])
        nm = sb("nm", [128, 4, 2])
        rs = sb("rs", [128, 4, 2])
        rr = sb("rr", [128, 4, 2])
        st = sb("st", [128, 2, 4, 6])
        mv = sb("mv", [128, 2, 4, 2])
        nw = sb("nw", [128, 2, 4, 4])
        gm0 = sb("gm0", [128, 4])
        gm1 = sb("gm1", [128, 4])
        gsum = sb("gsum", [128, 4])
        grec = sb("grec", [128, 4])
        Sx = sb("Sx", [128, 4, E])
        Tm = sb("Tm", [128, 4, E])
        gs = sb("gs", [128, 4, 8])
        g8 = sb("g8", [128, 4, 8])
        gi = sb("gi", [128, 4, 8], U32)
        geq = sb("geq", [128, 4, 3, 8])
        gk = sb("gk", [128, 4, 8])
        t8 = sb("t8", [128, 4, 8])
        ti = sb("ti", [128, 4, 8], U32)
        teq = sb("teq", [128, 4, 6, E], F16)
        M = sb("M", [128, 4, E], F16)
        MC = sb("MC", [128, E], F16)
        Ms = sb("Ms", [128, E])
        L = sb("L", [128, E])
        Ls = sb("Ls", [128, E])
        C1 = sb("C1", [128, 4, E])
        Lt = C1
        lowbits = C1[:, :, :].rearrange("p t e -> p (t e)").bitcast(U32)
        low1, low2 = Ms[:, 32:33], Ms[0:1, 33:34]
        low3 = Ms[0:1, 34:35].bitcast(U32)
        KP = Sx
        c8 = sb("c8", [128, 4, 8])
        ix = sb("ix", [128, 2, 4, 8], U32)
        zrow = sb("zrow", [128, ROW])

        Wf = W[:, :, :, :].rearrange("p a b c -> p (a b c)").bitcast(F32)
        at = [0]

        def take(n, dt=F32):
            a = Wf[:, at[0]:at[0] + n]
            at[0] += n
            return a if dt == F32 else a.bitcast(dt)

        sgf = take(1408).rearrange("p (m c n) -> p m c n", m=2, c=2)
        sdf = take(768).rearrange("p (j n) -> p j n", j=3)
        sgh = take(1408, F16).rearrange("p (l m c n) -> p l m c n", l=2, m=2, c=2)
        sdh = take(768, F16).rearrange("p (l j n) -> p l j n", l=2, j=3)
        sl = take(1024).rearrange("p (b n) -> p b n", b=2)
        af = take(1024).rearrange("p (b n) -> p b n", b=2)
        ah = take(3072, F16).rearrange("p (b l j n) -> p b l j n", b=2, l=2, j=3)
        yst = take(2048).rearrange("p (b t n) -> p b t n", b=2, t=4)
        shared_end = at[0]
        BE = take(NB * ROW).rearrange("p (b n) -> p b n", b=NB)
        BT = take(2 * 192).rearrange("p (b n) -> p b n", b=2)
        sl2 = take(2 * 192).rearrange("p (b n) -> p b n", b=2)
        ac2 = take(2 * 192).rearrange("p (b j n) -> p b j n", b=2, j=2)
        OW = take(4 * 256).rearrange("p (b n) -> p b n", b=4)
        OUT95 = take(256)
        LB = take(ROW)
        assert at[0] <= 16384
        fin = Wf[:, 0:3 * 3 * 1024].rearrange("p (b k t n) -> p b k t n", b=3, k=3, t=4)
        ft = Wf[:, 9216:9216 + 2048].rearrange("p (b t n) -> p b t n", b=2, t=4)
        assert 9216 + 2048 <= shared_end
        EG = RB[:, 0:NRING * 704].rearrange("p (b n) -> p b n", b=NRING)
        ED = RB[:, NRING * 704:NRING * (704 + 512)].rearrange("p (b n) -> p b n", b=NRING)
        W95T = HT[0:64, :, :, :].rearrange("p a b c -> p (a b c)").bitcast(F32)[:, 0:4096]
        wix = sb("wix", [96, NB, 1], U32)
        lmax = sb("lmax", [64, 1])
        lix = sb("lix", [64, 1], U32)

        names = ("c0 cg cd gt S nm e r pn pt ph pl pv oh ol wo q qh ql k kh kl v vh vl xc po fc wm wh wl "
                 "lf lc fd hd bi yi dd lb sw swh swl sg ssl saf sah sal sdn sy et ebt eg esl eac eo eow wix wt wtc").split()
        s = {n: sem(f"s_{n}") for n in names + ["mx"]}
        s_x = [sem(f"s_x{i}") for i in range(4)]
        s_st = [sem(f"s_st{i}") for i in range(NST)]
        s_x1 = [sem(f"s_x1{i}") for i in range(2)]
        s_sc = [sem(f"s_sc{i}") for i in range(2)]
        s_ew = [sem(f"s_ew{i}") for i in range(NRING)]
        s_be = [sem(f"s_be{i}") for i in range(NB)]
        s_ya = [sem(f"s_ya{i}") for i in range(2)]
        s_o95 = [sem(f"s_o95{i}") for i in range(4)]
        s_ys = [sem(f"s_ys{i}") for i in range(2)]
        s_fl = [sem(f"s_fl{i}") for i in range(3)]
        s_fo = [sem(f"s_fo{i}") for i in range(2)]

        plan = {k: {} for k in ("pe", "act", "act_late", "dve", "pool", "sp")}
        XC, PO, LC = Chain(s["xc"], plan), Chain(s["po"], plan), Chain(s["lc"], plan)
        FC = [Chain(s["fc"], plan), Chain(s["fd"], plan)]
        PRO = -1
        END = NU + 3

        def stats(ch, which, slots, src, waits=()):
            v, y, a, b = (nw[:, which, k, :] for k in range(4))

            def bn(eng):
                for t in range(4):
                    r = eng.bn_stats(st[:, which, t, :], src(t))
                return r

            def ag(eng):
                for t in range(4):
                    r = eng.bn_aggr(mv[:, which, t, :], st[:, which, t, :])
                return r

            ch.step("dve", slots[0], bn, waits)
            ch.step("dve", slots[0], ag)
            ch.step("dve", slots[1], lambda e: e.tensor_scalar(v, mv[:, which, :, 1], EPS, None, ALU.add))
            ch.step("dve", slots[1], lambda e: e.tensor_scalar(y.bitcast(I32), v.bitcast(I32), -0.5, RSQRT_MAGIC,
                                                              ALU.mult, ALU.add))
            for k in range(3):
                sl_ = slots[1 + k]
                ch.step("dve", sl_, lambda e: e.tensor_tensor(a, y, y, ALU.mult))
                ch.step("dve", sl_, lambda e: e.scalar_tensor_tensor(out=b, in0=a, scalar=-0.5, in1=v,
                                                                     op0=ALU.mult, op1=ALU.mult))
                ch.step("dve", sl_, lambda e: e.scalar_tensor_tensor(out=y, in0=b, scalar=1.5, in1=y,
                                                                     op0=ALU.add, op1=ALU.mult))

        def normal(ch, which, slot, dst, src, waits=()):
            y, b = nw[:, which, 1, :], nw[:, which, 3, :]
            ch.step("dve", slot, lambda e: e.scalar_tensor_tensor(out=b, in0=mv[:, which, :, 0], scalar=-1.0, in1=y,
                                                                 op0=ALU.mult, op1=ALU.mult))

            def f(tiles):
                def run(eng):
                    for t in tiles:
                        r = eng.activation(dst(t), src(t), ACT.Identity, bias=nw[:, which, 3, t:t + 1],
                                           scale=nw[:, which, 1, t:t + 1])
                    return r
                return run

            if slot < 0 or slot >= END:
                return ch.step("act", slot, f(range(4)), waits)
            ch.step("act_late", slot, f((0, 1)), waits)
            return ch.step("act_late", slot + 1, f((2, 3)))

        p1_busy = {}

        def turn(ch, slot, src, c, dst, waits=(), wr=()):
            def pe(eng):
                for t in range(4):
                    r = eng.transpose(bP1[:, t * 128:(t + 1) * 128], src(t, c), ident[:, :])
                return r
            ch.step("pe", slot, pe, waits)
            ch.step("act", slot + 1 if slot >= 0 else slot,
                    lambda e: e.activation(dst(0), bP1[:, :], ACT.Copy, scale=SX), wr)
            n = ch.step("dve", slot + 1 if slot >= 0 else slot,
                        lambda e: e.scalar_tensor_tensor(out=dst(1), in0=bP1[:, :], scalar=SX, in1=dst(0),
                                                         op0=ALU.mult, op1=ALU.subtract))
            p1_busy[slot] = (ch.sem, n)

        def k_read(slot):
            return (s["kl"], min(NI, slot // 2 + 2))

        xt_ready = {}

        def x_jobs(bp):
            g = bp % 4
            base = (bp - 1) * 32

            def load(eng):
                if bp >= 4:
                    eng.wait_ge(s_x1[bp % 2], 16 * ((bp - 4) // 2 + 1))
                eng.dma_start(X[:, g, :, :], x[bp * 512:(bp + 1) * 512, :].rearrange("(t p) d -> p t d", p=128)
                              ).then_inc(s_x[g], 16)

            plan["sp"].setdefault(PRO if bp < 3 else base, []).append(load)
            sl_ = [PRO] * 8 if bp == 0 else [base + k for k in (2, 3, 4, 5, 6, 11, 13)]
            stats(XC, 0, sl_, lambda t: X[:, g, t, :], [(s_x[g], 16 * (bp // 4 + 1))])
            normal(XC, 0, sl_[4], lambda t: XN[:, t, :], lambda t: X[:, g, t, :])
            for c in range(2):
                w = [(s["cg"], 2)] if bp == 0 else [k_read(sl_[5 + c])]
                turn(XC, sl_[5 + c], lambda t, c: XN[:, t, c * 128:(c + 1) * 128], c,
                     lambda l, c=c: XT[:, bp % 2, l, c, :], w, [(s["k"], max(0, 16 * (bp - 1)))])
            xt_ready[bp] = XC.n

        wjobs = []
        for m, ch in [(0, 0), (1, 0), (2, 0), (2, 1), (3, 0), (0, 1), (1, 1), (2, 2), (3, 1),
                      (0, 2), (1, 2), (2, 3), (3, 2), (0, 3), (1, 3), (3, 3)]:
            wjobs += [(m, ch, 0), (m, ch, 1)]
        w_ready = {}

        def w_job(n):
            m, chn, c = wjobs[n]
            b = n % NST
            slot = PRO if n < 6 else {6: 0, 7: 0, 8: 1, 9: 1, 10: 2, 11: 2, 12: 3, 13: 3}.get(n, n - 10)

            def load(eng):
                if n >= NST:
                    eng.wait_ge(s["wl"], n - NST + 1)
                h = chn * 4 + c * 2
                for buf, q, o in ((SC_, wc, wo_c), (SS_, wsc, wo_s)):
                    if m < 3:
                        eng.dma_start(buf[:, b, :], q[m, c * 128:(c + 1) * 128, chn * 512:(chn + 1) * 512]
                                      ).then_inc(s_st[b], 16)
                    else:
                        eng.dma_start(buf[:, b, :].rearrange("p (h n) -> p h n", h=2),
                                      o[h * 128:(h + 2) * 128, :].rearrange("(h p) n -> p h n", p=128)
                                      ).then_inc(s_st[b], 16)

            cnt = 2 * (n // NST + 1)
            plan["sp"].setdefault(slot, []).append(load)
            if m < 3:
                o = c * 2048 + chn * 512
            else:
                o = (chn * 4 + c * 2) * 256
            hi, lo = W[:, m, 0, o:o + 512], W[:, m, 1, o:o + 512]

            def scaled(eng):
                eng.wait_ge(s_st[b], 16 * cnt)
                eng.tensor_tensor(SC_[:, b, :], SC_[:, b, :], SS_[:, b, :], ALU.mult).then_inc(s["wm"], 1)

            def high(eng):
                eng.wait_ge(s["wm"], n + 1)
                eng.activation(hi, SC_[:, b, :], ACT.Copy, scale=SW).then_inc(s["wh"], 1)

            def low(eng):
                eng.wait_ge(s["wh"], n + 1)
                eng.scalar_tensor_tensor(out=lo, in0=SC_[:, b, :], scalar=SW, in1=hi,
                                         op0=ALU.mult, op1=ALU.subtract).then_inc(s["wl"], 1)
                eng.wait_ge(s["wl"], n + 1)
                if n == 0:
                    eng.tensor_scalar(lowbits, lo.bitcast(U32), NOSIGN, None, ALU.bitwise_and).then_inc(s["lf"], 1)
                else:
                    eng.wait_ge(s["lf"], n)
                    eng.scalar_tensor_tensor(out=lowbits, in0=lo.bitcast(U32), scalar=NOSIGN, in1=lowbits,
                                             op0=ALU.bitwise_and, op1=ALU.bitwise_or).then_inc(s["lf"], 1)

            now = n < 14
            plan["pool"].setdefault(slot, []).append(scaled)
            plan["act"].setdefault(slot if now else slot + 1, []).append(high)
            plan["dve"].setdefault(slot if now else slot + 2, []).append(low)
            w_ready[wjobs[n]] = n + 1

        def flag_jobs():
            def rows(eng):
                eng.wait_ge(s["lf"], 32)
                return eng.tensor_reduce(low1, lowbits, AX, ALU.max)

            LC.step("dve", 25, rows)
            LC.step("pe", 27, lambda e: e.transpose(bP1[0:1, 0:128], low1, ident[:, :]), [k_read(27)])
            n = LC.step("dve", 28, lambda e: e.tensor_reduce(low2, bP1[0:1, 0:128], AX, ALU.max))
            p1_busy[27] = (LC.sem, n)
            return LC.step("dve", 28, lambda e: e.tensor_scalar(low3, low2, 1.0, None, ALU.min))

        ht_ready, acc_free, m_ready = {}, {}, {}

        def post_jobs(bp):
            g, base = bp % 4, (bp + 1) * 32
            rt = bp % 2

            def at_(k):
                return base + k

            for h in range(2):
                acc_free[(bp, h)] = PO.step(
                    "dve", at_(2 + h),
                    lambda e, h=h: e.scalar_tensor_tensor(out=A[:, 2 * h:2 * h + 2, :].rearrange("p t n -> p (t n)"),
                                                          in0=bACC[h][:, :], scalar=1.0 / (SO * SW), in1=bo2[:, :],
                                                          op0=ALU.mult, op1=ALU.add),
                    [(s["wo"], (bp + 1) * 32 - 1 + h), (s["cd"], 16 * 3)])
            stats(PO, 1, [at_(k) for k in (4, 5, 6, 7)], lambda t: A[:, t, :])
            normal(PO, 1, at_(7), lambda t: A[:, t, :], lambda t: A[:, t, :])
            for h in range(2):
                PO.step("pool", at_(9 + h), lambda e, h=h: e.tensor_tensor(
                    X[:, g, 2 * h:2 * h + 2, :], X[:, g, 2 * h:2 * h + 2, :], A[:, 2 * h:2 * h + 2, :], ALU.add))
            stats(PO, 1, [at_(k) for k in (11, 12, 12, 13)], lambda t: X[:, g, t, :])
            w = []
            if bp >= 2:
                w = [(s_sc[rt], 16 * 24 * (bp // 2)), (s["hd"], 16 * (bp - 1))]
            n = normal(PO, 1, at_(13), lambda t: RT[:, rt, t, 0:D], lambda t: X[:, g, t, :], w)

            def store(eng, n=n):
                eng.wait_ge(s["po"], n)
                eng.dma_start(Xd[bp * 512:(bp + 1) * 512, :].rearrange("(t p) d -> p t d", p=128), X[:, g, :, :]
                              ).then_inc(s_x1[bp % 2], 16)
                if bp:
                    eng.wait_ge(s["hd"], 16 * bp)
                eng.dma_start(Hd[bp * 512:(bp + 1) * 512, :].rearrange("(t p) d -> p t d", p=128),
                              RT[:, rt, :, 0:D]).then_inc(s["hd"], 16)

            plan["sp"].setdefault(at_(14), []).append(store)
            for c in range(2):
                w = [k_read(at_(15 + 2 * c))]
                turn(PO, at_(15 + 2 * c), lambda t, c: RT[:, rt, t, c * 128:(c + 1) * 128], c,
                     lambda l, c=c: HT[:, l, c, bp * 512:(bp + 1) * 512], w)
            ht_ready[bp] = PO.n

            def logits(eng):
                for t in range(4):
                    k = 0
                    for c in range(2):
                        for a, b in ((0, 0), (0, 1), (1, 0)):
                            r = eng.matmul(bP1[:, t * E:(t + 1) * E],
                                           HT[:, a, c, bp * 512 + t * 128:bp * 512 + (t + 1) * 128],
                                           gT[:, b, c, :], start=(k == 0), stop=(k == 5))
                            k += 1
                return r

            PO.step("pe", at_(21), logits, [k_read(at_(21)), (s["c0"], 4)])
            lg = bP1[:, 0:4 * E].rearrange("p (t e) -> p t e", t=4)
            PO.step("dve", at_(22), lambda e: e.tensor_reduce(gm0[:, :], lg, AX, ALU.max, negate=True))
            PO.step("dve", at_(22), lambda e: e.tensor_scalar(gm1[:, :], gm0[:, :], 1.0 / (SX * SG), None, ALU.mult))

            def gexp(eng):
                for t in range(4):
                    r = eng.activation(Sx[:, t, :], bP1[:, t * E:(t + 1) * E], ACT.Exp, bias=gm1[:, t:t + 1],
                                       scale=1.0 / (SX * SG), accum_out=gsum[:, t:t + 1])
                return r

            n = PO.step("act_late" if at_(22) < END else "act", at_(22), gexp)
            p1_busy[at_(21)] = (PO.sem, n)
            PO.step("dve", at_(23), lambda e: e.reciprocal(grec[:, :], gsum[:, :]))
            PO.step("dve", at_(23), lambda e: e.tensor_tensor(Sx[:, :, :], Sx[:, :, :],
                                                              grec[:, :].unsqueeze(2).broadcast_to([128, 4, E]), ALU.mult))
            PO.step("dve", at_(23), lambda e: e.tensor_reduce(
                gs[:, :, :], Sx[:, :, :].rearrange("p t (g k) -> p t g k", k=8), AX, ALU.max))

            def four(f):
                def run(eng):
                    for t in range(4):
                        r = f(eng, t)
                    return r
                return run

            PO.step("dve", at_(24), four(lambda e, t: e.max(g8[:, t, :], gs[:, t, :])))
            PO.step("dve", at_(24), four(lambda e, t: e.max_index(gi[:, t, :], g8[:, t, :], gs[:, t, :])))
            PO.step("dve", at_(24), lambda e: e.tensor_tensor(
                geq[:, :, :, :], iota8[:, :].unsqueeze(1).unsqueeze(1).broadcast_to([128, 4, 3, 8]),
                gi[:, :, 0:3].unsqueeze(3).broadcast_to([128, 4, 3, 8]), ALU.is_equal), [(s["cg"], 13)])
            PO.step("dve", at_(24), lambda e: e.tensor_reduce(
                gk[:, :, :], geq[:, :, :, :].rearrange("p t k g -> p t g k"), AX, ALU.max))
            PO.step("dve", at_(25), lambda e: e.tensor_tensor(
                Tm[:, :, :].rearrange("p t (g k) -> p (t g) k", k=8),
                Sx[:, :, :].rearrange("p t (g k) -> p (t g) k", k=8),
                gk[:, :, :].rearrange("p t g -> p (t g)").unsqueeze(2).broadcast_to([128, 32, 8]), ALU.mult))
            PO.step("dve", at_(25), four(lambda e, t: e.max(t8[:, t, :], Tm[:, t, :])))
            PO.step("dve", at_(25), four(lambda e, t: e.max_index(ti[:, t, :], t8[:, t, :], Tm[:, t, :])))
            for t in range(4):
                PO.step("dve", at_(26 + t // 2), lambda e, t=t: e.tensor_tensor(
                    teq[:, t, :, :], iota64[:, :].unsqueeze(1).broadcast_to([128, 6, E]),
                    ti[:, t, 0:6].unsqueeze(2).broadcast_to([128, 6, E]), ALU.is_equal))
            PO.step("dve", at_(27), four(lambda e, t: e.tensor_reduce(
                M[:, t, :], teq[:, t, :, :].rearrange("p k e -> p e k"), AX, ALU.max)))
            PO.step("dve", at_(28), lambda e: e.tensor_tensor(RT[:, rt, :, D:D + E], Tm[:, :, :], M[:, :, :], ALU.mult))
            PO.step("dve", at_(28), lambda e: e.tensor_copy(RT[:, rt, :, D + E], tid[:, 4 * bp:4 * bp + 4]))

            def pos(eng):
                for t in range(4):
                    o = bP1[:, t * E:(t + 1) * E]
                    eng.matmul(o, ones[:, :], MC[:, :], start=True, stop=False)
                    for q in range(t):
                        eng.matmul(o, ones[:, :], M[:, q, :], start=False, stop=False)
                    r = eng.matmul(o, tri[:, :], M[:, t, :], start=False, stop=True)
                return r

            PO.step("pe", at_(29), pos, [k_read(at_(29))])
            pp = bP1[:, 0:4 * E].rearrange("p (t e) -> p t e", t=4)
            PO.step("dve", at_(30), lambda e: e.scalar_tensor_tensor(
                out=W95[:, 4 * bp:4 * bp + 4, :], in0=pp, scalar=CAP - 1.5, in1=RT[:, rt, :, D:D + E],
                op0=ALU.is_ge, op1=ALU.mult))
            PO.step("dve", at_(30), lambda e: e.scalar_tensor_tensor(
                out=KP[:, :, :], in0=pp, scalar=CAP - 1.5, in1=M[:, :, :], op0=ALU.is_lt, op1=ALU.mult))
            n = PO.step("dve", at_(30), lambda e: e.scalar_tensor_tensor(
                out=C1[:, :, :], in0=pp, scalar=-float(E), in1=K64[:, :].unsqueeze(1).broadcast_to([128, 4, E]),
                op0=ALU.mult, op1=ALU.add))
            p1_busy[at_(29)] = (PO.sem, n)
            PO.step("dve", at_(31), lambda e: e.tensor_tensor(C1[:, :, :], C1[:, :, :], KP[:, :, :], ALU.mult))
            PO.step("dve", at_(31), four(lambda e, t: e.max(c8[:, t, :], C1[:, t, :])))
            w = [(s_sc[rt], 16 * 24 * (bp // 2))] if bp >= 2 else []
            n = PO.step("dve", at_(31), lambda e: e.tensor_scalar(
                ix[:, rt, :, :].rearrange("p t k -> p (t k)"), c8[:, :, :].rearrange("p t k -> p (t k)"),
                -1.0, 8192.0, ALU.mult, ALU.add), w)
            for t in range(4):
                for k in range(6):
                    def scatter(eng, t=t, k=k, n=n):
                        eng.wait_ge(s["po"], n)
                        eng.wait_ge(s["bi"], 16 * 4)
                        eng.indirect_dma_start(BUF, bass.IndirectOffsetOnAxis(ap=ix[:, rt, t, k:k + 1], axis=0),
                                               RT[:, rt, t, :], None, bounds_check=CAP * E - 1, oob_is_err=False
                                               ).then_inc(s_sc[rt], 16)
                    plan["pool"].setdefault(at_(32 + t * 6 + k), []).append(scatter)
            PO.step("dve", at_(31), lambda e: e.tensor_reduce(
                Ms[:, :], M[:, :, :].rearrange("p t e -> p e t"), AX, ALU.add))
            PO.step("dve", at_(31), lambda e: e.tensor_tensor(MC[:, :], MC[:, :], Ms[:, :], ALU.add))
            PO.step("dve", at_(32), lambda e: e.scalar_tensor_tensor(
                out=Lt[:, :, :], in0=tid[:, 4 * bp:4 * bp + 4].unsqueeze(2).broadcast_to([128, 4, E]), scalar=1.0,
                in1=M[:, :, :], op0=ALU.add, op1=ALU.mult))
            PO.step("dve", at_(32), lambda e: e.tensor_reduce(
                Ls[:, :], Lt[:, :, :].rearrange("p t e -> p e t"), AX, ALU.max))
            PO.step("dve", at_(32), lambda e: e.tensor_tensor(L[:, :], L[:, :], Ls[:, :], ALU.max))

        x_jobs(0)
        for n in range(32):
            w_job(n)
        LOW_READY = flag_jobs()
        for bp in range(NP):
            if bp + 1 < NP:
                x_jobs(bp + 1)
            post_jobs(bp)

        LAST = NU + 33
        PO.step("dve", LAST, lambda e: e.memset(LB[0:E, D:D + E], 1.0), [(s["wo"], NU)])
        PO.step("dve", LAST, lambda e: e.memset(LB[0:E, D + E:ROW], FAR))
        PO.step("pe", LAST, lambda e: e.transpose(bP1[0:E, 0:128], L[:, :], ident[:, :]))
        PO.step("dve", LAST, lambda e: e.tensor_reduce(lmax[:, :], bP1[0:E, 0:128], AX, ALU.max))
        PO_END = PO.step("dve", LAST, lambda e: e.tensor_scalar(lix[:, :], lmax[:, :], -1.0, 0.0, ALU.add, ALU.max))

        fin_out = {}

        def final_jobs(g):
            b, b3, slot, ch = g % 2, g % 3, 1000 + g // 2, FC[g % 2]
            banks = (bACC[0], bACC[1]) if b == 0 else (bP0, bP1)

            def mm(eng):
                for t in range(4):
                    r = eng.matmul(banks[t // 2][:, t % 2 * 256:(t % 2 + 1) * 256],
                                   W95T[:, (4 * g + t) * 128:(4 * g + t + 1) * 128], OUT95[0:E, :],
                                   start=True, stop=True)
                return r

            def add(e, k, h):
                a = ft[:, b, 2 * h:2 * h + 2, :].rearrange("p t n -> p (t n)")
                f = fin[:, b3, k, 2 * h:2 * h + 2, :].rearrange("p t n -> p (t n)")
                return e.tensor_tensor(a, banks[h][:, :] if k == 0 else a, f, ALU.add)

            v, y, a, c = (nw[:, b, k, :] for k in range(4))
            w = [(s["wtc"], NP)] + [(s_o95[k], 16 * E // 4) for k in range(4)] if g < 2 else []
            yield ch.step("pe", slot, mm, w)
            w = [(s_fl[b3], 48 * (g // 3 + 1))] + ([(s_fo[b], 16 * (g // 2))] if g >= 2 else [])
            for h in range(2):
                yield ch.step("dve", slot, lambda e, h=h: add(e, 0, h), w)
            yield ch.step("pool", slot, lambda e: add(e, 1, 0))
            yield ch.step("dve", slot, lambda e: add(e, 1, 1))

            def bn(eng):
                for t in range(4):
                    r = eng.bn_stats(st[:, b, t, :], ft[:, b, t, :])
                return r

            def ag(eng):
                for t in range(4):
                    r = eng.bn_aggr(mv[:, b, t, :], st[:, b, t, :])
                return r

            yield ch.step("dve", slot, bn)
            yield ch.step("dve", slot, ag)
            yield ch.step("dve", slot, lambda e: e.tensor_scalar(v, mv[:, b, :, 1], EPS, None, ALU.add))
            yield ch.step("dve", slot, lambda e: e.tensor_scalar(y.bitcast(I32), v.bitcast(I32), -0.5, RSQRT_MAGIC,
                                                                ALU.mult, ALU.add))
            for k in range(3):
                yield ch.step("dve", slot, lambda e: e.tensor_tensor(a, y, y, ALU.mult))
                yield ch.step("dve", slot, lambda e: e.scalar_tensor_tensor(out=c, in0=a, scalar=-0.5, in1=v,
                                                                            op0=ALU.mult, op1=ALU.mult))
                yield ch.step("dve", slot, lambda e: e.scalar_tensor_tensor(out=y, in0=c, scalar=1.5, in1=y,
                                                                            op0=ALU.add, op1=ALU.mult))
            normal(ch, b, slot, lambda t: ft[:, b, t, :], lambda t: ft[:, b, t, :])
            yield
            yield ch.step("pool", slot, lambda e: add(e, 2, 0))
            fin_out[g] = ch.step("dve", slot, lambda e: add(e, 2, 1))
            yield

        last_slot = max(max(v) for v in plan.values())
        for g in range(0, NP, 2):
            for _ in zip(final_jobs(g), final_jobs(g + 1)):
                pass

        def run_plan(who, eng, slot):
            for f in plan[who].get(slot, []):
                f(eng)

        SLOTS = range(0, END)
        TAIL = range(END, last_slot + 1)
        UP = {NU + 6: 0, NU + 12: 1, NU + 20: 2, NU + 26: 3, NU + 34: 4, NU + 35: 5, NU + 36: 6, NU + 37: 7}
        DN = {NU + 19: 0, NU + 24: 1, NU + 30: 2, NU + 34: 3, NU + 35: 4, NU + 36: 5, NU + 37: 6, NU + 38: 7}
        GB = ((bS[0], bS[1]), (bPT, bO))
        MT = (128, 128, 96)

        block = ctx.enter_context(nc.Block())

        @block.sync
        def _(eng):
            eng.dma_start(bqk[:, :, :], bqkv).then_inc(s["cd"], 16)
            for k in range(2):
                eng.dma_start(bo2[:, 256 * k:256 * k + 256],
                              bo.rearrange("(a n) -> a n", a=1).broadcast_to([128, 256])).then_inc(s["cd"], 16)
            eng.dma_start(gTf[:, :, :], gateT.rearrange("(c p) e -> p c e", p=128)).then_inc(s["gt"], 16)
            run_plan("sp", eng, PRO)
            for slot in SLOTS:
                run_plan("sp", eng, slot)
                if 24 <= slot < 32 and slot % 2 == 0:
                    n = (slot - 24) // 2
                    eng.wait_ge(s["S"], slot)
                    eng.wait_ge(s["cg"], 11)
                    eng.dma_start(BUF[n * 1536:(n + 1) * 1536, :].rearrange("(k p) c -> p k c", p=128),
                                  zrow[:, :].unsqueeze(1).broadcast_to([128, 12, ROW])).then_inc(s["bi"], 16)
                if 32 <= slot < 48 and slot % 2 == 0:
                    n = (slot - 32) // 2
                    eng.wait_ge(s["S"], slot)
                    eng.dma_start(Y[1][n * 512:(n + 1) * 512, :].rearrange("(k p) c -> p k c", p=128),
                                  zrow[:, 0:D].unsqueeze(1).broadcast_to([128, 4, D])).then_inc(s["yi"], 16)
            eng.wait_ge(s["wo"], NU)
            for m in range(2):
                eng.dma_start(sgf[:, m, :, :], sguT[m].rearrange("(c p) n -> p c n", p=128)).then_inc(s["sw"], 16)
            eng.dma_start(sdf[:, 0:2, :], sdT[0:256, :].rearrange("(j p) n -> p j n", p=128)).then_inc(s["sw"], 16)
            eng.dma_start(sdf[0:96, 2, :], sdT[256:352, :]).then_inc(s["sw"], 16)

            def expert_weights(e):
                b = e % NRING
                if e >= NRING:
                    eng.wait_ge(s["eo"], e - NRING + 1)
                eng.dma_start(EG[:, b, :], ewT[e]).then_inc(s_ew[b], 16)
                eng.dma_start(ED[0:88, b, :], ewd[e]).then_inc(s_ew[b], 16)

            def expert_rows(e):
                b = e % NB
                if e >= NB:
                    eng.wait_ge(s["eow"], e - NB + 1)
                    eng.wait_ge(s["wix"], e - NB + 1)
                eng.dma_start(BE[0:CAP, b, :], BUF.rearrange("(s e) c -> e s c", e=E)[e]).then_inc(s_be[b], 16)

            for e in range(NRING):
                expert_weights(e)
            g = 0
            for slot in TAIL:
                run_plan("sp", eng, slot)
                if slot - 1 in DN:
                    eng.wait_ge(s["sy"], 2 * (g + 1))
                    eng.dma_start(Y[0][g * 512:(g + 1) * 512, :].rearrange("(t p) d -> p t d", p=128),
                                  yst[:, g % 2, :, :]).then_inc(s_ys[g % 2], 16)
                    g += 1
            assert g == NP
            eng.wait_ge(s["lb"], 16)
            eng.wait_ge(s["po"], PO_END)
            for k in range(2):
                eng.wait_ge(s_sc[k], 16 * 24 * 4)
            eng.dma_start(BUF[(CAP - 1) * E:CAP * E, :], LB[0:E, :]).then_inc(s["dd"], 16)
            eng.wait_ge(s["dd"], 16)
            for e in range(NB):
                expert_rows(e)
            for e in range(E):
                if e + NRING < E:
                    expert_weights(e + NRING)
                if e + NB < E:
                    expert_rows(e + NB)
                eng.wait_ge(s["eow"], e + 1)
                eng.dma_start(OUT95[e:e + 1, :], OW[CAP - 1:CAP, e % 4, :]).then_inc(s_o95[e % 4], 16)

            def put(g):
                eng.wait_ge(s["fd" if g % 2 else "fc"], fin_out[g])
                eng.dma_start(out[g * 512:(g + 1) * 512, :].rearrange("(t p) d -> p t d", p=128), ft[:, g % 2, :, :]
                              ).then_inc(s_fo[g % 2], 16)

            def get(g):
                for k, src in enumerate((Y[0], Y[1], Xd)):
                    eng.dma_start(fin[:, g % 3, k, :, :],
                                  src[g * 512:(g + 1) * 512, :].rearrange("(t p) d -> p t d", p=128)
                                  ).then_inc(s_fl[g % 3], 16)

            for k in range(2):
                eng.wait_ge(s_ya[k], 16 * 32)
                eng.wait_ge(s_x1[k], 16 * 4)
            eng.wait_ge(s["sdn"], 4 * NP)
            for g in range(3):
                get(g)
            for g in range(NP):
                put(g)
                if g + 3 < NP:
                    get(g + 3)
            for k in range(2):
                eng.wait_ge(s_fo[k], 16 * 4)

        @block.gpsimd
        def _(eng):
            cg = [0]

            def c(ins, wait=False):
                ins.then_inc(s["cg"], 1)
                cg[0] += 1
                if wait:
                    eng.wait_ge(s["cg"], cg[0])

            c(eng.memset(ident[:, :], 0.0), True)
            c(eng.affine_select(out=ident[:, :], in_=ident[:, :], compare_op=ALU.not_equal, fill=1.0, base=0,
                                pattern=[[-1, 128]], channel_multiplier=1))
            run_plan("pool", eng, PRO)
            c(eng.memset(tri[:, :], 1.0), True)
            c(eng.affine_select(out=tri[:, :], in_=tri[:, :], compare_op=ALU.is_gt, fill=0.0, base=0,
                                pattern=[[1, 128]], channel_multiplier=-1))
            c(eng.memset(ones[:, :], 1.0))
            for t_, pat, base, cm in ((iota8, [[1, 8]], 0, 0), (iota64, [[1, E]], 0, 0), (K64, [[-1, E]], 8192, 0),
                                      (tid, [[128, 32]], 0, 1)):
                c(eng.iota(t_[:, :], pattern=pat, base=base, channel_multiplier=cm,
                           allow_small_or_imprecise_dtypes=True))
            c(eng.memset(zrow[:, :], 0.0), True)
            c(eng.memset(zrow[:, ROW - 1:ROW], FAR))
            c(eng.memset(MC[:, :], 0.0))
            c(eng.memset(L[:, :], 0.0))
            for u in SLOTS:
                w = u - 1
                if 0 <= w < NU:
                    eng.wait_ge(s["r"], w + 1)
                    p = P[:, w % 2, :].rearrange("p (t k) -> p t k", t=2)
                    eng.tensor_tensor(p, p, rr[:, w % 4, :].unsqueeze(2).broadcast_to([128, 2, 256]), ALU.mult
                                      ).then_inc(s["pn"], 1)
                run_plan("pool", eng, u)
            for slot in TAIL:
                run_plan("pool", eng, slot)
            eng.wait_ge(s["po"], PO_END)
            eng.wait_ge(s["hd"], 16 * NP)
            eng.indirect_dma_start(LB[0:E, 0:D], None, Hd, bass.IndirectOffsetOnAxis(ap=lix[:, 0:1], axis=0),
                                   bounds_check=4095, oob_is_err=False).then_inc(s["lb"], 16)
            for k in range(2):
                eng.wait_ge(s_ys[k], 16 * 4)
            eng.wait_ge(s["yi"], 16 * 8)
            for e in range(E):
                eng.wait_ge(s["eow"], e + 1)
                eng.wait_ge(s["wix"], e + 1)
                if e >= 2:
                    eng.wait_ge(s_ya[e % 2], 16 * (e // 2))
                eng.indirect_dma_start(Y[e % 2], bass.IndirectOffsetOnAxis(ap=wix[:, e % NB, :], axis=0),
                                       OW[0:CAP, e % 4, :], None, bounds_check=4095, oob_is_err=False,
                                       compute_op=ALU.add).then_inc(s_ya[e % 2], 16)
            for g in range(NP // 2):
                run_plan("pool", eng, 1000 + g)

        @block.tensor
        def _(eng):
            PASS = ((0, 0), (0, 1), (1, 0))

            def passes(w, low):
                return [p for p in PASS if low or p[w] == 0]

            def proj_qk(i, m, low):
                bp, h = i // NH, i % NH
                bk_ = bP0 if m == 0 else bP1
                eng.wait_ge(s["xc"], xt_ready[bp])
                if bp == 0:
                    eng.wait_ge(s["wl"], w_ready[(m, h // 4, 1)])
                if m == 0:
                    if i:
                        eng.wait_ge(s["vl"], min(NI, i + 2))
                else:
                    eng.wait_ge(s["kl"], i)
                    if 2 * (i - 1) - 1 in p1_busy and i:
                        eng.wait_ge(*p1_busy[2 * (i - 1) - 1])
                k, n = 0, 2 * len(passes(0, low))
                for c in range(2):
                    for a, b in passes(0, low):
                        r = eng.matmul(bk_[:, :], W[:, m, a, c * 2048 + h * 128:c * 2048 + (h + 1) * 128],
                                       XT[:, bp % 2, b, c, :], start=(k == 0), stop=(k == n - 1))
                        k += 1
                r.then_inc(s["q" if m == 0 else "k"], 1)

            def proj_v(j, low):
                g, t = j // 4, j % 4
                bp, hg = g // 4, g % 4
                eng.wait_ge(s["xc"], xt_ready[bp])
                if bp == 0:
                    eng.wait_ge(s["wl"], w_ready[(2, hg, 1)])
                eng.wait_ge(s["ql"], 1 if j < 3 else min(NI, j - 1))
                if j < 3:
                    eng.wait_ge(s["vl"], j)
                k, n = 0, 2 * len(passes(1, low))
                for c in range(2):
                    for a, b in passes(1, low):
                        r = eng.matmul(bP0[:, :], XT[:, bp % 2, a, c, t * 128:(t + 1) * 128],
                                       W[:, 2, b, c * 2048 + hg * 512:c * 2048 + (hg + 1) * 512],
                                       start=(k == 0), stop=(k == n - 1))
                        k += 1
                r.then_inc(s["v"], 1)

            def scores(u):
                i, q = u // 2, u % 2
                if q == 0:
                    eng.wait_ge(s["ql"], i + 1)
                    eng.wait_ge(s["kl"], i + 1)
                if u >= 2:
                    eng.wait_ge(s["e"], u - 1)
                for t in range(2):
                    for k, (a, b) in enumerate(PASS):
                        r = eng.matmul(bS[u % 2][:, t * 256:(t + 1) * 256],
                                       QK[:, i % 2, 0, a, q * 256 + t * 128:q * 256 + (t + 1) * 128],
                                       QK[:, i % 2, 1, b, q * 256:(q + 1) * 256], start=(k == 0), stop=(k == 2))
                r.then_inc(s["S"], 1)

            def turn_p(u):
                eng.wait_ge(s["pn"], u + 1)
                eng.wait_ge(s["pl"], u)
                for kc in range(2):
                    for t in range(2):
                        r = eng.transpose(bPT[:, kc * 256 + t * 128:kc * 256 + (t + 1) * 128],
                                          P[:, u % 2, t * 256 + kc * 128:t * 256 + (kc + 1) * 128], ident[:, :])
                r.then_inc(s["pt"], 1)

            def pv(u):
                i, q = u // 2, u % 2
                h = i % NH
                if u % 8 == 0:
                    eng.wait_ge(s["vl"], 4 * (i // 4 + 1))
                eng.wait_ge(s["pl"], u + 1)
                eng.wait_ge(s["ol"], u)
                k = 0
                for kc in range(2):
                    for a, b in PASS:
                        r = eng.matmul(bO[:, 0:256],
                                       V[:, i // 4 % 2, a, 2 * q + kc, h % 4 * 128:(h % 4 + 1) * 128],
                                       PT[:, u % 2, b, kc * 256:(kc + 1) * 256], start=(k == 0), stop=(k == 5))
                        k += 1
                r.then_inc(s["pv"], 1)

            def proj_o(u, low):
                i, q = u // 2, u % 2
                bp, h = i // NH, i % NH
                if bp == 0:
                    eng.wait_ge(s["wl"], w_ready[(3, h // 4, 1)])
                if h == 0 and bp:
                    eng.wait_ge(s["po"], acc_free[(bp - 1, q)])
                eng.wait_ge(s["ol"], u + 1)
                n = len(passes(1, low))
                for t in range(2):
                    for k, (a, b) in enumerate(passes(1, low)):
                        r = eng.matmul(bACC[q][:, t * 256:(t + 1) * 256], O[:, u % 2, a, t * 128:(t + 1) * 128],
                                       W[:, 3, b, h * 256:(h + 1) * 256], start=(h == 0 and t == 0 and k == 0),
                                       stop=(h == NH - 1 and k == n - 1), skip_group_check=True)
                r.then_inc(s["wo"], 1)

            run_plan("pe", eng, PRO)
            proj_qk(0, 0, True)
            proj_qk(0, 1, True)
            for j in range(3):
                proj_v(j, True)

            def attention(slots, low):
                for u in slots:
                    i = u // 2
                    if u < NU:
                        scores(u)
                        if u % 2 == 0 and i + 1 < NI:
                            proj_qk(i + 1, 0, low)
                        if u % 2 == 1 and i + 3 < NI:
                            proj_v(i + 3, low)
                    if 0 <= u - 3 < NU:
                        proj_o(u - 3, low)
                    if 0 <= u - 1 < NU:
                        turn_p(u - 1)
                    if 0 <= u - 2 < NU:
                        pv(u - 2)
                    if u % 2 == 0 and i + 1 < NI:
                        proj_qk(i + 1, 1, low)
                    run_plan("pe", eng, u)

            attention(range(0, 32), True)
            eng.wait_ge(s["lc"], LOW_READY)
            low = eng.value_load(low3[0:1, 0:1], min_val=0, max_val=1)
            with eng.If(low == 0):
                attention(range(32, END), False)
            with eng.Else():
                attention(range(32, END), True)

            def shared_up(g):
                for j in range(3):
                    k = 3 * g + j
                    M_ = MT[j]
                    if k == 0:
                        eng.wait_ge(s["swl"], 3)
                        eng.wait_ge(s["e"], NU)
                    if k == 1:
                        eng.wait_ge(s["pl"], NU)
                        eng.wait_ge(s["ol"], NU)
                    if k >= 2:
                        eng.wait_ge(s["saf"], k - 1)
                    if j == 0:
                        eng.wait_ge(s["po"], ht_ready[g])
                    for m in range(2):
                        q = 0
                        for c in range(2):
                            for a, b in PASS:
                                r = eng.matmul(GB[k % 2][m][0:M_, :], sgh[:, a, m, c, j * 128:j * 128 + M_],
                                               HT[:, b, c, g * 512:(g + 1) * 512], start=(q == 0), stop=(q == 5))
                                q += 1
                    r.then_inc(s["sg"], 1)

            def shared_down(g):
                eng.wait_ge(s["sal"], 3 * (g + 1))
                for t in range(4):
                    if t % 2 == 0:
                        if g == 0:
                            eng.wait_ge(s["po"], acc_free[(NP - 1, t // 2)])
                        else:
                            eng.wait_ge(s["sy"], 2 * (g - 1) + t // 2 + 1)
                    q = 0
                    for j in range(3):
                        for a, b in PASS:
                            r = eng.matmul(bACC[t // 2][:, t % 2 * 256:(t % 2 + 1) * 256],
                                           ah[0:MT[j], g % 2, a, j, t * 128:(t + 1) * 128],
                                           sdh[0:MT[j], b, j, :], start=(q == 0), stop=(q == 8))
                            q += 1
                    r.then_inc(s["sdn"], 1)

            for slot in TAIL:
                run_plan("pe", eng, slot)
                if slot in UP:
                    shared_up(UP[slot])
                if slot in DN:
                    shared_down(DN[slot])

            for g in range(NP):
                if g == 0:
                    eng.wait_ge(s["sy"], 2 * NP)
                    eng.wait_ge(s["po"], PO_END)
                if g >= 2:
                    eng.wait_ge(s["wtc"], g - 1)
                for t in range(4):
                    r = eng.transpose(bACC[g % 2][0:E, t * 128:(t + 1) * 128], W95[:, 4 * g + t, :], ident[:, :])
                r.then_inc(s["wt"], 1)

            def e_turn(e):
                b = e % NB
                eng.wait_ge(s_be[b], 16 * (e // NB + 1))
                if e >= 2:
                    eng.wait_ge(s["ebt"], e - 1)
                for c in range(2):
                    r = eng.transpose((bP0, bP1)[e % 2][:, c * CAP:(c + 1) * CAP],
                                      BE[0:CAP, b, c * 128:(c + 1) * 128], ident[0:CAP, 0:CAP])
                r.then_inc(s["et"], 1)

            def e_up(e):
                b = e % NRING
                eng.wait_ge(s_ew[b], 32 * (e // NRING + 1))
                eng.wait_ge(s["ebt"], e + 1)
                if e >= 2:
                    eng.wait_ge(s["eac"], e - 1)
                else:
                    eng.wait_ge(s["saf"], 3 * NP)
                for m in range(2):
                    for j in range(2):
                        for c in range(2):
                            o = (m * 2 + c) * 176 + j * 88
                            r = eng.matmul(bS[e % 2][0:88, (m * 2 + j) * CAP:(m * 2 + j + 1) * CAP],
                                           EG[:, b, o:o + 88], BT[:, e % 2, c * CAP:(c + 1) * CAP],
                                           start=(c == 0), stop=(c == 1))
                r.then_inc(s["eg"], 1)

            def e_down(e):
                b = e % NRING
                eng.wait_ge(s["eac"], e + 1)
                if e >= 2:
                    eng.wait_ge(s["eow"], e - 1)
                for j in range(2):
                    r = eng.matmul((bPT, bO)[e % 2][0:CAP, 0:256], ac2[0:88, e % 2, j, :],
                                   ED[0:88, b, j * 256:(j + 1) * 256], start=(j == 0), stop=(j == 1))
                r.then_inc(s["eo"], 1)

            for e in range(E + 2):
                if e < E:
                    e_turn(e)
                if 0 <= e - 1 < E:
                    e_up(e - 1)
                if 0 <= e - 2 < E:
                    e_down(e - 2)
            for g in range(NP // 2):
                run_plan("pe", eng, 1000 + g)

        @block.scalar
        def _(eng):
            def q_high(i, m):
                h = i % NH
                eng.wait_ge(s["q" if m == 0 else "k"], i + 1)
                if i >= 2:
                    eng.wait_ge(s["S"], 2 * i - 2)
                if i == 0:
                    eng.wait_ge(s["c0"], 2)
                eng.activation(QK[:, i % 2, m, 0, :], (bP0 if m == 0 else bP1)[:, :], ACT.Identity,
                               bias=bqk[:, m, h:h + 1]).then_inc(s["qh" if m == 0 else "kh"], 1)

            def v_high(j):
                eng.wait_ge(s["v"], j + 1)
                if j >= 8:
                    eng.wait_ge(s["pv"], 8 * (j // 4 - 1))
                eng.activation(V[:, j // 4 % 2, 0, j % 4, :], bP0[:, :], ACT.Copy, scale=SV / (SX * SW)
                               ).then_inc(s["vh"], 1)

            run_plan("act", eng, PRO)
            q_high(0, 0)
            q_high(0, 1)
            for j in range(3):
                v_high(j)
            for u in SLOTS:
                i = u // 2
                if u % 2 == 1 and i + 1 < NI:
                    q_high(i + 1, 1)
                if 0 <= u - 3 < NU:
                    w = u - 3
                    h = w // 2 % NH
                    eng.wait_ge(s["pv"], w + 1)
                    if w >= 2:
                        eng.wait_ge(s["wo"], w - 1)
                    eng.activation(O[:, w % 2, 0, :], bO[:, 0:256], ACT.Identity, bias=bqk[:, 2, h:h + 1]
                                   ).then_inc(s["oh"], 1)
                run_plan("act", eng, u)
                if u < NU:
                    if u % 2 == 0 and i + 1 < NI:
                        q_high(i + 1, 0)
                    if u % 2 == 1 and i + 3 < NI:
                        v_high(i + 3)
                    eng.wait_ge(s["nm"], u + 1)
                    if u >= 2:
                        eng.wait_ge(s["pt"], u - 1)
                    for t in range(2):
                        r = eng.activation(P[:, u % 2, t * 256:(t + 1) * 256], bS[u % 2][:, t * 256:(t + 1) * 256],
                                           ACT.Exp, bias=nm[:, u % 4, t:t + 1], scale=SCALE / (SQ * SQ),
                                           accum_out=rs[:, u % 4, t:t + 1])
                    r.then_inc(s["e"], 1)
                if 0 <= u - 1 < NU:
                    w = u - 1
                    eng.wait_ge(s["pt"], w + 1)
                    if w >= 2:
                        eng.wait_ge(s["pv"], w - 1)
                    eng.activation(PT[:, w % 2, 0, :], bPT[:, :], ACT.Copy, scale=SP_).then_inc(s["ph"], 1)
                run_plan("act_late", eng, u)
            eng.wait_ge(s["sw"], 16 * 4)
            eng.activation(sgh[:, 0, :, :, :], sgf, ACT.Copy, scale=SG).then_inc(s["swh"], 1)
            eng.activation(sdh[:, 0, 0:2, :], sdf[:, 0:2, :], ACT.Copy, scale=SG).then_inc(s["swh"], 1)
            eng.activation(sdh[0:96, 0, 2, :], sdf[0:96, 2, :], ACT.Copy, scale=SG).then_inc(s["swh"], 1)

            def act_up(g):
                for j in range(3):
                    k = 3 * g + j
                    eng.wait_ge(s["sg"], k + 1)
                    if k >= 2:
                        eng.wait_ge(s["saf"], k - 1)
                    eng.activation(sl[0:MT[j], k % 2, :], GB[k % 2][0][0:MT[j], :], ACT.Silu, scale=1.0 / (SX * SG)
                                   ).then_inc(s["ssl"], 1)
                    eng.wait_ge(s["saf"], k + 1)
                    if g >= 2:
                        eng.wait_ge(s["sdn"], 4 * (g - 1))
                    eng.activation(ah[0:MT[j], g % 2, 0, j, :], af[0:MT[j], k % 2, :], ACT.Copy
                                   ).then_inc(s["sah"], 1)

            def act_down(g):
                for h in range(2):
                    eng.wait_ge(s["sdn"], 4 * g + 2 * h + 2)
                    if g >= 2:
                        eng.wait_ge(s_ys[g % 2], 16 * (g // 2))
                    eng.activation(yst[:, g % 2, 2 * h:2 * h + 2, :].rearrange("p t n -> p (t n)"), bACC[h][:, :],
                                   ACT.Copy, scale=1.0 / (SA * SG)).then_inc(s["sy"], 1)

            for slot in TAIL:
                run_plan("act", eng, slot)
                if slot in UP:
                    act_up(UP[slot])
                if slot in DN:
                    act_down(DN[slot])
            for g in range(NP):
                eng.wait_ge(s["wt"], g + 1)
                if g == 0:
                    eng.wait_ge(s["sg"], 3 * NP)
                eng.activation(W95T[:, g * 512:(g + 1) * 512], bACC[g % 2][0:E, :], ACT.Copy).then_inc(s["wtc"], 1)

            def e_silu(e):
                eng.wait_ge(s["eg"], e + 1)
                if e >= 2:
                    eng.wait_ge(s["eac"], e - 1)
                eng.activation(sl2[0:88, e % 2, :], bS[e % 2][0:88, 0:192], ACT.Silu).then_inc(s["esl"], 1)

            def e_out(e):
                eng.wait_ge(s["eo"], e + 1)
                if e >= 4:
                    eng.wait_ge(s_ya[e % 2], 16 * (e // 2 - 1))
                    eng.wait_ge(s_o95[e % 4], 16 * (e // 4))
                eng.activation(OW[0:CAP, e % 4, :], (bPT, bO)[e % 2][0:CAP, 0:256], ACT.Copy,
                               scale=BE[0:CAP, e % NB, D + e:D + e + 1]).then_inc(s["eow"], 1)

            for e in range(E + 2):
                if 0 <= e - 1 < E:
                    e_silu(e - 1)
                if 0 <= e - 2 < E:
                    e_out(e - 2)
            for g in range(NP // 2):
                run_plan("act", eng, 1000 + g)

        @block.vector
        def _(eng):
            eng.wait_ge(s["cd"], 16 * 3)
            eng.tensor_scalar(bqk[:, 0:2, :], bqk[:, 0:2, :], SQ, None, ALU.mult).then_inc(s["c0"], 1)
            eng.tensor_scalar(bqk[:, 2, :], bqk[:, 2, :], SO, None, ALU.mult).then_inc(s["c0"], 1)
            run_plan("dve", eng, PRO)

            def q_low(i, m):
                h = i % NH
                eng.wait_ge(s["qh" if m == 0 else "kh"], i + 1)
                eng.scalar_tensor_tensor(out=QK[:, i % 2, m, 1, :], in0=(bP0 if m == 0 else bP1)[:, :],
                                         scalar=bqk[:, m, h:h + 1], in1=QK[:, i % 2, m, 0, :],
                                         op0=ALU.add, op1=ALU.subtract).then_inc(s["ql" if m == 0 else "kl"], 1)

            def v_low(j):
                eng.wait_ge(s["vh"], j + 1)
                eng.scalar_tensor_tensor(out=V[:, j // 4 % 2, 1, j % 4, :], in0=bP0[:, :], scalar=SV / (SX * SW),
                                         in1=V[:, j // 4 % 2, 0, j % 4, :], op0=ALU.mult, op1=ALU.subtract
                                         ).then_inc(s["vl"], 1)

            q_low(0, 0)
            q_low(0, 1)
            for j in range(3):
                v_low(j)
            eng.wait_ge(s["gt"], 16)
            eng.tensor_scalar(gT[:, 0, :, :], gTf[:, :, :], SG, None, ALU.mult).then_inc(s["c0"], 1)
            eng.wait_ge(s["c0"], 3)
            eng.scalar_tensor_tensor(out=gT[:, 1, :, :], in0=gTf[:, :, :], scalar=SG, in1=gT[:, 0, :, :],
                                     op0=ALU.mult, op1=ALU.subtract).then_inc(s["c0"], 1)
            for u in SLOTS:
                i = u // 2
                if 0 <= u - 1 < NU:
                    w = u - 1
                    eng.wait_ge(s["e"], w + 1)
                    eng.reciprocal(rr[:, w % 4, :], rs[:, w % 4, :]).then_inc(s["r"], 1)
                if 0 <= u - 2 < NU:
                    w = u - 2
                    eng.wait_ge(s["ph"], w + 1)
                    eng.scalar_tensor_tensor(out=PT[:, w % 2, 1, :], in0=bPT[:, :], scalar=SP_,
                                             in1=PT[:, w % 2, 0, :], op0=ALU.mult, op1=ALU.subtract
                                             ).then_inc(s["pl"], 1)
                if u < NU:
                    eng.wait_ge(s["S"], u + 1)
                    eng.tensor_reduce(nm0[:, u % 4, :], bS[u % 2][:, :].rearrange("p (t k) -> p t k", t=2), AX,
                                      ALU.max, negate=True).then_inc(s["mx"], 1)
                if 0 <= u - 3 < NU:
                    w = u - 3
                    h = w // 2 % NH
                    eng.wait_ge(s["oh"], w + 1)
                    eng.scalar_tensor_tensor(out=O[:, w % 2, 1, :], in0=bO[:, 0:256], scalar=bqk[:, 2, h:h + 1],
                                             in1=O[:, w % 2, 0, :], op0=ALU.add, op1=ALU.subtract
                                             ).then_inc(s["ol"], 1)
                if u < NU:
                    eng.wait_ge(s["mx"], u + 1)
                    eng.tensor_scalar(nm[:, u % 4, :], nm0[:, u % 4, :], SCALE / (SQ * SQ), None, ALU.mult
                                      ).then_inc(s["nm"], 1)
                if u % 2 == 1 and i + 1 < NI:
                    q_low(i + 1, 1)
                run_plan("dve", eng, u)
                if u < NU:
                    if u % 2 == 0 and i + 1 < NI:
                        q_low(i + 1, 0)
                    if u % 2 == 1 and i + 3 < NI:
                        v_low(i + 3)
            for n, (lo, f, hi) in enumerate(((sgh[:, 1, :, :, :], sgf, sgh[:, 0, :, :, :]),
                                             (sdh[:, 1, 0:2, :], sdf[:, 0:2, :], sdh[:, 0, 0:2, :]),
                                             (sdh[0:96, 1, 2, :], sdf[0:96, 2, :], sdh[0:96, 0, 2, :]))):
                eng.wait_ge(s["swh"], n + 1)
                for m in range(2 if n == 0 else 1):
                    pick = (lambda a: a[:, m, :, :]) if n == 0 else (lambda a: a)
                    r = eng.scalar_tensor_tensor(out=pick(lo), in0=pick(f), scalar=SG, in1=pick(hi),
                                                 op0=ALU.mult, op1=ALU.subtract)
                r.then_inc(s["swl"], 1)

            def dve_up(g):
                for j in range(3):
                    k = 3 * g + j
                    eng.wait_ge(s["ssl"], k + 1)
                    eng.scalar_tensor_tensor(out=af[0:MT[j], k % 2, :], in0=GB[k % 2][1][0:MT[j], :],
                                             scalar=SA / (SX * SG), in1=sl[0:MT[j], k % 2, :],
                                             op0=ALU.mult, op1=ALU.mult).then_inc(s["saf"], 1)
                    eng.wait_ge(s["sah"], k + 1)
                    eng.tensor_tensor(ah[0:MT[j], g % 2, 1, j, :], af[0:MT[j], k % 2, :],
                                      ah[0:MT[j], g % 2, 0, j, :], ALU.subtract).then_inc(s["sal"], 1)

            for slot in TAIL:
                run_plan("dve", eng, slot)
                if slot in UP:
                    dve_up(UP[slot])

            def e_rows(e):
                eng.wait_ge(s["et"], e + 1)
                if e >= 2:
                    eng.wait_ge(s["eg"], e - 1)
                eng.tensor_copy(BT[:, e % 2, :], (bP0, bP1)[e % 2][:, 0:192]).then_inc(s["ebt"], 1)
                if e >= NB:
                    eng.wait_ge(s_ya[e % 2], 16 * ((e - NB) // 2 + 1))
                eng.tensor_copy(wix[:, e % NB, :], BE[0:CAP, e % NB, ROW - 1:ROW]).then_inc(s["wix"], 1)

            def e_act(e):
                eng.wait_ge(s["esl"], e + 1)
                if e >= 2:
                    eng.wait_ge(s["eo"], e - 1)
                eng.tensor_tensor(ac2[0:88, e % 2, :, :].rearrange("p j n -> p (j n)"), bS[e % 2][0:88, 192:384],
                                  sl2[0:88, e % 2, :], ALU.mult).then_inc(s["eac"], 1)

            for e in range(E + 1):
                if e < E:
                    e_rows(e)
                if e >= 1:
                    e_act(e - 1)
            for g in range(NP // 2):
                run_plan("dve", eng, 1000 + g)


def kernel(**inputs):
    import numpy as _np
    import concourse.bacc as _bacc
    from concourse import mybir as _mybir
    from concourse.bass_utils import run_bass_kernel_spmd as _run

    g = {k: _np.asarray(v) for k, v in inputs.items()}
    at = lambda n: g["L0_attn_" + n]
    ff = lambda n: g["L0_ffn_" + n]
    gu = _np.stack([ff("Wg"), ff("Wu")], 1)
    arrays = {
        "in_x": at("x").reshape(4096, 256),
        "in_wc": _np.stack([at("wq_codes"), at("wk_codes"), at("wv_codes")]),
        "in_ws": _np.repeat(_np.stack([at("wq_scales"), at("wk_scales"), at("wv_scales")]), 32, axis=1),
        "in_oc": at("wo_codes"),
        "in_os": _np.repeat(at("wo_scales"), 32, axis=0),
        "in_b": _np.stack([at("bq"), at("bk"), at("bv")]).reshape(3, 16, 128).transpose(2, 0, 1),
        "in_bo": at("bo"),
        "in_gate": ff("gate_weight").T,
        "in_sgu": _np.stack([ff("Sg").T, ff("Su").T]),
        "in_sd": ff("Sd").T,
        "in_ewT": gu.reshape(64, 2, 176, 2, 128).transpose(0, 4, 1, 3, 2).reshape(64, 128, 704),
        "in_ewd": ff("Wd").reshape(64, 256, 2, 88).transpose(0, 3, 2, 1).reshape(64, 88, 512),
    }
    arrays = {k: _np.ascontiguousarray(v) for k, v in arrays.items()}
    nc = _bacc.Bacc("TRN2", target_bir_lowering=False, num_devices=1)
    args = [nc.dram_tensor(k, a.shape, _mybir.dt.from_np(a.dtype), kind="ExternalInput").ap()
            for k, a in arrays.items()]
    out = nc.dram_tensor("out_0", (4096, 256), _mybir.dt.float32, kind="ExternalOutput").ap()
    build(nc, *args, out)
    r = _run(nc, [arrays], core_ids=[0])
    return r.results[0]["out_0"].reshape(16, 256, 256)
```

```python
from contextlib import ExitStack

import concourse.bass as bass
from concourse import mybir

F32 = mybir.dt.float32
F16 = mybir.dt.float16
U32 = mybir.dt.uint32
I32 = mybir.dt.int32
ALU = mybir.AluOpType
ACT = mybir.ActivationFunctionType
AX = mybir.AxisListType.X

NP = 8
NH = 16
NI = NP * NH
NU = 2 * NI
D = 256
E = 64
CAP = 96
NST = 8
SCALE = 128.0 ** -0.5
SX, SW, SQ, SV, SP_, SO = 4.0, 4.0, 16.0, 2.0, 64.0, 128.0
SG, SA = 64.0, 64.0
LEAD = (2, 0, 8, 10)
EPS = 1e-5
RSQRT_MAGIC = float(0x5F3759DF)
NOSIGN = 0x7FFF7FFF
FAR = 1.0e6
ROW = D + E + 1
NRING = 6
NB = 6


ORDER = {
    "pe": ([("S", 0), ("Q", -2), ("PV", 2), ("WO", 3), ("PT", 1), ("bg", 0), ("K", -2)],
           [("S", 0), ("V", -5), ("PT", 1), ("WO", 3), ("PV", 2), ("bg", 0)]),
    "act": ([("bg", 0), ("Q", -2), ("late", 0), ("exp", 0), ("PT", 1)],
            [("K", -1), ("O", 3), ("bg", 0), ("V", -5), ("PT", 1), ("exp", 0), ("late", 0), ("O", 2)]),
    "dve": ([("recip", 1), ("O", 3), ("max", 0), ("bg", 0), ("nm", 0), ("bg", 0), ("bg", 0), ("bg", 0), ("bg", 0),
             ("Q", -2), ("recip", 0)],
            [("PT", 2), ("max", 0), ("O", 3), ("nm", 0), ("bg", 0), ("K", -1), ("bg", 0), ("V", -5), ("PT", 1)]),
    "pool": ([("norm", 1), ("bg", 0)],
             [("norm", 1), ("bg", 0)]),
}
FIRST = {"Q": 1, "K": 1, "V": 3}


def slot_work(who, u, work):
    order, part = ORDER[who][u % 2], 0
    for name, lag in order:
        w = u - lag
        if name in FIRST:
            assert w % 2 == 0
            if FIRST[name] <= w // 2 < NI:
                work[name](w // 2)
        elif name == "late":
            work[name](u)
        elif name == "bg":
            work[name](u, part, sum(n == "bg" for n, _ in order))
            part += 1
        elif 0 <= w < NU:
            work[name](w)


class Chain:

    def __init__(self, sem, plan):
        self.sem, self.plan, self.n = sem, plan, 0

    def step(self, engine, slot, fn, waits=()):
        before = self.n
        self.n += 1

        def run(eng):
            eng.wait_ge(self.sem, before)
            for s, v in waits:
                eng.wait_ge(s, v)
            fn(eng).then_inc(self.sem, 1)

        self.plan[engine].setdefault(slot, []).append(run)
        return self.n


def build(nc, x, wc, wsc, wo_c, wo_s, bqkv, bo, gateT, sguT, sdT, ewT, ewd, out):
    ctx = ExitStack()
    with ctx:
        def sb(name, shape, dt=F32):
            return ctx.enter_context(nc.sbuf_tensor(name, shape, dt))

        def sem(name):
            return ctx.enter_context(nc.semaphore(name))

        bank = [ctx.enter_context(nc.psum_tensor(f"bank{i}", [128, 512], F32)) for i in range(8)]
        bS, bPT, bO, bACC, bP0, bP1 = bank[0:2], bank[2], bank[3], bank[4:6], bank[6], bank[7]

        Hd = nc.dram_tensor("Hd", [4096, D], F32, kind="Internal").ap()
        Xd = nc.dram_tensor("Xd", [2048, D], F32, kind="Internal").ap()
        BUF = nc.dram_tensor("BUF", [CAP * E, ROW], F32, kind="Internal").ap()
        Y = [nc.dram_tensor(f"Y{i}", [4096, D], F32, kind="Internal").ap() for i in range(2)]

        X = sb("X", [128, 4, 4, D])
        W = sb("W", [128, 4, 2, 4096], F16)
        SCf = sb("SCf", [128, 1408])
        SSf = sb("SSf", [128, 1024])
        XN = sb("XN", [128, 4, D])
        RB = sb("RB", [128, 8192])
        RBh = RB[:, :].bitcast(F16)
        XT = RBh[:, 0:4096].rearrange("p (b l c n) -> p b l c n", b=2, l=2, c=2)
        QK = RBh[:, 4096:8192].rearrange("p (b m l n) -> p b m l n", b=2, m=2, l=2)
        V = RBh[:, 8192:16384].rearrange("p (b l t n) -> p b l t n", b=2, l=2, t=4)
        P = sb("P", [128, 2, 512])
        PT = sb("PT", [128, 2, 2, 512], F16)
        O = sb("O", [128, 2, 2, 256], F16)
        A = sb("A", [128, 4, D])
        RT = sb("RT", [128, 2, 4, ROW])
        HT = sb("HT", [128, 2, 2, 4096], F16)
        stage = HT[:, :, :, :].rearrange("p a b c -> p (a b c)").bitcast(F32).rearrange("p (k b n) -> p k b n",
                                                                                      k=2, b=NST)
        SC_, SS_ = stage[:, 0, :, :], stage[:, 1, :, :]
        W95 = sb("W95", [128, 32, E])
        ident = sb("ident", [128, 128])
        tri = sb("tri", [128, 128], F16)
        ones = sb("ones", [128, 128], F16)
        bo2 = sb("bo2", [128, 512])
        bqk = sb("bqk", [128, 3, NH])
        gTf = sb("gTf", [128, 2, E])
        gT = sb("gT", [128, 2, 2, E], F16)
        iota64 = sb("iota64", [128, E])
        iota8 = sb("iota8", [128, 8])
        K64 = sb("K64", [128, E])
        tid = sb("tid", [128, 32])
        nm0 = sb("nm0", [128, 4, 2])
        nm = sb("nm", [128, 4, 2])
        rs = sb("rs", [128, 4, 2])
        rr = sb("rr", [128, 4, 2])
        st = sb("st", [128, 2, 4, 6])
        mv = sb("mv", [128, 2, 4, 2])
        nw = sb("nw", [128, 2, 4, 4])
        Af = A[:, :, :].rearrange("p t n -> p (t n)")
        ST = [st[:, k, :, :] for k in range(2)] + [
            Af[:, k * 24:(k + 1) * 24].rearrange("p (t n) -> p t n", t=4) for k in range(4)]
        MV = [mv[:, k, :, :] for k in range(2)] + [
            Af[:, 96 + k * 8:96 + (k + 1) * 8].rearrange("p (t n) -> p t n", t=4) for k in range(4)]
        NW = [nw[:, k, :, :] for k in range(2)] + [
            Af[:, 128 + k * 16:128 + (k + 1) * 16].rearrange("p (t n) -> p t n", t=4) for k in range(4)]
        gm0 = sb("gm0", [128, 4])
        gm1 = sb("gm1", [128, 4])
        gsum = sb("gsum", [128, 4])
        grec = sb("grec", [128, 4])
        Sx = sb("Sx", [128, 4, E])
        Tm = sb("Tm", [128, 4, E])
        gs = sb("gs", [128, 4, 8])
        g8 = sb("g8", [128, 4, 8])
        gi = sb("gi", [128, 4, 8], U32)
        geq = sb("geq", [128, 4, 3, 8])
        gk = sb("gk", [128, 4, 8])
        t8 = sb("t8", [128, 4, 8])
        ti = sb("ti", [128, 4, 8], U32)
        teq = sb("teq", [128, 4, 6, E], F16)
        M = sb("M", [128, 4, E], F16)
        MC = sb("MC", [128, E], F16)
        Ms = sb("Ms", [128, E])
        L = sb("L", [128, E])
        Ls = sb("Ls", [128, E])
        C1 = sb("C1", [128, 4, E])
        Lt = C1
        lowbits = C1[:, :, :].rearrange("p t e -> p (t e)").bitcast(U32)
        low1, low2 = Ms[:, 32:33], Ms[0:1, 33:34]
        low3 = Ms[0:1, 34:35].bitcast(U32)
        KP = Sx
        c8 = sb("c8", [128, 4, 8])
        ix = sb("ix", [128, 2, 4, 8], U32)
        zrow = sb("zrow", [128, ROW])

        Wf = W[:, :, :, :].rearrange("p a b c -> p (a b c)").bitcast(F32)
        at = [0]

        def take(n, dt=F32):
            a = Wf[:, at[0]:at[0] + n]
            at[0] += n
            return a if dt == F32 else a.bitcast(dt)

        sgf = SCf[:, 0:1408].rearrange("p (m c n) -> p m c n", m=2, c=2)
        sdf = SSf[:, 0:768].rearrange("p (j n) -> p j n", j=3)
        sgh = take(1408, F16).rearrange("p (l m c n) -> p l m c n", l=2, m=2, c=2)
        sdh = take(768, F16).rearrange("p (l j n) -> p l j n", l=2, j=3)
        sl = take(1024).rearrange("p (b n) -> p b n", b=2)
        af = take(1024).rearrange("p (b n) -> p b n", b=2)
        ah = take(3072, F16).rearrange("p (b l j n) -> p b l j n", b=2, l=2, j=3)
        yst = take(2048).rearrange("p (b t n) -> p b t n", b=2, t=4)
        shared_end = at[0]
        BE = take(NB * ROW).rearrange("p (b n) -> p b n", b=NB)
        BT = take(2 * 192).rearrange("p (b n) -> p b n", b=2)
        sl2 = take(2 * 192).rearrange("p (b n) -> p b n", b=2)
        ac2 = take(2 * 192).rearrange("p (b j n) -> p b j n", b=2, j=2)
        OW = take(4 * 256).rearrange("p (b n) -> p b n", b=4)
        OUT95 = take(256)
        LB = take(ROW)
        assert at[0] <= 16384
        assert 8192 <= shared_end
        fin = [(RB if g < 4 else Wf)[:, g % 4 * 2048:(g % 4 + 1) * 2048].rearrange("p (k t n) -> p k t n", k=2, t=4)
               for g in range(NP)]
        x1 = [SCf[:, 0:1024].rearrange("p (t n) -> p t n", t=4), SSf[:, 0:1024].rearrange("p (t n) -> p t n", t=4),
              XN[:, :, :], P[:, :, :].rearrange("p a (b n) -> p (a b) n", n=D)] + [X[:, g, :, :] for g in range(4)]
        EG = RB[:, 0:NRING * 704].rearrange("p (b n) -> p b n", b=NRING)
        ED = RB[:, NRING * 704:NRING * (704 + 512)].rearrange("p (b n) -> p b n", b=NRING)
        W95T = HT[0:64, :, :, :].rearrange("p a b c -> p (a b c)").bitcast(F32)[:, 0:4096]
        wix = sb("wix", [96, NB, 1], U32)
        lmax = sb("lmax", [64, 1])
        lix = sb("lix", [64, 1], U32)

        names = ("c0 cg cd gt S nm e r pn pt ph pl pv oh ol wo q qh ql k kh kl v vh vl xc po wm wh wl "
                 "lf lc xr fo hd bi yi dd lb sw swh swl sg ssl saf sah sal sdn sy et ebt eg esl eac eo eow wix wt wtc").split()
        s = {n: sem(f"s_{n}") for n in names + ["mx"]}
        s_x = [sem(f"s_x{i}") for i in range(4)]
        s_st = [sem(f"s_st{i}") for i in range(NST)]
        s_x1 = [sem(f"s_x1{i}") for i in range(2)]
        s_sc = [sem(f"s_sc{i}") for i in range(2)]
        s_ew = [sem(f"s_ew{i}") for i in range(NRING)]
        s_be = [sem(f"s_be{i}") for i in range(NB)]
        s_ya = [sem(f"s_ya{i}") for i in range(2)]
        s_o95 = [sem(f"s_o95{i}") for i in range(4)]
        s_ys = [sem(f"s_ys{i}") for i in range(2)]
        s_fl = [sem(f"s_fl{i}") for i in range(NP)]
        s_fc = [sem(f"s_fc{i}") for i in range(4)]

        plan = {k: {} for k in ("pe", "act", "act_late", "dve", "pool", "sp")}
        XC, PO, LC = Chain(s["xc"], plan), Chain(s["po"], plan), Chain(s["lc"], plan)
        FC = [Chain(k, plan) for k in s_fc]
        PRO = -1
        END = NU + 3

        def stats(ch, which, slots, src, waits=()):
            v, y, a, b = (NW[which][:, k, :] for k in range(4))

            def bn(eng):
                for t in range(4):
                    r = eng.bn_stats(ST[which][:, t, :], src(t))
                return r

            def ag(eng):
                for t in range(4):
                    r = eng.bn_aggr(MV[which][:, t, :], ST[which][:, t, :])
                return r

            yield ch.step("dve", slots[0], bn, waits)
            yield ch.step("dve", slots[0], ag)
            yield ch.step("dve", slots[1], lambda e: e.tensor_scalar(v, MV[which][:, :, 1], EPS, None, ALU.add))
            yield ch.step("dve", slots[1], lambda e: e.tensor_scalar(y.bitcast(I32), v.bitcast(I32), -0.5, RSQRT_MAGIC,
                                                              ALU.mult, ALU.add))
            for k in range(3):
                sl_ = slots[1 + k]
                yield ch.step("dve", sl_, lambda e: e.tensor_tensor(a, y, y, ALU.mult))
                yield ch.step("dve", sl_, lambda e: e.scalar_tensor_tensor(out=b, in0=a, scalar=-0.5, in1=v,
                                                                     op0=ALU.mult, op1=ALU.mult))
                yield ch.step("dve", sl_, lambda e: e.scalar_tensor_tensor(out=y, in0=b, scalar=1.5, in1=y,
                                                                     op0=ALU.add, op1=ALU.mult))

        def normal(ch, which, slot, dst, src, waits=()):
            y, b = NW[which][:, 1, :], NW[which][:, 3, :]
            yield ch.step("dve", slot, lambda e: e.scalar_tensor_tensor(out=b, in0=MV[which][:, :, 0], scalar=-1.0, in1=y,
                                                                 op0=ALU.mult, op1=ALU.mult))

            def f(tiles):
                def run(eng):
                    for t in tiles:
                        r = eng.activation(dst(t), src(t), ACT.Identity, bias=NW[which][:, 3, t:t + 1],
                                           scale=NW[which][:, 1, t:t + 1])
                    return r
                return run

            if slot < 0 or slot >= END:
                yield ch.step("act", slot, f(range(4)), waits)
            else:
                yield ch.step("act_late", slot, f((0, 1)), waits)
                yield ch.step("act_late", slot + 1, f((2, 3)))

        def put(steps, *args):
            for n in steps(*args):
                pass
            return n

        p1_busy = {}

        def turn(ch, slot, src, c, dst, waits=(), wr=()):
            def pe(eng):
                for t in range(4):
                    r = eng.transpose(bP1[:, t * 128:(t + 1) * 128], src(t, c), ident[:, :])
                return r
            ch.step("pe", slot, pe, waits)
            ch.step("act", slot + 1 if slot >= 0 else slot,
                    lambda e: e.activation(dst(0), bP1[:, :], ACT.Copy, scale=SX), wr)
            n = ch.step("dve", slot + 1 if slot >= 0 else slot,
                        lambda e: e.scalar_tensor_tensor(out=dst(1), in0=bP1[:, :], scalar=SX, in1=dst(0),
                                                         op0=ALU.mult, op1=ALU.subtract))
            p1_busy[slot] = (ch.sem, n)

        def k_read(slot):
            return (s["kl"], min(NI, slot // 2 + 2))

        xt_ready = {}

        def x_jobs(bp):
            g = bp % 4
            base = (bp - 1) * 32

            def load(eng):
                if bp >= 4:
                    eng.wait_ge(s_x1[bp % 2], 16 * ((bp - 4) // 2 + 1))
                eng.dma_start(X[:, g, :, :], x[bp * 512:(bp + 1) * 512, :].rearrange("(t p) d -> p t d", p=128)
                              ).then_inc(s_x[g], 16)

            plan["sp"].setdefault(PRO if bp < 3 else base, []).append(load)
            sl_ = [PRO] * 8 if bp == 0 else [base + k for k in (2, 3, 4, 5, 6, 11, 13)]
            put(stats, XC, 0, sl_, lambda t: X[:, g, t, :], [(s_x[g], 16 * (bp // 4 + 1))])
            put(normal, XC, 0, sl_[4], lambda t: XN[:, t, :], lambda t: X[:, g, t, :])
            for c in range(2):
                w = [(s["cg"], 2)] if bp == 0 else [k_read(sl_[5 + c])]
                turn(XC, sl_[5 + c], lambda t, c: XN[:, t, c * 128:(c + 1) * 128], c,
                     lambda l, c=c: XT[:, bp % 2, l, c, :], w, [(s["k"], max(0, 16 * (bp - 1)))])
            xt_ready[bp] = XC.n

        wjobs = []
        for m, ch in [(0, 0), (1, 0), (2, 0), (2, 1), (3, 0), (0, 1), (1, 1), (2, 2), (3, 1),
                      (0, 2), (1, 2), (2, 3), (3, 2), (0, 3), (1, 3), (3, 3)]:
            wjobs += [(m, ch, 0), (m, ch, 1)]
        w_ready = {}

        def w_job(n):
            m, chn, c = wjobs[n]
            b = n % NST
            slot = PRO if n < 6 else {6: 0, 7: 1, 8: 1, 9: 2, 10: 3, 11: 3, 12: 4, 13: 4}.get(n, n - 10)

            def load(eng):
                if n >= NST:
                    eng.wait_ge(s["wl"], n - NST + 1)
                h = chn * 4 + c * 2
                for buf, q, o in ((SC_, wc, wo_c), (SS_, wsc, wo_s)):
                    if m < 3:
                        eng.dma_start(buf[:, b, :], q[m, c * 128:(c + 1) * 128, chn * 512:(chn + 1) * 512]
                                      ).then_inc(s_st[b], 16)
                    else:
                        eng.dma_start(buf[:, b, :].rearrange("p (h n) -> p h n", h=2),
                                      o[h * 128:(h + 2) * 128, :].rearrange("(h p) n -> p h n", p=128)
                                      ).then_inc(s_st[b], 16)

            cnt = 2 * (n // NST + 1)
            plan["sp"].setdefault(slot, []).append(load)
            if m < 3:
                o = c * 2048 + chn * 512
            else:
                o = (chn * 4 + c * 2) * 256
            hi, lo = W[:, m, 0, o:o + 512], W[:, m, 1, o:o + 512]

            def scaled(eng):
                eng.wait_ge(s_st[b], 16 * cnt)
                eng.tensor_tensor(SC_[:, b, :], SC_[:, b, :], SS_[:, b, :], ALU.mult).then_inc(s["wm"], 1)

            def high(eng):
                eng.wait_ge(s["wm"], n + 1)
                eng.activation(hi, SC_[:, b, :], ACT.Copy, scale=SW).then_inc(s["wh"], 1)

            def low(eng):
                eng.wait_ge(s["wh"], n + 1)
                eng.scalar_tensor_tensor(out=lo, in0=SC_[:, b, :], scalar=SW, in1=hi,
                                         op0=ALU.mult, op1=ALU.subtract).then_inc(s["wl"], 1)
                eng.wait_ge(s["wl"], n + 1)
                if n == 0:
                    eng.tensor_scalar(lowbits, lo.bitcast(U32), NOSIGN, None, ALU.bitwise_and).then_inc(s["lf"], 1)
                else:
                    eng.wait_ge(s["lf"], n)
                    eng.scalar_tensor_tensor(out=lowbits, in0=lo.bitcast(U32), scalar=NOSIGN, in1=lowbits,
                                             op0=ALU.bitwise_and, op1=ALU.bitwise_or).then_inc(s["lf"], 1)

            now = n < 14
            plan["pool"].setdefault(PRO if n < NST else slot, []).append(scaled)
            plan["act"].setdefault(slot if now else slot + 1, []).append(high)
            plan["dve"].setdefault(slot if now else slot + 2, []).append(low)
            w_ready[wjobs[n]] = n + 1

        def flag_jobs():
            def rows(eng):
                eng.wait_ge(s["lf"], 32)
                return eng.tensor_reduce(low1, lowbits, AX, ALU.max)

            LC.step("dve", 25, rows)
            LC.step("pe", 27, lambda e: e.transpose(bP1[0:1, 0:128], low1, ident[:, :]), [k_read(27)])
            n = LC.step("dve", 28, lambda e: e.tensor_reduce(low2, bP1[0:1, 0:128], AX, ALU.max))
            p1_busy[27] = (LC.sem, n)
            return LC.step("dve", 28, lambda e: e.tensor_scalar(low3, low2, 1.0, None, ALU.min))

        ht_ready, acc_free, m_ready = {}, {}, {}

        def post_jobs(bp):
            g, base = bp % 4, (bp + 1) * 32
            rt = bp % 2

            def at_(k):
                return base + k

            for h in range(2):
                acc_free[(bp, h)] = PO.step(
                    "dve", at_(2 + h),
                    lambda e, h=h: e.scalar_tensor_tensor(out=A[:, 2 * h:2 * h + 2, :].rearrange("p t n -> p (t n)"),
                                                          in0=bACC[h][:, :], scalar=1.0 / (SO * SW), in1=bo2[:, :],
                                                          op0=ALU.mult, op1=ALU.add),
                    [(s["wo"], (bp + 1) * 32 - 1 + h), (s["cd"], 16 * 3)])
            put(stats, PO, 1, [at_(k) for k in (4, 5, 6, 7)], lambda t: A[:, t, :])
            put(normal, PO, 1, at_(7), lambda t: A[:, t, :], lambda t: A[:, t, :])
            for h in range(2):
                PO.step("pool" if bp + 1 < NP else "dve", at_(9 + h), lambda e, h=h: e.tensor_tensor(
                    X[:, g, 2 * h:2 * h + 2, :], X[:, g, 2 * h:2 * h + 2, :], A[:, 2 * h:2 * h + 2, :], ALU.add))
            put(stats, PO, 1, [at_(k) for k in (11, 12, 12, 13)], lambda t: X[:, g, t, :])
            w = []
            if bp >= 2:
                w = [(s_sc[rt], 16 * 24 * (bp // 2)), (s["hd"], 16 * (bp - 1))]
            n = put(normal, PO, 1, at_(13), lambda t: RT[:, rt, t, 0:D], lambda t: X[:, g, t, :], w)

            def store(eng, n=n):
                eng.wait_ge(s["po"], n)
                if bp < 4:
                    eng.dma_start(Xd[bp * 512:(bp + 1) * 512, :].rearrange("(t p) d -> p t d", p=128), X[:, g, :, :]
                                  ).then_inc(s_x1[bp % 2], 16)
                if bp:
                    eng.wait_ge(s["hd"], 16 * bp)
                eng.dma_start(Hd[bp * 512:(bp + 1) * 512, :].rearrange("(t p) d -> p t d", p=128),
                              RT[:, rt, :, 0:D]).then_inc(s["hd"], 16)

            plan["sp"].setdefault(at_(14), []).append(store)
            for c in range(2):
                w = [k_read(at_(15 + 2 * c))]
                turn(PO, at_(15 + 2 * c), lambda t, c: RT[:, rt, t, c * 128:(c + 1) * 128], c,
                     lambda l, c=c: HT[:, l, c, bp * 512:(bp + 1) * 512], w)
            ht_ready[bp] = PO.n

            def logits(eng):
                for t in range(4):
                    k = 0
                    for c in range(2):
                        for a, b in ((0, 0), (0, 1), (1, 0)):
                            r = eng.matmul(bP1[:, t * E:(t + 1) * E],
                                           HT[:, a, c, bp * 512 + t * 128:bp * 512 + (t + 1) * 128],
                                           gT[:, b, c, :], start=(k == 0), stop=(k == 5))
                            k += 1
                return r

            PO.step("pe", at_(21), logits, [k_read(at_(21)), (s["c0"], 4)])
            lg = bP1[:, 0:4 * E].rearrange("p (t e) -> p t e", t=4)
            PO.step("dve", at_(22), lambda e: e.tensor_reduce(gm0[:, :], lg, AX, ALU.max, negate=True))
            PO.step("dve", at_(22), lambda e: e.tensor_scalar(gm1[:, :], gm0[:, :], 1.0 / (SX * SG), None, ALU.mult))

            def gexp(eng):
                for t in range(4):
                    r = eng.activation(Sx[:, t, :], bP1[:, t * E:(t + 1) * E], ACT.Exp, bias=gm1[:, t:t + 1],
                                       scale=1.0 / (SX * SG), accum_out=gsum[:, t:t + 1])
                return r

            n = PO.step("act_late" if at_(22) < END else "act", at_(22), gexp)
            p1_busy[at_(21)] = (PO.sem, n)
            PO.step("dve", at_(23), lambda e: e.reciprocal(grec[:, :], gsum[:, :]))
            PO.step("dve", at_(23), lambda e: e.tensor_tensor(Sx[:, :, :], Sx[:, :, :],
                                                              grec[:, :].unsqueeze(2).broadcast_to([128, 4, E]), ALU.mult))
            PO.step("dve", at_(23), lambda e: e.tensor_reduce(
                gs[:, :, :], Sx[:, :, :].rearrange("p t (g k) -> p t g k", k=8), AX, ALU.max))

            def four(f):
                def run(eng):
                    for t in range(4):
                        r = f(eng, t)
                    return r
                return run

            PO.step("dve", at_(24), four(lambda e, t: e.max(g8[:, t, :], gs[:, t, :])))
            PO.step("dve", at_(24), four(lambda e, t: e.max_index(gi[:, t, :], g8[:, t, :], gs[:, t, :])))
            PO.step("dve", at_(24), lambda e: e.tensor_tensor(
                geq[:, :, :, :], iota8[:, :].unsqueeze(1).unsqueeze(1).broadcast_to([128, 4, 3, 8]),
                gi[:, :, 0:3].unsqueeze(3).broadcast_to([128, 4, 3, 8]), ALU.is_equal), [(s["cg"], 13)])
            PO.step("dve", at_(24), lambda e: e.tensor_reduce(
                gk[:, :, :], geq[:, :, :, :].rearrange("p t k g -> p t g k"), AX, ALU.max))
            PO.step("dve", at_(25), lambda e: e.tensor_tensor(
                Tm[:, :, :].rearrange("p t (g k) -> p (t g) k", k=8),
                Sx[:, :, :].rearrange("p t (g k) -> p (t g) k", k=8),
                gk[:, :, :].rearrange("p t g -> p (t g)").unsqueeze(2).broadcast_to([128, 32, 8]), ALU.mult))
            PO.step("dve", at_(25), four(lambda e, t: e.max(t8[:, t, :], Tm[:, t, :])))
            PO.step("dve", at_(25), four(lambda e, t: e.max_index(ti[:, t, :], t8[:, t, :], Tm[:, t, :])))
            for t in range(4):
                PO.step("dve", at_(26 + t // 2), lambda e, t=t: e.tensor_tensor(
                    teq[:, t, :, :], iota64[:, :].unsqueeze(1).broadcast_to([128, 6, E]),
                    ti[:, t, 0:6].unsqueeze(2).broadcast_to([128, 6, E]), ALU.is_equal))
            PO.step("dve", at_(27), four(lambda e, t: e.tensor_reduce(
                M[:, t, :], teq[:, t, :, :].rearrange("p k e -> p e k"), AX, ALU.max)))
            PO.step("dve", at_(28), lambda e: e.tensor_tensor(RT[:, rt, :, D:D + E], Tm[:, :, :], M[:, :, :], ALU.mult))
            PO.step("dve", at_(28), lambda e: e.tensor_copy(RT[:, rt, :, D + E], tid[:, 4 * bp:4 * bp + 4]))

            def pos(eng):
                for t in range(4):
                    o = bP1[:, t * E:(t + 1) * E]
                    eng.matmul(o, ones[:, :], MC[:, :], start=True, stop=False)
                    for q in range(t):
                        eng.matmul(o, ones[:, :], M[:, q, :], start=False, stop=False)
                    r = eng.matmul(o, tri[:, :], M[:, t, :], start=False, stop=True)
                return r

            PO.step("pe", at_(29), pos, [k_read(at_(29))])
            pp = bP1[:, 0:4 * E].rearrange("p (t e) -> p t e", t=4)
            PO.step("dve", at_(30), lambda e: e.scalar_tensor_tensor(
                out=W95[:, 4 * bp:4 * bp + 4, :], in0=pp, scalar=CAP - 1.5, in1=RT[:, rt, :, D:D + E],
                op0=ALU.is_ge, op1=ALU.mult))
            PO.step("dve", at_(30), lambda e: e.scalar_tensor_tensor(
                out=KP[:, :, :], in0=pp, scalar=CAP - 1.5, in1=M[:, :, :], op0=ALU.is_lt, op1=ALU.mult))
            n = PO.step("dve", at_(30), lambda e: e.scalar_tensor_tensor(
                out=C1[:, :, :], in0=pp, scalar=-float(E), in1=K64[:, :].unsqueeze(1).broadcast_to([128, 4, E]),
                op0=ALU.mult, op1=ALU.add))
            p1_busy[at_(29)] = (PO.sem, n)
            PO.step("dve", at_(31), lambda e: e.tensor_tensor(C1[:, :, :], C1[:, :, :], KP[:, :, :], ALU.mult))
            PO.step("dve", at_(31), four(lambda e, t: e.max(c8[:, t, :], C1[:, t, :])))
            w = [(s_sc[rt], 16 * 24 * (bp // 2))] if bp >= 2 else []
            n = PO.step("dve", at_(31), lambda e: e.tensor_scalar(
                ix[:, rt, :, :].rearrange("p t k -> p (t k)"), c8[:, :, :].rearrange("p t k -> p (t k)"),
                -1.0, 8192.0, ALU.mult, ALU.add), w)
            for t in range(4):
                for k in range(6):
                    def scatter(eng, t=t, k=k, n=n):
                        eng.wait_ge(s["po"], n)
                        eng.wait_ge(s["bi"], 16 * 4)
                        eng.indirect_dma_start(BUF, bass.IndirectOffsetOnAxis(ap=ix[:, rt, t, k:k + 1], axis=0),
                                               RT[:, rt, t, :], None, bounds_check=CAP * E - 1, oob_is_err=False
                                               ).then_inc(s_sc[rt], 16)
                    plan["pool"].setdefault(at_(32 + t * 6 + k), []).append(scatter)
            PO.step("dve", at_(31), lambda e: e.tensor_reduce(
                Ms[:, :], M[:, :, :].rearrange("p t e -> p e t"), AX, ALU.add))
            PO.step("dve", at_(31), lambda e: e.tensor_tensor(MC[:, :], MC[:, :], Ms[:, :], ALU.add))
            PO.step("dve", at_(32), lambda e: e.scalar_tensor_tensor(
                out=Lt[:, :, :], in0=tid[:, 4 * bp:4 * bp + 4].unsqueeze(2).broadcast_to([128, 4, E]), scalar=1.0,
                in1=M[:, :, :], op0=ALU.add, op1=ALU.mult))
            PO.step("dve", at_(32), lambda e: e.tensor_reduce(
                Ls[:, :], Lt[:, :, :].rearrange("p t e -> p e t"), AX, ALU.max))
            PO.step("dve", at_(32), lambda e: e.tensor_tensor(L[:, :], L[:, :], Ls[:, :], ALU.max))

        x_jobs(0)
        for n in range(32):
            w_job(n)
        LOW_READY = flag_jobs()
        for bp in range(NP):
            if bp + 1 < NP:
                x_jobs(bp + 1)
            post_jobs(bp)

        LAST = NU + 33
        PO.step("dve", LAST, lambda e: e.memset(LB[0:E, D:D + E], 1.0), [(s["wo"], NU)])
        PO.step("dve", LAST, lambda e: e.memset(LB[0:E, D + E:ROW], FAR))
        PO.step("pe", LAST, lambda e: e.transpose(bP1[0:E, 0:128], L[:, :], ident[:, :]))
        PO.step("dve", LAST, lambda e: e.tensor_reduce(lmax[:, :], bP1[0:E, 0:128], AX, ALU.max))
        PO_END = PO.step("dve", LAST, lambda e: e.tensor_scalar(lix[:, :], lmax[:, :], -1.0, 0.0, ALU.add, ALU.max))

        def last_tokens(eng):
            eng.wait_ge(s["po"], PO_END)
            eng.wait_ge(s["hd"], 16 * NP)
            eng.indirect_dma_start(LB[0:E, 0:D], None, Hd, bass.IndirectOffsetOnAxis(ap=lix[:, 0:1], axis=0),
                                   bounds_check=4095, oob_is_err=False).then_inc(s["lb"], 16)

        plan["pool"][LAST].append(last_tokens)

        def last_rows(eng):
            eng.wait_ge(s["lb"], 16)
            eng.wait_ge(s["po"], PO_END)
            eng.wait_ge(s["bi"], 16 * 4)
            eng.dma_start(BUF[(CAP - 1) * E:CAP * E, :], LB[0:E, :]).then_inc(s["dd"], 16)

        plan["sp"].setdefault(LAST + 2, []).append(last_rows)

        fin_out = {}

        def final_jobs(g):
            b, slot, ch = g % 4, 1000, FC[g % 4]
            banks = ((bACC[0], bACC[1]), (bP0, bP1), (bS[0], bS[1]), (bPT, bO))[b]
            f = fin[g]

            def mm(eng):
                for t in range(4):
                    r = eng.matmul(banks[t // 2][:, t % 2 * 256:(t % 2 + 1) * 256],
                                   W95T[:, (4 * g + t) * 128:(4 * g + t + 1) * 128], OUT95[0:E, :],
                                   start=True, stop=True)
                return r

            def half(a, h):
                return a[:, 2 * h:2 * h + 2, :].rearrange("p t n -> p (t n)")

            w = [(s["wtc"], NP)] + [(s_o95[k], 16 * E // 4) for k in range(4)] if g < 4 else []
            yield ch.step("pe", slot, mm, w)
            for h in range(2):
                yield ch.step("pool", slot, lambda e, h=h: e.tensor_tensor(
                    half(f[:, 0], h), half(f[:, 0], h), half(f[:, 1], h), ALU.add), [(s_fl[g], 32)])
            yield from [0] * LEAD[0]
            for h in range(2):
                yield ch.step("dve", slot, lambda e, h=h: e.tensor_tensor(
                    half(f[:, 0], h), banks[h][:, :], half(f[:, 0], h), ALU.add))
            yield from [0] * LEAD[1]
            yield from stats(ch, 2 + b, [slot] * 4, lambda t: f[:, 0, t, :])
            yield from normal(ch, 2 + b, slot, lambda t: f[:, 0, t, :], lambda t: f[:, 0, t, :])
            yield from [0] * LEAD[2]
            w = [(s["po"], PO_END)] if g >= 4 else [(s["xr"], 64)]
            for h, who in enumerate(("pool", "dve")):
                fin_out[g] = ch.step(who, slot, lambda e, h=h: e.tensor_tensor(
                    half(f[:, 0], h), half(f[:, 0], h), half(x1[g], h), ALU.add), w)
                yield

        last_slot = max(max(v) for v in plan.values() if v)
        jobs = [final_jobs(g) for g in range(NP)]
        for k in range(LEAD[3] * NP + 60):
            for g in range(NP):
                if k >= LEAD[3] * g:
                    next(jobs[g], None)

        def run_plan(who, eng, slot, k=0, n=1):
            fs = plan[who].get(slot, [])
            for f in fs[len(fs) * k // n:len(fs) * (k + 1) // n]:
                f(eng)

        SLOTS = range(0, END)
        TAIL = range(END, last_slot + 1)

        def part_slot(k):
            return NU + 4 + k * 28 // 16 if k < 17 else NU + 34 + k - 17

        PART = {part_slot(k): k for k in range(27)}

        def part(slot, after):
            g, rest = divmod(PART.get(slot, -1) - 2 - after, 3)
            return g if rest == 0 and 0 <= g < NP else None

        GB = ((bS[0], bS[1]), (bPT, bO))
        MT = (128, 128, 96)

        block = ctx.enter_context(nc.Block())

        @block.sync
        def _(eng):
            eng.dma_start(bqk[:, :, :], bqkv).then_inc(s["cd"], 16)
            for k in range(2):
                eng.dma_start(bo2[:, 256 * k:256 * k + 256],
                              bo.rearrange("(a n) -> a n", a=1).broadcast_to([128, 256])).then_inc(s["cd"], 16)
            eng.dma_start(gTf[:, :, :], gateT.rearrange("(c p) e -> p c e", p=128)).then_inc(s["gt"], 16)
            run_plan("sp", eng, PRO)
            for slot in SLOTS:
                run_plan("sp", eng, slot)
                if 24 <= slot < 32 and slot % 2 == 0:
                    n = (slot - 24) // 2
                    eng.wait_ge(s["S"], slot)
                    eng.wait_ge(s["cg"], 11)
                    eng.dma_start(BUF[n * 1536:(n + 1) * 1536, :].rearrange("(k p) c -> p k c", p=128),
                                  zrow[:, :].unsqueeze(1).broadcast_to([128, 12, ROW])).then_inc(s["bi"], 16)
                if slot == 48:
                    eng.wait_ge(s["wl"], 32)
                    for m in range(2):
                        eng.dma_start(sgf[:, m, :, :], sguT[m].rearrange("(c p) n -> p c n", p=128)
                                      ).then_inc(s["sw"], 16)
                    eng.dma_start(sdf[:, 0:2, :], sdT[0:256, :].rearrange("(j p) n -> p j n", p=128)
                                  ).then_inc(s["sw"], 16)
                    eng.dma_start(sdf[0:96, 2, :], sdT[256:352, :]).then_inc(s["sw"], 16)
                if 32 <= slot < 48 and slot % 2 == 0:
                    n = (slot - 32) // 2
                    eng.wait_ge(s["S"], slot)
                    eng.dma_start(Y[1][n * 512:(n + 1) * 512, :].rearrange("(k p) c -> p k c", p=128),
                                  zrow[:, 0:D].unsqueeze(1).broadcast_to([128, 4, D])).then_inc(s["yi"], 16)
            eng.wait_ge(s["wo"], NU)

            def expert_weights(e):
                b = e % NRING
                if e >= NRING:
                    eng.wait_ge(s["eo"], e - NRING + 1)
                eng.dma_start(EG[:, b, :], ewT[e]).then_inc(s_ew[b], 16)
                eng.dma_start(ED[0:88, b, :], ewd[e]).then_inc(s_ew[b], 16)

            def expert_rows(e):
                b = e % NB
                if e >= NB:
                    eng.wait_ge(s["eow"], e - NB + 1)
                    eng.wait_ge(s["wix"], e - NB + 1)
                eng.dma_start(BE[0:CAP, b, :], BUF.rearrange("(s e) c -> e s c", e=E)[e]).then_inc(s_be[b], 16)

            for e in range(NRING):
                expert_weights(e)
            eng.wait_ge(s["swl"], 3)
            eng.wait_ge(s["pt"], NU)
            eng.wait_ge(s["xc"], XC.n)
            for k in range(2):
                eng.wait_ge(s_x1[k], 16 * 2)
            for g in range(4):
                eng.dma_start(x1[g], Xd[g * 512:(g + 1) * 512, :].rearrange("(t p) d -> p t d", p=128)
                              ).then_inc(s["xr"], 16)
            for slot in TAIL:
                run_plan("sp", eng, slot)
                if PART.get(slot) == 3 * NP - 1:
                    eng.wait_ge(s["dd"], 16)
                    for k in range(2):
                        eng.wait_ge(s_sc[k], 16 * 24 * 4)
                    for e in range(NB):
                        expert_rows(e)
                g = part(slot, 3)
                if g is not None:
                    eng.wait_ge(s["sy"], 2 * (g + 1))
                    eng.dma_start(Y[0][g * 512:(g + 1) * 512, :].rearrange("(t p) d -> p t d", p=128),
                                  yst[:, g % 2, :, :]).then_inc(s_ys[g % 2], 16)
            for e in range(E):
                if e + NRING < E:
                    expert_weights(e + NRING)
                if e + NB < E:
                    expert_rows(e + NB)
                eng.wait_ge(s["eow"], e + 1)
                eng.dma_start(OUT95[e:e + 1, :], OW[CAP - 1:CAP, e % 4, :]).then_inc(s_o95[e % 4], 16)

            for k in range(2):
                eng.wait_ge(s_ya[k], 16 * 32)
            for g in range(NP):
                for k in range(2):
                    eng.dma_start(fin[g][:, k, :, :], Y[k][g * 512:(g + 1) * 512, :].rearrange(
                        "(t p) d -> p t d", p=128)).then_inc(s_fl[g], 16)
            for g in range(NP):
                eng.wait_ge(s_fc[g % 4], fin_out[g])
                eng.dma_start(out[g * 512:(g + 1) * 512, :].rearrange("(t p) d -> p t d", p=128), fin[g][:, 0, :, :]
                              ).then_inc(s["fo"], 16)
            eng.wait_ge(s["fo"], 16 * NP)

        @block.gpsimd
        def _(eng):
            cg = [0]

            def c(ins, wait=False):
                ins.then_inc(s["cg"], 1)
                cg[0] += 1
                if wait:
                    eng.wait_ge(s["cg"], cg[0])

            c(eng.memset(ident[:, :], 0.0), True)
            c(eng.affine_select(out=ident[:, :], in_=ident[:, :], compare_op=ALU.not_equal, fill=1.0, base=0,
                                pattern=[[-1, 128]], channel_multiplier=1))
            run_plan("pool", eng, PRO)
            c(eng.memset(tri[:, :], 1.0), True)
            c(eng.affine_select(out=tri[:, :], in_=tri[:, :], compare_op=ALU.is_gt, fill=0.0, base=0,
                                pattern=[[1, 128]], channel_multiplier=-1))
            c(eng.memset(ones[:, :], 1.0))
            for t_, pat, base, cm in ((iota8, [[1, 8]], 0, 0), (iota64, [[1, E]], 0, 0), (K64, [[-1, E]], 8192, 0),
                                      (tid, [[128, 32]], 0, 1)):
                c(eng.iota(t_[:, :], pattern=pat, base=base, channel_multiplier=cm,
                           allow_small_or_imprecise_dtypes=True))
            c(eng.memset(zrow[:, :], 0.0), True)
            c(eng.memset(zrow[:, ROW - 1:ROW], FAR))
            c(eng.memset(MC[:, :], 0.0))
            c(eng.memset(L[:, :], 0.0))

            def norm(w):
                eng.wait_ge(s["r"], w + 1)
                p = P[:, w % 2, :].rearrange("p (t k) -> p t k", t=2)
                eng.tensor_tensor(p, p, rr[:, w % 4, :].unsqueeze(2).broadcast_to([128, 2, 256]), ALU.mult
                                  ).then_inc(s["pn"], 1)

            for u in SLOTS:
                slot_work("pool", u, {"norm": norm, "bg": lambda *a: run_plan("pool", eng, *a)})
            for slot in TAIL:
                run_plan("pool", eng, slot)
            for k in range(2):
                eng.wait_ge(s_ys[k], 16 * 4)
            eng.wait_ge(s["yi"], 16 * 8)
            for e in range(E):
                eng.wait_ge(s["eow"], e + 1)
                eng.wait_ge(s["wix"], e + 1)
                if e >= 2:
                    eng.wait_ge(s_ya[e % 2], 16 * (e // 2))
                eng.indirect_dma_start(Y[e % 2], bass.IndirectOffsetOnAxis(ap=wix[:, e % NB, :], axis=0),
                                       OW[0:CAP, e % 4, :], None, bounds_check=4095, oob_is_err=False,
                                       compute_op=ALU.add).then_inc(s_ya[e % 2], 16)
            run_plan("pool", eng, 1000)

        @block.tensor
        def _(eng):
            PASS = ((0, 0), (0, 1), (1, 0))

            def passes(w, low):
                return [p for p in PASS if low or p[w] == 0]

            def proj_qk(i, m, low):
                bp, h = i // NH, i % NH
                bk_ = bP0 if m == 0 else bP1
                eng.wait_ge(s["xc"], xt_ready[bp])
                if bp == 0:
                    eng.wait_ge(s["wl"], w_ready[(m, h // 4, 1)])
                if m == 0:
                    if i:
                        eng.wait_ge(s["vl"], min(NI, i + 2))
                else:
                    eng.wait_ge(s["kl"], i)
                    if 2 * (i - 1) - 1 in p1_busy and i:
                        eng.wait_ge(*p1_busy[2 * (i - 1) - 1])
                k, n = 0, 2 * len(passes(0, low))
                for c in range(2):
                    for a, b in passes(0, low):
                        r = eng.matmul(bk_[:, :], W[:, m, a, c * 2048 + h * 128:c * 2048 + (h + 1) * 128],
                                       XT[:, bp % 2, b, c, :], start=(k == 0), stop=(k == n - 1))
                        k += 1
                r.then_inc(s["q" if m == 0 else "k"], 1)

            def proj_v(j, low):
                g, t = j // 4, j % 4
                bp, hg = g // 4, g % 4
                eng.wait_ge(s["xc"], xt_ready[bp])
                if bp == 0:
                    eng.wait_ge(s["wl"], w_ready[(2, hg, 1)])
                eng.wait_ge(s["ql"], 1 if j < 3 else min(NI, j - 1))
                if j < 3:
                    eng.wait_ge(s["vl"], j)
                k, n = 0, 2 * len(passes(1, low))
                for c in range(2):
                    for a, b in passes(1, low):
                        r = eng.matmul(bP0[:, :], XT[:, bp % 2, a, c, t * 128:(t + 1) * 128],
                                       W[:, 2, b, c * 2048 + hg * 512:c * 2048 + (hg + 1) * 512],
                                       start=(k == 0), stop=(k == n - 1))
                        k += 1
                r.then_inc(s["v"], 1)

            def scores(u):
                i, q = u // 2, u % 2
                if q == 0:
                    eng.wait_ge(s["ql"], i + 1)
                    eng.wait_ge(s["kl"], i + 1)
                if u >= 2:
                    eng.wait_ge(s["e"], u - 1)
                for t in range(2):
                    for k, (a, b) in enumerate(PASS):
                        r = eng.matmul(bS[u % 2][:, t * 256:(t + 1) * 256],
                                       QK[:, i % 2, 0, a, q * 256 + t * 128:q * 256 + (t + 1) * 128],
                                       QK[:, i % 2, 1, b, q * 256:(q + 1) * 256], start=(k == 0), stop=(k == 2))
                r.then_inc(s["S"], 1)

            def turn_p(u):
                eng.wait_ge(s["pn"], u + 1)
                eng.wait_ge(s["pl"], u)
                for kc in range(2):
                    for t in range(2):
                        r = eng.transpose(bPT[:, kc * 256 + t * 128:kc * 256 + (t + 1) * 128],
                                          P[:, u % 2, t * 256 + kc * 128:t * 256 + (kc + 1) * 128], ident[:, :])
                r.then_inc(s["pt"], 1)

            def pv(u):
                i, q = u // 2, u % 2
                h = i % NH
                if u % 8 == 0:
                    eng.wait_ge(s["vl"], 4 * (i // 4 + 1))
                eng.wait_ge(s["pl"], u + 1)
                eng.wait_ge(s["ol"], u)
                k = 0
                for kc in range(2):
                    for a, b in PASS:
                        r = eng.matmul(bO[:, 0:256],
                                       V[:, i // 4 % 2, a, 2 * q + kc, h % 4 * 128:(h % 4 + 1) * 128],
                                       PT[:, u % 2, b, kc * 256:(kc + 1) * 256], start=(k == 0), stop=(k == 5))
                        k += 1
                r.then_inc(s["pv"], 1)

            def proj_o(u, low):
                i, q = u // 2, u % 2
                bp, h = i // NH, i % NH
                if bp == 0:
                    eng.wait_ge(s["wl"], w_ready[(3, h // 4, 1)])
                if h == 0 and bp:
                    eng.wait_ge(s["po"], acc_free[(bp - 1, q)])
                eng.wait_ge(s["ol"], u + 1)
                n = len(passes(1, low))
                for t in range(2):
                    for k, (a, b) in enumerate(passes(1, low)):
                        r = eng.matmul(bACC[q][:, t * 256:(t + 1) * 256], O[:, u % 2, a, t * 128:(t + 1) * 128],
                                       W[:, 3, b, h * 256:(h + 1) * 256], start=(h == 0 and t == 0 and k == 0),
                                       stop=(h == NH - 1 and k == n - 1), skip_group_check=True)
                r.then_inc(s["wo"], 1)

            run_plan("pe", eng, PRO)
            proj_qk(0, 0, True)
            proj_qk(0, 1, True)
            for j in range(3):
                proj_v(j, True)

            def attention(slots, low):
                work = {"S": scores, "Q": lambda i: proj_qk(i, 0, low), "K": lambda i: proj_qk(i, 1, low),
                        "V": lambda j: proj_v(j, low), "WO": lambda w: proj_o(w, low), "PT": turn_p, "PV": pv,
                        "bg": lambda *a: run_plan("pe", eng, *a)}
                for u in slots:
                    slot_work("pe", u, work)

            attention(range(0, 32), True)
            eng.wait_ge(s["lc"], LOW_READY)
            low = eng.value_load(low3[0:1, 0:1], min_val=0, max_val=1)
            with eng.If(low == 0):
                attention(range(32, END), False)
            with eng.Else():
                attention(range(32, END), True)

            def shared_up(k):
                g, j = divmod(k, 3)
                M_ = MT[j]
                if k == 0:
                    eng.wait_ge(s["swl"], 3)
                    eng.wait_ge(s["e"], NU)
                if k == 1:
                    eng.wait_ge(s["pl"], NU)
                    eng.wait_ge(s["ol"], NU)
                if k >= 2:
                    eng.wait_ge(s["saf"], k - 1)
                if j == 0:
                    eng.wait_ge(s["po"], ht_ready[g])
                for m in range(2):
                    q = 0
                    for c in range(2):
                        for a, b in PASS:
                            r = eng.matmul(GB[k % 2][m][0:M_, :], sgh[:, a, m, c, j * 128:j * 128 + M_],
                                           HT[:, b, c, g * 512:(g + 1) * 512], start=(q == 0), stop=(q == 5))
                            q += 1
                r.then_inc(s["sg"], 1)

            def shared_down(g):
                eng.wait_ge(s["sal"], 3 * (g + 1))
                for t in range(4):
                    if t % 2 == 0:
                        if g == 0:
                            eng.wait_ge(s["po"], acc_free[(NP - 1, t // 2)])
                        else:
                            eng.wait_ge(s["sy"], 2 * (g - 1) + t // 2 + 1)
                    q = 0
                    for j in range(3):
                        for a, b in PASS:
                            r = eng.matmul(bACC[t // 2][:, t % 2 * 256:(t % 2 + 1) * 256],
                                           ah[0:MT[j], g % 2, a, j, t * 128:(t + 1) * 128],
                                           sdh[0:MT[j], b, j, :], start=(q == 0), stop=(q == 8))
                            q += 1
                    r.then_inc(s["sdn"], 1)

            for slot in TAIL:
                run_plan("pe", eng, slot)
                if 0 <= PART.get(slot, -1) < 3 * NP:
                    shared_up(PART[slot])
                if part(slot, 2) is not None:
                    shared_down(part(slot, 2))

            for g in range(NP):
                if g == 0:
                    eng.wait_ge(s["sy"], 2 * NP)
                    eng.wait_ge(s["po"], PO_END)
                if g >= 2:
                    eng.wait_ge(s["wtc"], g - 1)
                for t in range(4):
                    r = eng.transpose(bACC[g % 2][0:E, t * 128:(t + 1) * 128], W95[:, 4 * g + t, :], ident[:, :])
                r.then_inc(s["wt"], 1)

            def e_turn(e):
                b = e % NB
                eng.wait_ge(s_be[b], 16 * (e // NB + 1))
                if e >= 2:
                    eng.wait_ge(s["ebt"], e - 1)
                for c in range(2):
                    r = eng.transpose((bP0, bP1)[e % 2][:, c * CAP:(c + 1) * CAP],
                                      BE[0:CAP, b, c * 128:(c + 1) * 128], ident[0:CAP, 0:CAP])
                r.then_inc(s["et"], 1)

            def e_up(e):
                b = e % NRING
                eng.wait_ge(s_ew[b], 32 * (e // NRING + 1))
                eng.wait_ge(s["ebt"], e + 1)
                if e >= 2:
                    eng.wait_ge(s["eac"], e - 1)
                else:
                    eng.wait_ge(s["saf"], 3 * NP)
                for m in range(2):
                    for j in range(2):
                        for c in range(2):
                            o = (m * 2 + c) * 176 + j * 88
                            r = eng.matmul(bS[e % 2][0:88, (m * 2 + j) * CAP:(m * 2 + j + 1) * CAP],
                                           EG[:, b, o:o + 88], BT[:, e % 2, c * CAP:(c + 1) * CAP],
                                           start=(c == 0), stop=(c == 1))
                r.then_inc(s["eg"], 1)

            def e_down(e):
                b = e % NRING
                eng.wait_ge(s["eac"], e + 1)
                if e >= 2:
                    eng.wait_ge(s["eow"], e - 1)
                for j in range(2):
                    r = eng.matmul((bPT, bO)[e % 2][0:CAP, 0:256], ac2[0:88, e % 2, j, :],
                                   ED[0:88, b, j * 256:(j + 1) * 256], start=(j == 0), stop=(j == 1))
                r.then_inc(s["eo"], 1)

            for e in range(E + 2):
                if e < E:
                    e_turn(e)
                if 0 <= e - 1 < E:
                    e_up(e - 1)
                if 0 <= e - 2 < E:
                    e_down(e - 2)
            run_plan("pe", eng, 1000)

        @block.scalar
        def _(eng):
            def q_high(i, m):
                h = i % NH
                eng.wait_ge(s["q" if m == 0 else "k"], i + 1)
                if i >= 2:
                    eng.wait_ge(s["S"], 2 * i - 2)
                if i == 0:
                    eng.wait_ge(s["c0"], 2)
                eng.activation(QK[:, i % 2, m, 0, :], (bP0 if m == 0 else bP1)[:, :], ACT.Identity,
                               bias=bqk[:, m, h:h + 1]).then_inc(s["qh" if m == 0 else "kh"], 1)

            def v_high(j):
                eng.wait_ge(s["v"], j + 1)
                if j >= 8:
                    eng.wait_ge(s["pv"], 8 * (j // 4 - 1))
                eng.activation(V[:, j // 4 % 2, 0, j % 4, :], bP0[:, :], ACT.Copy, scale=SV / (SX * SW)
                               ).then_inc(s["vh"], 1)

            run_plan("act", eng, PRO)
            q_high(0, 0)
            q_high(0, 1)
            for j in range(3):
                v_high(j)

            def o_high(w):
                h = w // 2 % NH
                eng.wait_ge(s["pv"], w + 1)
                if w >= 2:
                    eng.wait_ge(s["wo"], w - 1)
                eng.activation(O[:, w % 2, 0, :], bO[:, 0:256], ACT.Identity, bias=bqk[:, 2, h:h + 1]
                               ).then_inc(s["oh"], 1)

            def exp(u):
                eng.wait_ge(s["nm"], u + 1)
                if u >= 2:
                    eng.wait_ge(s["pt"], u - 1)
                for t in range(2):
                    r = eng.activation(P[:, u % 2, t * 256:(t + 1) * 256], bS[u % 2][:, t * 256:(t + 1) * 256],
                                       ACT.Exp, bias=nm[:, u % 4, t:t + 1], scale=SCALE / (SQ * SQ),
                                       accum_out=rs[:, u % 4, t:t + 1])
                r.then_inc(s["e"], 1)

            def p_high(w):
                eng.wait_ge(s["pt"], w + 1)
                if w >= 2:
                    eng.wait_ge(s["pv"], w - 1)
                eng.activation(PT[:, w % 2, 0, :], bPT[:, :], ACT.Copy, scale=SP_).then_inc(s["ph"], 1)

            work = {"O": o_high, "Q": lambda i: q_high(i, 0), "K": lambda i: q_high(i, 1), "V": v_high,
                    "exp": exp, "PT": p_high, "bg": lambda *a: run_plan("act", eng, *a),
                    "late": lambda u: run_plan("act_late", eng, u)}
            for u in SLOTS:
                slot_work("act", u, work)
            eng.wait_ge(s["sw"], 16 * 4)
            eng.activation(sgh[:, 0, :, :, :], sgf, ACT.Copy, scale=SG).then_inc(s["swh"], 1)
            eng.activation(sdh[:, 0, 0:2, :], sdf[:, 0:2, :], ACT.Copy, scale=SG).then_inc(s["swh"], 1)
            eng.activation(sdh[0:96, 0, 2, :], sdf[0:96, 2, :], ACT.Copy, scale=SG).then_inc(s["swh"], 1)

            def act_up(k):
                g, j = divmod(k, 3)
                eng.wait_ge(s["sg"], k + 1)
                if k >= 2:
                    eng.wait_ge(s["saf"], k - 1)
                eng.activation(sl[0:MT[j], k % 2, :], GB[k % 2][0][0:MT[j], :], ACT.Silu, scale=1.0 / (SX * SG)
                               ).then_inc(s["ssl"], 1)
                eng.wait_ge(s["saf"], k + 1)
                if g >= 2:
                    eng.wait_ge(s["sdn"], 4 * (g - 1))
                eng.activation(ah[0:MT[j], g % 2, 0, j, :], af[0:MT[j], k % 2, :], ACT.Copy).then_inc(s["sah"], 1)

            def act_down(g):
                for h in range(2):
                    eng.wait_ge(s["sdn"], 4 * g + 2 * h + 2)
                    if g >= 2:
                        eng.wait_ge(s_ys[g % 2], 16 * (g // 2))
                    eng.activation(yst[:, g % 2, 2 * h:2 * h + 2, :].rearrange("p t n -> p (t n)"), bACC[h][:, :],
                                   ACT.Copy, scale=1.0 / (SA * SG)).then_inc(s["sy"], 1)

            for slot in TAIL:
                run_plan("act", eng, slot)
                if 1 <= PART.get(slot, -1) <= 3 * NP:
                    act_up(PART[slot] - 1)
                if part(slot, 3) is not None:
                    act_down(part(slot, 3))
            for g in range(NP):
                eng.wait_ge(s["wt"], g + 1)
                if g == 0:
                    eng.wait_ge(s["sg"], 3 * NP)
                eng.activation(W95T[:, g * 512:(g + 1) * 512], bACC[g % 2][0:E, :], ACT.Copy).then_inc(s["wtc"], 1)

            def e_silu(e):
                eng.wait_ge(s["eg"], e + 1)
                if e >= 2:
                    eng.wait_ge(s["eac"], e - 1)
                eng.activation(sl2[0:88, e % 2, :], bS[e % 2][0:88, 0:192], ACT.Silu).then_inc(s["esl"], 1)

            def e_out(e):
                eng.wait_ge(s["eo"], e + 1)
                if e >= 4:
                    eng.wait_ge(s_ya[e % 2], 16 * (e // 2 - 1))
                    eng.wait_ge(s_o95[e % 4], 16 * (e // 4))
                eng.activation(OW[0:CAP, e % 4, :], (bPT, bO)[e % 2][0:CAP, 0:256], ACT.Copy,
                               scale=BE[0:CAP, e % NB, D + e:D + e + 1]).then_inc(s["eow"], 1)

            for e in range(E + 2):
                if 0 <= e - 1 < E:
                    e_silu(e - 1)
                if 0 <= e - 2 < E:
                    e_out(e - 2)
            run_plan("act", eng, 1000)

        @block.vector
        def _(eng):
            eng.wait_ge(s["cd"], 16 * 3)
            eng.tensor_scalar(bqk[:, 0:2, :], bqk[:, 0:2, :], SQ, None, ALU.mult).then_inc(s["c0"], 1)
            eng.tensor_scalar(bqk[:, 2, :], bqk[:, 2, :], SO, None, ALU.mult).then_inc(s["c0"], 1)
            run_plan("dve", eng, PRO)

            def q_low(i, m):
                h = i % NH
                eng.wait_ge(s["qh" if m == 0 else "kh"], i + 1)
                eng.scalar_tensor_tensor(out=QK[:, i % 2, m, 1, :], in0=(bP0 if m == 0 else bP1)[:, :],
                                         scalar=bqk[:, m, h:h + 1], in1=QK[:, i % 2, m, 0, :],
                                         op0=ALU.add, op1=ALU.subtract).then_inc(s["ql" if m == 0 else "kl"], 1)

            def v_low(j):
                eng.wait_ge(s["vh"], j + 1)
                eng.scalar_tensor_tensor(out=V[:, j // 4 % 2, 1, j % 4, :], in0=bP0[:, :], scalar=SV / (SX * SW),
                                         in1=V[:, j // 4 % 2, 0, j % 4, :], op0=ALU.mult, op1=ALU.subtract
                                         ).then_inc(s["vl"], 1)

            q_low(0, 0)
            q_low(0, 1)
            for j in range(3):
                v_low(j)
            eng.wait_ge(s["gt"], 16)
            eng.tensor_scalar(gT[:, 0, :, :], gTf[:, :, :], SG, None, ALU.mult).then_inc(s["c0"], 1)
            eng.wait_ge(s["c0"], 3)
            eng.scalar_tensor_tensor(out=gT[:, 1, :, :], in0=gTf[:, :, :], scalar=SG, in1=gT[:, 0, :, :],
                                     op0=ALU.mult, op1=ALU.subtract).then_inc(s["c0"], 1)

            def recip(w):
                eng.wait_ge(s["e"], w + 1)
                eng.reciprocal(rr[:, w % 4, :], rs[:, w % 4, :]).then_inc(s["r"], 1)

            def p_low(w):
                eng.wait_ge(s["ph"], w + 1)
                eng.scalar_tensor_tensor(out=PT[:, w % 2, 1, :], in0=bPT[:, :], scalar=SP_,
                                         in1=PT[:, w % 2, 0, :], op0=ALU.mult, op1=ALU.subtract
                                         ).then_inc(s["pl"], 1)

            def row_max(u):
                eng.wait_ge(s["S"], u + 1)
                eng.tensor_reduce(nm0[:, u % 4, :], bS[u % 2][:, :].rearrange("p (t k) -> p t k", t=2), AX,
                                  ALU.max, negate=True).then_inc(s["mx"], 1)

            def neg_max(u):
                eng.wait_ge(s["mx"], u + 1)
                eng.tensor_scalar(nm[:, u % 4, :], nm0[:, u % 4, :], SCALE / (SQ * SQ), None, ALU.mult
                                  ).then_inc(s["nm"], 1)

            def o_low(w):
                h = w // 2 % NH
                eng.wait_ge(s["oh"], w + 1)
                eng.scalar_tensor_tensor(out=O[:, w % 2, 1, :], in0=bO[:, 0:256], scalar=bqk[:, 2, h:h + 1],
                                         in1=O[:, w % 2, 0, :], op0=ALU.add, op1=ALU.subtract
                                         ).then_inc(s["ol"], 1)

            work = {"recip": recip, "PT": p_low, "max": row_max, "nm": neg_max, "O": o_low,
                    "Q": lambda i: q_low(i, 0), "K": lambda i: q_low(i, 1), "V": v_low,
                    "bg": lambda *a: run_plan("dve", eng, *a)}
            for u in SLOTS:
                slot_work("dve", u, work)
            for n, (lo, f, hi) in enumerate(((sgh[:, 1, :, :, :], sgf, sgh[:, 0, :, :, :]),
                                             (sdh[:, 1, 0:2, :], sdf[:, 0:2, :], sdh[:, 0, 0:2, :]),
                                             (sdh[0:96, 1, 2, :], sdf[0:96, 2, :], sdh[0:96, 0, 2, :]))):
                eng.wait_ge(s["swh"], n + 1)
                for m in range(2 if n == 0 else 1):
                    pick = (lambda a: a[:, m, :, :]) if n == 0 else (lambda a: a)
                    r = eng.scalar_tensor_tensor(out=pick(lo), in0=pick(f), scalar=SG, in1=pick(hi),
                                                 op0=ALU.mult, op1=ALU.subtract)
                r.then_inc(s["swl"], 1)

            def dve_up(k):
                g, j = divmod(k, 3)
                eng.wait_ge(s["ssl"], k + 1)
                eng.scalar_tensor_tensor(out=af[0:MT[j], k % 2, :], in0=GB[k % 2][1][0:MT[j], :],
                                         scalar=SA / (SX * SG), in1=sl[0:MT[j], k % 2, :],
                                         op0=ALU.mult, op1=ALU.mult).then_inc(s["saf"], 1)
                eng.wait_ge(s["sah"], k + 1)
                eng.tensor_tensor(ah[0:MT[j], g % 2, 1, j, :], af[0:MT[j], k % 2, :],
                                  ah[0:MT[j], g % 2, 0, j, :], ALU.subtract).then_inc(s["sal"], 1)

            for slot in TAIL:
                run_plan("dve", eng, slot)
                if 1 <= PART.get(slot, -1) <= 3 * NP:
                    dve_up(PART[slot] - 1)

            def e_rows(e):
                eng.wait_ge(s["et"], e + 1)
                if e >= 2:
                    eng.wait_ge(s["eg"], e - 1)
                eng.tensor_copy(BT[:, e % 2, :], (bP0, bP1)[e % 2][:, 0:192]).then_inc(s["ebt"], 1)
                if e >= NB:
                    eng.wait_ge(s_ya[e % 2], 16 * ((e - NB) // 2 + 1))
                eng.tensor_copy(wix[:, e % NB, :], BE[0:CAP, e % NB, ROW - 1:ROW]).then_inc(s["wix"], 1)

            def e_act(e):
                eng.wait_ge(s["esl"], e + 1)
                if e >= 2:
                    eng.wait_ge(s["eo"], e - 1)
                eng.tensor_tensor(ac2[0:88, e % 2, :, :].rearrange("p j n -> p (j n)"), bS[e % 2][0:88, 192:384],
                                  sl2[0:88, e % 2, :], ALU.mult).then_inc(s["eac"], 1)

            for e in range(E + 1):
                if e < E:
                    e_rows(e)
                if e >= 1:
                    e_act(e - 1)
            run_plan("dve", eng, 1000)


def kernel(**inputs):
    import numpy as _np
    import concourse.bacc as _bacc
    from concourse import mybir as _mybir
    from concourse.bass_utils import run_bass_kernel_spmd as _run

    g = {k: _np.asarray(v) for k, v in inputs.items()}
    at = lambda n: g["L0_attn_" + n]
    ff = lambda n: g["L0_ffn_" + n]
    gu = _np.stack([ff("Wg"), ff("Wu")], 1)
    arrays = {
        "in_x": at("x").reshape(4096, 256),
        "in_wc": _np.stack([at("wq_codes"), at("wk_codes"), at("wv_codes")]),
        "in_ws": _np.repeat(_np.stack([at("wq_scales"), at("wk_scales"), at("wv_scales")]), 32, axis=1),
        "in_oc": at("wo_codes"),
        "in_os": _np.repeat(at("wo_scales"), 32, axis=0),
        "in_b": _np.stack([at("bq"), at("bk"), at("bv")]).reshape(3, 16, 128).transpose(2, 0, 1),
        "in_bo": at("bo"),
        "in_gate": ff("gate_weight").T,
        "in_sgu": _np.stack([ff("Sg").T, ff("Su").T]),
        "in_sd": ff("Sd").T,
        "in_ewT": gu.reshape(64, 2, 176, 2, 128).transpose(0, 4, 1, 3, 2).reshape(64, 128, 704),
        "in_ewd": ff("Wd").reshape(64, 256, 2, 88).transpose(0, 3, 2, 1).reshape(64, 88, 512),
    }
    arrays = {k: _np.ascontiguousarray(v) for k, v in arrays.items()}
    nc = _bacc.Bacc("TRN2", target_bir_lowering=False, num_devices=1)
    args = [nc.dram_tensor(k, a.shape, _mybir.dt.from_np(a.dtype), kind="ExternalInput").ap()
            for k, a in arrays.items()]
    out = nc.dram_tensor("out_0", (4096, 256), _mybir.dt.float32, kind="ExternalOutput").ap()
    build(nc, *args, out)
    r = _run(nc, [arrays], core_ids=[0])
    return r.results[0]["out_0"].reshape(16, 256, 256)
```
